# Optimizing a Trainium2 kernel written in Bass

```python
import numpy as np
import jax
import jax.numpy as jnp

def _softmax(x, axis=-1):
    return jax.nn.softmax(x, axis=axis)

def _gelu(x):
    return jax.nn.gelu(x, approximate=True)

def _silu(x):
    return jax.nn.silu(x)

def _sigmoid(x):
    return jax.nn.sigmoid(x)

def _layernorm(x, axis=-1, eps=1e-05):
    m = jnp.mean(x, axis=axis, keepdims=True)
    v = jnp.var(x, axis=axis, keepdims=True)
    return (x - m) / jnp.sqrt(v + eps)

def _scatter_add(tgt, idx, src, axis=0):
    return tgt.at[idx].add(src)

def _segment_sum(src, seg, n):
    return jax.ops.segment_sum(src, seg, n)
kernel_name = 'mk_decoder_postln_d2_seqx_r8_8cbe1a'

def setup_inputs(seed: int=0):
    np.random.seed(seed)
    _w = jnp.asarray

    def _rec_inputs():
        import jax
        import jax.numpy as jnp
        _rk = jax.random.key(seed)
        x = 7.22e-05 + 1 * jax.random.normal(jax.random.fold_in(_rk, 1), (4, 256, 256), jnp.float32)
        _lenS = 256 - jax.random.randint(jax.random.fold_in(_rk, 7), (4,), 0, max(1, 256 // 4) + 1, jnp.int32)
        _lenS2 = 256 - jax.random.randint(jax.random.fold_in(_rk, 8), (4,), 0, max(1, 256 // 4) + 1, jnp.int32)
        _ctx_2048P = jax.random.normal(jax.random.fold_in(_rk, 11), (4, 16, 256), jnp.float32)
        _ctx_2048c = jax.random.dirichlet(jax.random.fold_in(_rk, 511), 0.3 * jnp.ones((16,), jnp.float32), (4, 256))
        _ctx_2048t = jnp.einsum('bsk,bkd->bsd', _ctx_2048c, _ctx_2048P)
        _ctx_2048t = _ctx_2048t * jax.lax.rsqrt(jnp.mean(jnp.square(_ctx_2048t)) + 1e-12) * 0.953939
        ctx_2048 = 4.13588e-05 + 0.999923 * (_ctx_2048t + 0.3 * jax.random.normal(jax.random.fold_in(_rk, 611), (4, 256, 256), jnp.float32))
        pos_BxS2 = jnp.broadcast_to(jnp.arange(256, dtype=jnp.int32), (4, 256))
        itok_BxS_4096_4607 = jax.random.randint(jax.random.fold_in(_rk, 13), (4, 256), 512, 576, jnp.int32)
        return (x, ctx_2048, pos_BxS2, itok_BxS_4096_4607)
    x, ctx_2048, pos_BxS2, itok_BxS_4096_4607 = _rec_inputs()

    def _L0_attn_setup():
        import jax, jax.numpy as jnp
        import numpy as np
        B, L = (2, 128)
        D_MODEL, D_INNER, D_STATE, D_CONV, DT_RANK = (256, 512, 16, 4, 128)
        key = jax.random.key(seed)
        ks = jax.random.split(key, 9)
        s = 0.02
        x = jax.random.normal(ks[0], (B, L, D_MODEL), jnp.float32)
        W_in = jax.random.normal(ks[1], (2 * D_INNER, D_MODEL), jnp.float32) * s
        conv_w = jax.random.normal(ks[2], (D_INNER, D_CONV), jnp.float32) * s
        conv_b = jax.random.normal(ks[3], (D_INNER,), jnp.float32) * s
        W_x = jax.random.normal(ks[4], (DT_RANK + 2 * D_STATE, D_INNER), jnp.float32) * s
        W_dt = jax.random.normal(ks[5], (D_INNER, DT_RANK), jnp.float32) * s
        b_dt = jax.random.normal(ks[6], (D_INNER,), jnp.float32) * s
        A_log = jnp.log(jnp.broadcast_to(jnp.arange(1, D_STATE + 1, dtype=jnp.float32), (D_INNER, D_STATE)))
        D = jnp.ones((D_INNER,), jnp.float32)
        W_out = jax.random.normal(ks[7], (D_MODEL, D_INNER), jnp.float32) * s
        return {'x': x, 'W_in': W_in, 'conv_w': conv_w, 'conv_b': conv_b, 'W_x': W_x, 'W_dt': W_dt, 'b_dt': b_dt, 'A_log': A_log, 'D': D, 'W_out': W_out}
    _L0_attn_all = _L0_attn_setup()
    _L0_attn_in = {k: v for k, v in _L0_attn_all.items() if k in ('W_in', 'conv_w', 'conv_b', 'W_x', 'W_dt', 'b_dt', 'A_log', 'D', 'W_out')}
    del _L0_attn_all

    def _L0_xattn_setup():
        import jax, jax.numpy as jnp
        import numpy as np
        N_HEAD = 8
        key = jax.random.key(seed)
        k1, k2, k3 = jax.random.split(key, 3)
        b, d, m = (4, 128, 256)
        c, n = (128, 256)
        q = jax.random.normal(k1, (b, d, m), dtype=jnp.float32)
        k = jax.random.normal(k2, (d // d * b, d, n), dtype=jnp.float32).reshape(b, d, n)
        v = jax.random.normal(k3, (b, c, n), dtype=jnp.float32)
        return {'q': q, 'k': k, 'v': v}
    _L0_xattn_all = _L0_xattn_setup()
    _L0_xattn_in = {k: v for k, v in _L0_xattn_all.items() if k in ()}
    del _L0_xattn_all

    def _L0_ffn_setup():
        import jax, jax.numpy as jnp
        import numpy as np
        B, S, D, H = (4, 256, 256, 1024)

        def fwht(x):
            orig_shape = x.shape
            n = orig_shape[-1]
            x = x.reshape(-1, n)
            h = 1
            while h < n:
                xb = x.reshape(-1, n // (2 * h), 2, h)
                a = xb[:, :, 0, :]
                b = xb[:, :, 1, :]
                x = jnp.stack([a + b, a - b], axis=2).reshape(-1, n)
                h *= 2
            scale = jnp.asarray(1.0 / np.sqrt(n), dtype=x.dtype)
            return (x * scale).reshape(orig_shape)
        key = jax.random.key(seed)
        kx, k1, k2, k3 = jax.random.split(key, 4)
        x = jax.random.normal(kx, (B, S, D), dtype=jnp.float32)
        W1 = jax.random.normal(k1, (H, D), dtype=jnp.float32) * (1.0 / np.sqrt(D))
        W2 = jax.random.normal(k2, (D, H), dtype=jnp.float32) * (1.0 / np.sqrt(H))
        W3 = jax.random.normal(k3, (H, D), dtype=jnp.float32) * (1.0 / np.sqrt(D))
        return {'x': x, 'W1': W1, 'W2': W2, 'W3': W3}
    _L0_ffn_all = _L0_ffn_setup()
    _L0_ffn_in = {k: v for k, v in _L0_ffn_all.items() if k in ('W1', 'W2', 'W3')}
    del _L0_ffn_all

    def _L1_attn_setup():
        import jax, jax.numpy as jnp
        import numpy as np
        DIM = 256
        HEAD_DIM = 128
        H = DIM // HEAD_DIM
        D_H = 128
        CHUNK = 256
        B, L = (1, 1024)
        BASE_LR = 0.01
        LN_EPS = 1e-06
        NS_COEFS = [(4.0848, -6.8946, 2.927), (3.9505, -6.3029, 2.6377), (3.7418, -5.5913, 2.3037), (2.8769, -3.1427, 1.2046), (2.8366, -3.0525, 1.2012)]

        def silu(x):
            return x * jax.nn.sigmoid(x)

        def silu_backprop(dy, x):
            s = jax.nn.sigmoid(x)
            return dy * s * (1 + x * (1 - s))

        def l2_norm(x, eps=1e-05):
            return x / (jnp.linalg.norm(x, axis=-1, keepdims=True) + eps)

        def zeropower_ns5(G):
            X = G
            transposed = G.shape[1] > G.shape[2]
            if transposed:
                X = jnp.swapaxes(X, 1, 2)
            X = X / (jnp.linalg.norm(X, axis=(1, 2), keepdims=True) + 1e-07)
            for a, b, c in NS_COEFS:
                A = X @ jnp.swapaxes(X, 1, 2)
                Bm = b * A + c * (A @ A)
                X = a * X + Bm @ X
            if transposed:
                X = jnp.swapaxes(X, 1, 2)
            return X

        def block_causal_lact_swiglu(w0, w1, w2, q, k, v, lr0, lr1, lr2, momentum):
            bh, l, d = k.shape
            v = jnp.swapaxes(v, 1, 2)
            q = jnp.swapaxes(q, 1, 2)
            w0_norm = jnp.linalg.norm(w0, axis=2, keepdims=True)
            w1_norm = jnp.linalg.norm(w1, axis=2, keepdims=True)
            w2_norm = jnp.linalg.norm(w2, axis=2, keepdims=True)
            outs = []
            for i in range(0, l - CHUNK, CHUNK):
                s, e = (i, i + CHUNK)
                ki = k[:, s:e, :]
                vi = v[:, :, s:e]
                qi = q[:, :, s:e]
                lr0i, lr1i, lr2i = (lr0[:, s:e, :], lr1[:, s:e, :], lr2[:, s:e, :])
                h = w2 @ qi
                gate = silu(w0 @ qi)
                outs.append(w1 @ (gate * h))
                kiT = jnp.swapaxes(ki, 1, 2)
                gate_before = w0 @ kiT
                hidden_before = w2 @ kiT
                hidden = silu(gate_before) * hidden_before
                dhidden = jnp.swapaxes(w1, 1, 2) @ vi
                dhidden_before = dhidden * silu(gate_before)
                dgate = dhidden * hidden_before
                dgate_before = silu_backprop(dgate, gate_before)
                lr1iT = jnp.swapaxes(lr1i, 1, 2)
                dw1 = vi @ jnp.swapaxes(hidden * lr1iT, 1, 2)
                dw0 = dgate_before @ (ki * lr0i)
                dw2 = dhidden_before @ (ki * lr2i)
                if momentum is not None:
                    m_i = jnp.mean(momentum[:, s:e, :], axis=1, keepdims=True)
                    dw0 = dw0 + dw0 * m_i
                    dw1 = dw1 + dw1 * m_i
                    dw2 = dw2 + dw2 * m_i
                dw0 = zeropower_ns5(dw0)
                dw1 = zeropower_ns5(dw1)
                dw2 = zeropower_ns5(dw2)
                w0 = w0 + dw0
                w1 = w1 + dw1
                w2 = w2 + dw2
                w0 = w0 / (jnp.linalg.norm(w0, axis=2, keepdims=True) + 1e-05) * w0_norm
                w1 = w1 / (jnp.linalg.norm(w1, axis=2, keepdims=True) + 1e-05) * w1_norm
                w2 = w2 / (jnp.linalg.norm(w2, axis=2, keepdims=True) + 1e-05) * w2_norm
            qi = q[:, :, l - CHUNK:]
            h = w2 @ qi
            gate = silu(w0 @ qi)
            outs.append(w1 @ (gate * h))
            out = jnp.concatenate(outs, axis=2)
            return jnp.swapaxes(out, 1, 2)

        def _forward(x, W_qkv, W_lr, W_o, W_m, b_m, W_s, b_s, ln_g, ln_b, w0, w1, w2):
            b, l, _ = x.shape
            h, d = (H, HEAD_DIM)
            qkv = silu(x @ W_qkv).reshape(b, l, h, 3 * d)
            ttt_q, ttt_k, ttt_v = jnp.split(qkv, 3, axis=-1)
            ttt_q = l2_norm(ttt_q).reshape(b * h, l, d)
            ttt_k = l2_norm(ttt_k).reshape(b * h, l, d)
            ttt_v = ttt_v.reshape(b * h, l, d)
            base_lr_inv = BASE_LR + jnp.log(-jnp.expm1(jnp.float32(-BASE_LR)))
            lr = jax.nn.softplus(x @ W_lr + base_lr_inv)
            lr = lr.reshape(b, l, 3, h).transpose(2, 0, 3, 1).reshape(3, b * h, l, 1)
            lr0, lr1, lr2 = (lr[0], lr[1], lr[2])
            w0b = jnp.tile(w0, (b, 1, 1))
            w1b = jnp.tile(w1, (b, 1, 1))
            w2b = jnp.tile(w2, (b, 1, 1))
            momentum = jax.nn.sigmoid(x @ W_m + b_m)
            momentum = momentum.reshape(b, l, h, 1).transpose(0, 2, 1, 3).reshape(b * h, l, 1)
            out = block_causal_lact_swiglu(w0b, w1b, w2b, ttt_q, ttt_k, ttt_v, lr0, lr1, lr2, momentum)
            mu = jnp.mean(out, axis=-1, keepdims=True)
            var = jnp.mean(jnp.square(out - mu), axis=-1, keepdims=True)
            out = (out - mu) * jax.lax.rsqrt(var + LN_EPS) * ln_g + ln_b
            scale = silu(x @ W_s + b_s).reshape(b, l, h, 1).transpose(0, 2, 1, 3).reshape(b * h, l, 1)
            out = out * scale
            out = out.reshape(b, h, l, d).transpose(0, 2, 1, 3).reshape(b, l, h * d)
            return out @ W_o
        ks = jax.random.split(jax.random.key(seed), 11)
        sd = 1.0 / np.sqrt(DIM)
        return {'x': jax.random.normal(ks[0], (B, L, DIM), jnp.float32), 'W_qkv': jax.random.normal(ks[1], (DIM, 3 * DIM), jnp.float32) * sd, 'W_lr': jax.random.normal(ks[2], (DIM, 3 * H), jnp.float32) * sd, 'W_o': jax.random.normal(ks[3], (DIM, DIM), jnp.float32) * sd, 'W_m': jax.random.normal(ks[4], (DIM, H), jnp.float32) * sd, 'b_m': jnp.zeros((H,), jnp.float32), 'W_s': jax.random.normal(ks[5], (DIM, H), jnp.float32) * sd, 'b_s': jnp.zeros((H,), jnp.float32), 'ln_g': jnp.ones((HEAD_DIM,), jnp.float32), 'ln_b': jnp.zeros((HEAD_DIM,), jnp.float32), 'w0': jax.random.normal(ks[6], (H, D_H, HEAD_DIM), jnp.float32) / np.sqrt(HEAD_DIM), 'w1': jax.random.normal(ks[7], (H, HEAD_DIM, D_H), jnp.float32) / np.sqrt(D_H), 'w2': jax.random.normal(ks[8], (H, D_H, HEAD_DIM), jnp.float32) / np.sqrt(HEAD_DIM)}
    _L1_attn_all = _L1_attn_setup()
    _L1_attn_in = {k: v for k, v in _L1_attn_all.items() if k in ('W_qkv', 'W_lr', 'W_o', 'W_m', 'b_m', 'W_s', 'b_s', 'ln_g', 'ln_b', 'w0', 'w1', 'w2')}
    del _L1_attn_all

    def _L1_xattn_setup():
        import jax, jax.numpy as jnp
        import numpy as np
        B, CTX, DRAFT, D = (2, 512, 64, 256)
        H, KVH, HD = (16, 4, 128)
        N_REP = H // KVH
        EPS = 1e-06
        THETA = 10000.0
        SCALE = 1.0 / np.sqrt(HD).astype(np.float32)

        def _rms_norm(x, w):
            v = jnp.mean(jnp.square(x.astype(jnp.float32)), axis=-1, keepdims=True)
            return (w * (x.astype(jnp.float32) * jax.lax.rsqrt(v + EPS))).astype(x.dtype)

        def _rotate_half(x):
            x1, x2 = jnp.split(x, 2, axis=-1)
            return jnp.concatenate((-x2, x1), axis=-1)

        def _rope(x, pos):
            inv_freq = 1.0 / THETA ** (jnp.arange(0, HD, 2, dtype=jnp.float32) / HD)
            freqs = pos.astype(jnp.float32)[:, None, :, None] * inv_freq
            emb = jnp.concatenate((freqs, freqs), axis=-1)
            return x * jnp.cos(emb) + _rotate_half(x) * jnp.sin(emb)
        key = jax.random.key(seed)
        ks = jax.random.split(key, 6)
        return {'draft_hidden': jax.random.normal(ks[0], (B, DRAFT, D), jnp.float32), 'context_hidden': jax.random.normal(ks[1], (B, CTX, D), jnp.float32), 'Wq': jax.random.normal(ks[2], (H * HD, D), jnp.float32) * 0.02, 'Wk': jax.random.normal(ks[3], (KVH * HD, D), jnp.float32) * 0.02, 'Wv': jax.random.normal(ks[4], (KVH * HD, D), jnp.float32) * 0.02, 'Wo': jax.random.normal(ks[5], (D, H * HD), jnp.float32) * 0.02, 'q_norm_w': jnp.ones((HD,), jnp.float32), 'k_norm_w': jnp.ones((HD,), jnp.float32), 'context_position_ids': jnp.broadcast_to(jnp.arange(CTX, dtype=jnp.int32), (B, CTX)), 'draft_position_ids': jnp.broadcast_to(CTX + jnp.arange(DRAFT, dtype=jnp.int32), (B, DRAFT))}
    _L1_xattn_all = _L1_xattn_setup()
    _L1_xattn_in = {k: v for k, v in _L1_xattn_all.items() if k in ('Wq', 'Wk', 'Wv', 'Wo', 'q_norm_w', 'k_norm_w')}
    del _L1_xattn_all

    def _L1_ffn_setup():
        import jax, jax.numpy as jnp
        import numpy as np
        B, S, D, F, E, SH, K = (2, 256, 256, 128, 16, 2, 2)

        def _experts_all(x, g, gb, w1, b1, w2, b2):
            y = jax.nn.gelu(jnp.einsum('bsd,edf->bsef', x, g) + gb, approximate=False)
            y = y * (jnp.einsum('bsd,edf->bsef', x, w1) + b1)
            return jnp.einsum('bsef,efd->bsed', y, w2) + b2
        key = jax.random.key(seed)
        ks = jax.random.split(key, 8)
        std = 0.02
        mk = lambda k, sh: jax.random.normal(k, sh, jnp.float32) * std
        return {'x': jax.random.normal(ks[0], (B, S, D), jnp.float32), 'wa': mk(ks[1], (D, E)), 'rg': mk(ks[2], (E, D, F)), 'rgb': jnp.zeros((E, F), jnp.float32), 'rw1': mk(ks[3], (E, D, F)), 'rb1': jnp.zeros((E, F), jnp.float32), 'rw2': mk(ks[4], (E, F, D)), 'rb2': jnp.zeros((E, D), jnp.float32), 'sg': mk(ks[5], (SH, D, F)), 'sgb': jnp.zeros((SH, F), jnp.float32), 'sw1': mk(ks[6], (SH, D, F)), 'sb1': jnp.zeros((SH, F), jnp.float32), 'sw2': mk(ks[7], (SH, F, D)), 'sb2': jnp.zeros((SH, D), jnp.float32)}
    _L1_ffn_all = _L1_ffn_setup()
    _L1_ffn_in = {k: v for k, v in _L1_ffn_all.items() if k in ('wa', 'rg', 'rgb', 'rw1', 'rb1', 'rw2', 'rb2', 'sg', 'sgb', 'sw1', 'sb1', 'sw2', 'sb2')}
    del _L1_ffn_all
    return {'x': x, 'ctx_2048': ctx_2048, 'pos_BxS2': pos_BxS2, 'itok_BxS_4096_4607': itok_BxS_4096_4607, 'L0_attn_W_in': _L0_attn_in['W_in'], 'L0_attn_conv_w': _L0_attn_in['conv_w'], 'L0_attn_conv_b': _L0_attn_in['conv_b'], 'L0_attn_W_x': _L0_attn_in['W_x'], 'L0_attn_W_dt': _L0_attn_in['W_dt'], 'L0_attn_b_dt': _L0_attn_in['b_dt'], 'L0_attn_A_log': _L0_attn_in['A_log'], 'L0_attn_D': _L0_attn_in['D'], 'L0_attn_W_out': _L0_attn_in['W_out'], 'L0_ffn_W1': _L0_ffn_in['W1'], 'L0_ffn_W2': _L0_ffn_in['W2'], 'L0_ffn_W3': _L0_ffn_in['W3'], 'L1_attn_W_qkv': _L1_attn_in['W_qkv'], 'L1_attn_W_lr': _L1_attn_in['W_lr'], 'L1_attn_W_o': _L1_attn_in['W_o'], 'L1_attn_W_m': _L1_attn_in['W_m'], 'L1_attn_b_m': _L1_attn_in['b_m'], 'L1_attn_W_s': _L1_attn_in['W_s'], 'L1_attn_b_s': _L1_attn_in['b_s'], 'L1_attn_ln_g': _L1_attn_in['ln_g'], 'L1_attn_ln_b': _L1_attn_in['ln_b'], 'L1_attn_w0': _L1_attn_in['w0'], 'L1_attn_w1': _L1_attn_in['w1'], 'L1_attn_w2': _L1_attn_in['w2'], 'L1_xattn_Wq': _L1_xattn_in['Wq'], 'L1_xattn_Wk': _L1_xattn_in['Wk'], 'L1_xattn_Wv': _L1_xattn_in['Wv'], 'L1_xattn_Wo': _L1_xattn_in['Wo'], 'L1_xattn_q_norm_w': _L1_xattn_in['q_norm_w'], 'L1_xattn_k_norm_w': _L1_xattn_in['k_norm_w'], 'L1_ffn_wa': _L1_ffn_in['wa'], 'L1_ffn_rg': _L1_ffn_in['rg'], 'L1_ffn_rgb': _L1_ffn_in['rgb'], 'L1_ffn_rw1': _L1_ffn_in['rw1'], 'L1_ffn_rb1': _L1_ffn_in['rb1'], 'L1_ffn_rw2': _L1_ffn_in['rw2'], 'L1_ffn_rb2': _L1_ffn_in['rb2'], 'L1_ffn_sg': _L1_ffn_in['sg'], 'L1_ffn_sgb': _L1_ffn_in['sgb'], 'L1_ffn_sw1': _L1_ffn_in['sw1'], 'L1_ffn_sb1': _L1_ffn_in['sb1'], 'L1_ffn_sw2': _L1_ffn_in['sw2'], 'L1_ffn_sb2': _L1_ffn_in['sb2']}

def reference(x, ctx_2048, pos_BxS2, itok_BxS_4096_4607, L0_attn_W_in, L0_attn_conv_w, L0_attn_conv_b, L0_attn_W_x, L0_attn_W_dt, L0_attn_b_dt, L0_attn_A_log, L0_attn_D, L0_attn_W_out, L0_ffn_W1, L0_ffn_W2, L0_ffn_W3, L1_attn_W_qkv, L1_attn_W_lr, L1_attn_W_o, L1_attn_W_m, L1_attn_b_m, L1_attn_W_s, L1_attn_b_s, L1_attn_ln_g, L1_attn_ln_b, L1_attn_w0, L1_attn_w1, L1_attn_w2, L1_xattn_Wq, L1_xattn_Wk, L1_xattn_Wv, L1_xattn_Wo, L1_xattn_q_norm_w, L1_xattn_k_norm_w, L1_ffn_wa, L1_ffn_rg, L1_ffn_rgb, L1_ffn_rw1, L1_ffn_rb1, L1_ffn_rw2, L1_ffn_rb2, L1_ffn_sg, L1_ffn_sgb, L1_ffn_sw1, L1_ffn_sb1, L1_ffn_sw2, L1_ffn_sb2):
    import jax
    import jax.numpy as jnp

    def _L0_attn_ref(x, W_in, conv_w, conv_b, W_x, W_dt, b_dt, A_log, D, W_out):
        import jax, jax.numpy as jnp
        import numpy as np
        B, L = (2, 128)
        D_MODEL, D_INNER, D_STATE, D_CONV, DT_RANK = (256, 512, 16, 4, 128)
        silu = jax.nn.silu
        b, l, _ = x.shape
        d_inner, d_conv = conv_w.shape
        dt_rank = W_dt.shape[1]
        d_state = A_log.shape[1]
        proj = x @ W_in.T
        xs, z = jnp.split(proj, 2, axis=-1)
        xp = jnp.pad(xs, ((0, 0), (d_conv - 1, 0), (0, 0)))
        conv = conv_b
        for k in range(d_conv):
            conv = conv + xp[:, k:k + l, :] * conv_w[:, k]
        u = silu(conv)
        x_dbl = u @ W_x.T
        dt_r = x_dbl[..., :dt_rank]
        Bm = x_dbl[..., dt_rank:dt_rank + d_state]
        Cm = x_dbl[..., dt_rank + d_state:]
        dt = jax.nn.softplus(dt_r @ W_dt.T + b_dt)
        A = -jnp.exp(A_log)
        dA = jnp.exp(dt[..., None] * A)
        dBu = dt[..., None] * Bm[:, :, None, :] * u[..., None]

        def step(h, inp):
            dA_t, dBu_t, C_t = inp
            h = dA_t * h + dBu_t
            y = jnp.einsum('bds,bs->bd', h, C_t)
            return (h, y)
        h0 = jnp.zeros((b, d_inner, d_state), x.dtype)
        _, ys = jax.lax.scan(step, h0, (jnp.moveaxis(dA, 1, 0), jnp.moveaxis(dBu, 1, 0), jnp.moveaxis(Cm, 1, 0)))
        y = jnp.moveaxis(ys, 0, 1) + u * D
        y = y * silu(z)
        return y @ W_out.T

    def _L0_xattn_ref(q, k, v):
        import jax, jax.numpy as jnp
        import numpy as np
        N_HEAD = 8
        b, d, m = q.shape
        c = v.shape[1]
        h = N_HEAD
        qh = q.reshape(b * h, d // h, m)
        kh = k.reshape(b * h, d // h, -1)
        vh = v.reshape(b * h, c // h, -1)
        scale = 1.0 / jnp.sqrt(jnp.asarray(d // h, dtype=q.dtype))
        qk = jnp.einsum('bdm,bdn->bmn', qh, kh) * scale
        sm = jax.nn.softmax(qk, axis=-1)
        ret = jnp.einsum('bmn,bcn->bcm', sm, vh)
        return ret.reshape(b, c, m)

    def _L0_ffn_ref(x, W1, W2, W3):
        import jax, jax.numpy as jnp
        import numpy as np
        B, S, D, H = (4, 256, 256, 1024)

        def fwht(x):
            orig_shape = x.shape
            n = orig_shape[-1]
            x = x.reshape(-1, n)
            h = 1
            while h < n:
                xb = x.reshape(-1, n // (2 * h), 2, h)
                a = xb[:, :, 0, :]
                b = xb[:, :, 1, :]
                x = jnp.stack([a + b, a - b], axis=2).reshape(-1, n)
                h *= 2
            scale = jnp.asarray(1.0 / np.sqrt(n), dtype=x.dtype)
            return (x * scale).reshape(orig_shape)
        up_gate = jnp.einsum('bsd,hd->bsh', x, W1)
        up_lin = jnp.einsum('bsd,hd->bsh', x, W3)
        hidden = jax.nn.silu(up_gate) * up_lin
        hidden = fwht(hidden)
        out = jnp.einsum('bsh,dh->bsd', hidden, W2)
        return out

    def _L1_attn_ref(x, W_qkv, W_lr, W_o, W_m, b_m, W_s, b_s, ln_g, ln_b, w0, w1, w2):
        import jax, jax.numpy as jnp
        import numpy as np
        DIM = 256
        HEAD_DIM = 128
        H = DIM // HEAD_DIM
        D_H = 128
        CHUNK = 256
        B, L = (1, 1024)
        BASE_LR = 0.01
        LN_EPS = 1e-06
        NS_COEFS = [(4.0848, -6.8946, 2.927), (3.9505, -6.3029, 2.6377), (3.7418, -5.5913, 2.3037), (2.8769, -3.1427, 1.2046), (2.8366, -3.0525, 1.2012)]

        def silu(x):
            return x * jax.nn.sigmoid(x)

        def silu_backprop(dy, x):
            s = jax.nn.sigmoid(x)
            return dy * s * (1 + x * (1 - s))

        def l2_norm(x, eps=1e-05):
            return x / (jnp.linalg.norm(x, axis=-1, keepdims=True) + eps)

        def zeropower_ns5(G):
            X = G
            transposed = G.shape[1] > G.shape[2]
            if transposed:
                X = jnp.swapaxes(X, 1, 2)
            X = X / (jnp.linalg.norm(X, axis=(1, 2), keepdims=True) + 1e-07)
            for a, b, c in NS_COEFS:
                A = X @ jnp.swapaxes(X, 1, 2)
                Bm = b * A + c * (A @ A)
                X = a * X + Bm @ X
            if transposed:
                X = jnp.swapaxes(X, 1, 2)
            return X

        def block_causal_lact_swiglu(w0, w1, w2, q, k, v, lr0, lr1, lr2, momentum):
            bh, l, d = k.shape
            v = jnp.swapaxes(v, 1, 2)
            q = jnp.swapaxes(q, 1, 2)
            w0_norm = jnp.linalg.norm(w0, axis=2, keepdims=True)
            w1_norm = jnp.linalg.norm(w1, axis=2, keepdims=True)
            w2_norm = jnp.linalg.norm(w2, axis=2, keepdims=True)
            outs = []
            for i in range(0, l - CHUNK, CHUNK):
                s, e = (i, i + CHUNK)
                ki = k[:, s:e, :]
                vi = v[:, :, s:e]
                qi = q[:, :, s:e]
                lr0i, lr1i, lr2i = (lr0[:, s:e, :], lr1[:, s:e, :], lr2[:, s:e, :])
                h = w2 @ qi
                gate = silu(w0 @ qi)
                outs.append(w1 @ (gate * h))
                kiT = jnp.swapaxes(ki, 1, 2)
                gate_before = w0 @ kiT
                hidden_before = w2 @ kiT
                hidden = silu(gate_before) * hidden_before
                dhidden = jnp.swapaxes(w1, 1, 2) @ vi
                dhidden_before = dhidden * silu(gate_before)
                dgate = dhidden * hidden_before
                dgate_before = silu_backprop(dgate, gate_before)
                lr1iT = jnp.swapaxes(lr1i, 1, 2)
                dw1 = vi @ jnp.swapaxes(hidden * lr1iT, 1, 2)
                dw0 = dgate_before @ (ki * lr0i)
                dw2 = dhidden_before @ (ki * lr2i)
                if momentum is not None:
                    m_i = jnp.mean(momentum[:, s:e, :], axis=1, keepdims=True)
                    dw0 = dw0 + dw0 * m_i
                    dw1 = dw1 + dw1 * m_i
                    dw2 = dw2 + dw2 * m_i
                dw0 = zeropower_ns5(dw0)
                dw1 = zeropower_ns5(dw1)
                dw2 = zeropower_ns5(dw2)
                w0 = w0 + dw0
                w1 = w1 + dw1
                w2 = w2 + dw2
                w0 = w0 / (jnp.linalg.norm(w0, axis=2, keepdims=True) + 1e-05) * w0_norm
                w1 = w1 / (jnp.linalg.norm(w1, axis=2, keepdims=True) + 1e-05) * w1_norm
                w2 = w2 / (jnp.linalg.norm(w2, axis=2, keepdims=True) + 1e-05) * w2_norm
            qi = q[:, :, l - CHUNK:]
            h = w2 @ qi
            gate = silu(w0 @ qi)
            outs.append(w1 @ (gate * h))
            out = jnp.concatenate(outs, axis=2)
            return jnp.swapaxes(out, 1, 2)

        def _forward(x, W_qkv, W_lr, W_o, W_m, b_m, W_s, b_s, ln_g, ln_b, w0, w1, w2):
            b, l, _ = x.shape
            h, d = (H, HEAD_DIM)
            qkv = silu(x @ W_qkv).reshape(b, l, h, 3 * d)
            ttt_q, ttt_k, ttt_v = jnp.split(qkv, 3, axis=-1)
            ttt_q = l2_norm(ttt_q).reshape(b * h, l, d)
            ttt_k = l2_norm(ttt_k).reshape(b * h, l, d)
            ttt_v = ttt_v.reshape(b * h, l, d)
            base_lr_inv = BASE_LR + jnp.log(-jnp.expm1(jnp.float32(-BASE_LR)))
            lr = jax.nn.softplus(x @ W_lr + base_lr_inv)
            lr = lr.reshape(b, l, 3, h).transpose(2, 0, 3, 1).reshape(3, b * h, l, 1)
            lr0, lr1, lr2 = (lr[0], lr[1], lr[2])
            w0b = jnp.tile(w0, (b, 1, 1))
            w1b = jnp.tile(w1, (b, 1, 1))
            w2b = jnp.tile(w2, (b, 1, 1))
            momentum = jax.nn.sigmoid(x @ W_m + b_m)
            momentum = momentum.reshape(b, l, h, 1).transpose(0, 2, 1, 3).reshape(b * h, l, 1)
            out = block_causal_lact_swiglu(w0b, w1b, w2b, ttt_q, ttt_k, ttt_v, lr0, lr1, lr2, momentum)
            mu = jnp.mean(out, axis=-1, keepdims=True)
            var = jnp.mean(jnp.square(out - mu), axis=-1, keepdims=True)
            out = (out - mu) * jax.lax.rsqrt(var + LN_EPS) * ln_g + ln_b
            scale = silu(x @ W_s + b_s).reshape(b, l, h, 1).transpose(0, 2, 1, 3).reshape(b * h, l, 1)
            out = out * scale
            out = out.reshape(b, h, l, d).transpose(0, 2, 1, 3).reshape(b, l, h * d)
            return out @ W_o
        return _forward(x, W_qkv, W_lr, W_o, W_m, b_m, W_s, b_s, ln_g, ln_b, w0, w1, w2)

    def _L1_xattn_ref(draft_hidden, context_hidden, Wq, Wk, Wv, Wo, q_norm_w, k_norm_w, context_position_ids, draft_position_ids):
        import jax, jax.numpy as jnp
        import numpy as np
        B, CTX, DRAFT, D = (2, 512, 64, 256)
        H, KVH, HD = (16, 4, 128)
        N_REP = H // KVH
        EPS = 1e-06
        THETA = 10000.0
        SCALE = 1.0 / np.sqrt(HD).astype(np.float32)

        def _rms_norm(x, w):
            v = jnp.mean(jnp.square(x.astype(jnp.float32)), axis=-1, keepdims=True)
            return (w * (x.astype(jnp.float32) * jax.lax.rsqrt(v + EPS))).astype(x.dtype)

        def _rotate_half(x):
            x1, x2 = jnp.split(x, 2, axis=-1)
            return jnp.concatenate((-x2, x1), axis=-1)

        def _rope(x, pos):
            inv_freq = 1.0 / THETA ** (jnp.arange(0, HD, 2, dtype=jnp.float32) / HD)
            freqs = pos.astype(jnp.float32)[:, None, :, None] * inv_freq
            emb = jnp.concatenate((freqs, freqs), axis=-1)
            return x * jnp.cos(emb) + _rotate_half(x) * jnp.sin(emb)
        bsz, draft_len, _ = draft_hidden.shape
        ctx_len = context_hidden.shape[1]
        total_len = ctx_len + draft_len
        q = (draft_hidden @ Wq.T).reshape(bsz, draft_len, H, HD)
        q = _rms_norm(q, q_norm_w).transpose(0, 2, 1, 3)
        kv_in = jnp.concatenate([context_hidden, draft_hidden], axis=1)
        k = (kv_in @ Wk.T).reshape(bsz, total_len, KVH, HD)
        v = (kv_in @ Wv.T).reshape(bsz, total_len, KVH, HD).transpose(0, 2, 1, 3)
        k = _rms_norm(k, k_norm_w).transpose(0, 2, 1, 3)
        full_position_ids = jnp.concatenate([context_position_ids, draft_position_ids], axis=1)
        q = _rope(q, draft_position_ids)
        k = _rope(k, full_position_ids)
        k = jnp.repeat(k, N_REP, axis=1)
        v = jnp.repeat(v, N_REP, axis=1)
        scores = jnp.einsum('bhqd,bhkd->bhqk', q, k) * SCALE
        probs = jax.nn.softmax(scores, axis=-1)
        attn = jnp.einsum('bhqk,bhkd->bhqd', probs, v)
        attn = attn.transpose(0, 2, 1, 3).reshape(bsz, draft_len, H * HD)
        return attn @ Wo.T

    def _L1_ffn_ref(x, wa, rg, rgb, rw1, rb1, rw2, rb2, sg, sgb, sw1, sb1, sw2, sb2):
        import jax, jax.numpy as jnp
        import numpy as np
        B, S, D, F, E, SH, K = (2, 256, 256, 128, 16, 2, 2)

        def _experts_all(x, g, gb, w1, b1, w2, b2):
            y = jax.nn.gelu(jnp.einsum('bsd,edf->bsef', x, g) + gb, approximate=False)
            y = y * (jnp.einsum('bsd,edf->bsef', x, w1) + b1)
            return jnp.einsum('bsef,efd->bsed', y, w2) + b2
        aff = jax.nn.sigmoid(jnp.einsum('bsd,de->bse', x, wa))
        topk_p, topk_i = jax.lax.top_k(aff, K)
        topk_p = topk_p / jnp.sum(topk_p, axis=-1, keepdims=True)
        combine = jnp.sum(jax.nn.one_hot(topk_i, E, dtype=x.dtype) * topk_p[..., None], axis=2)
        routed = jnp.einsum('bsed,bse->bsd', _experts_all(x, rg, rgb, rw1, rb1, rw2, rb2), combine)
        shared = jnp.sum(_experts_all(x, sg, sgb, sw1, sb1, sw2, sb2), axis=2)
        return x + shared + routed
    x = _layernorm(x + _L0_attn_ref(x, L0_attn_W_in, L0_attn_conv_w, L0_attn_conv_b, L0_attn_W_x, L0_attn_W_dt, L0_attn_b_dt, L0_attn_A_log, L0_attn_D, L0_attn_W_out), axis=-1)
    x = _layernorm(x + _L0_xattn_ref(x, ctx_2048, ctx_2048), axis=-1)
    x = _layernorm(x + _L0_ffn_ref(x, L0_ffn_W1, L0_ffn_W2, L0_ffn_W3), axis=-1)
    x = _layernorm(x + _L1_attn_ref(x, L1_attn_W_qkv, L1_attn_W_lr, L1_attn_W_o, L1_attn_W_m, L1_attn_b_m, L1_attn_W_s, L1_attn_b_s, L1_attn_ln_g, L1_attn_ln_b, L1_attn_w0, L1_attn_w1, L1_attn_w2), axis=-1)
    x = _layernorm(x + _L1_xattn_ref(x, ctx_2048, L1_xattn_Wq, L1_xattn_Wk, L1_xattn_Wv, L1_xattn_Wo, L1_xattn_q_norm_w, L1_xattn_k_norm_w, pos_BxS2, itok_BxS_4096_4607), axis=-1)
    x = _layernorm(x + _L1_ffn_ref(x, L1_ffn_wa, L1_ffn_rg, L1_ffn_rgb, L1_ffn_rw1, L1_ffn_rb1, L1_ffn_rw2, L1_ffn_rb2, L1_ffn_sg, L1_ffn_sgb, L1_ffn_sw1, L1_ffn_sb1, L1_ffn_sw2, L1_ffn_sb2), axis=-1)
    return x

_drawn_inputs = setup_inputs


def setup_inputs(seed=0):
    import zlib

    import numpy as np

    out = dict(_drawn_inputs(seed))
    spreads = {'L0_attn_D': (1.0, 0.6),
     'L1_attn_b_m': (0.0, 0.1),
     'L1_attn_b_s': (0.0, 0.8),
     'L1_attn_ln_g': (1.0, 0.2),
     'L1_attn_ln_b': (0.0, 0.1),
     'L1_xattn_q_norm_w': (1.0, 0.6),
     'L1_xattn_k_norm_w': (1.0, 0.6),
     'L1_ffn_rgb': (0.0, 0.8),
     'L1_ffn_rb1': (0.0, 0.8),
     'L1_ffn_rb2': (0.0, 0.8),
     'L1_ffn_sgb': (0.0, 0.8),
     'L1_ffn_sb1': (0.0, 0.8),
     'L1_ffn_sb2': (0.0, 0.496)}
    factors = {'L0_attn_W_in': 8.0,
     'L0_attn_conv_w': 8.0,
     'L0_attn_conv_b': 8.0,
     'L0_attn_W_x': 8.0,
     'L0_attn_W_dt': 8.0,
     'L0_attn_b_dt': 8.0,
     'L0_attn_A_log': 8.0,
     'L0_attn_W_out': 8.0,
     'L1_ffn_rg': 8.0,
     'L1_ffn_rw1': 8.0,
     'L1_ffn_rw2': 8.0,
     'L1_ffn_sg': 6.238,
     'L1_ffn_sw1': 6.028,
     'L1_ffn_sw2': 5.797}
    for name, (base, spread) in spreads.items():
        noise = np.random.default_rng([zlib.crc32(name.encode()), seed]).standard_normal(out[name].shape)
        drawn = base * np.exp(spread * noise) if base else spread * noise
        out[name] = jnp.asarray(drawn.astype(out[name].dtype))
    for name, factor in factors.items():
        out[name] = (out[name] * factor).astype(out[name].dtype)
    return out
```

```python
from contextlib import ExitStack

import numpy as np

import concourse.bass as bass
from concourse import mybir

F32 = mybir.dt.float32
BF16 = mybir.dt.bfloat16
I32 = mybir.dt.int32
U32 = mybir.dt.uint32
ALU = mybir.AluOpType
ACT = mybir.ActivationFunctionType
AX = mybir.AxisListType

P = 128
B, L, D = 4, 256, 256
T = B * L
NT = T // P
KD = D // P
LN_EPS = 1e-5

DI, NS, DCONV, RANK = 512, 16, 4, 128
NBLK = DI // P
PAD = L + DCONV - 1
STEP0_DT = 1e28

XH = 8
XR = L // XH
XSCALE = float(1.0 / np.sqrt(np.float32(XR)))

FF = 1024
NFB = FF // P

TH, THD = 2, 128
TTT_EPS = 1e-6

QH, KVH, HD = 16, 4, 128
CTXT_TILES = L // P
KT = 2 * CTXT_TILES
ROPE = HD // 2
ASCALE = float(np.float32(1.0 / np.sqrt(HD).astype(np.float32)))
RMS_EPS = 1e-6

NE, NSH, EF = 16, 2, 128
NX = NE + NSH



class Region:

    def __init__(self, start):
        self.at = start

    def take(self, words):
        start, self.at = self.at, self.at + words
        return start, words


PACKS = {
    "in": [("xT", KD * T), ("w_inT", KD * 2 * DI)],
    "mamba": [("w_xT", NBLK * (RANK + 2 * NS)), ("w_dtT", DI), ("w_outT", NBLK * D), ("conv_w", NBLK * DCONV),
              ("conv_b", NBLK), ("b_dt", NBLK), ("a_log", NBLK * NS), ("d_skip", NBLK),
              ("sel3", 2 * NS)],
    "ident": [("ident", P)],
    "x": [("x", NT * D)],
    "ctx": [("ctx", NT * D), ("ctxT", KD * T)],
    "ttt": [("w_qs", KD * (TH * THD + TH)), ("w0T", TH * P), ("w2T", TH * P), ("w1T", TH * P), ("w_oT", TH * D),
            ("ln_g", P), ("ln_b", P), ("b_s", TH)],
    "ffn": [("ffn1T", KD * FF), ("ffn3T", KD * FF), ("ffn2T", NFB * D), ("hadamard", P)],
    "attn": [("wqT", KD * QH * HD), ("wkT", KD * KVH * HD), ("wvT", KD * KVH * HD), ("woT", QH * D),
             ("q_w", HD), ("q_w_swap", HD), ("k_w", HD), ("k_w_swap", HD), ("inv_freq", ROPE)],
    "moe": [("wa", KD * NE), ("wg", NX * KD * EF), ("w1", NX * KD * EF), ("w2", NX * D), ("gb", NX), ("b1", NX),
            ("b2", D), ("iota", NE)],
}


def pack_words(name):
    return sum(w for _, w in PACKS[name])

ROUND = float(1.5 * 2 ** 23)
TURN_HI = 6.28125
TURN_LO = float(2 * np.pi - TURN_HI)
PI_MAX = 3.1415925

SEMAPHORES = """
    x_added x_ready stored xt_ready xt_ps xs_copied proj_ps u_ready z_ready dbl_ps dtr_copied bc_ready dt_ps
    spz_ready hc_ready y_used hc_summed dbu_ready b_ps c_copied c_ps y_ready out_ps p_ready sc_ps pt_odd pt_even
    pt_ps ot_ready o_ps bf_ready had_ps w2h_ready hid_ready up_ps q4_copied q4_ps q4_ready qt4_copied qt4_ps
    gh_ready f4_ps o4_copied o4_ps o4_normed ot4_copied ot4_ps kq_copied kq_ps rope_sum tr_copied k_scaled tr_ps
    at_copied pt5_copied p5_ready at_ps v_ps v_copied s5_ps p5_normed pt5_ps aff_ps cmb_ready ct_ps ct_ready
    ye_ready ge_ps cb_ps ft_copied ye_used ln_var ln_std conv_done a_exp act_step spa_ready dt_ready a_ready
    h_ready da_ready nbias_ready sg_ready s4_copied s4_raw s4_ready ss4_ready ss4_std sg4_ready o4_var o4_std
    ang_ready sines_ready ss_ready sq_ready rs_std nb5_ready aff_exp ct_copied ge_ready dve_step t1_ready
    krs_ready
"""

LAST = 6


def decoder(nc: bass.Bass, dram, out: bass.AP):
    with ExitStack() as ctx:
        def sem(name):
            return ctx.enter_context(nc.semaphore(name))

        kept = Region(0)
        X_ = kept.take(NT * D)
        XT_ = kept.take(KD * T)
        CTX_ = kept.take(NT * D)
        CTXT_ = kept.take(KD * T)
        IDENT_ = kept.take(P)
        SMALL_ = kept.take(512)
        TTTW_ = kept.take(pack_words("ttt"))
        wa_start = kept.at
        wb_start = wa_start + max(pack_words("moe"), pack_words("ffn") + NFB * D)
        c_start = wb_start + pack_words("attn")
        total = c_start + 17248

        arena = ctx.enter_context(nc.sbuf_tensor("arena", [P, total], F32))
        psum = ctx.enter_context(nc.psum_tensor("psum", [P, 8, 512], F32))
        pos_i = ctx.enter_context(nc.sbuf_tensor("pos_i", [P, B * KT], I32))
        top_i = ctx.enter_context(nc.sbuf_tensor("top_i", [P, NT, 8], U32))

        def view(span, parts=P):
            return arena[0:parts, span[0]:span[0] + span[1]]

        def views(name, start):
            r = Region(start)
            got = {part: view(r.take(w)) for part, w in PACKS[name]}
            return got, arena[:, start:start + pack_words(name)]

        def bank(b, n=1):
            return psum[:, b:b + n, :].rearrange("p b n -> p (b n)")

        X = view(X_).rearrange("p (t d) -> p t d", t=NT)
        XT = view(XT_).rearrange("p (k t) -> p k t", k=KD)
        ident = view(IDENT_)
        CTX = view(CTX_).rearrange("p (t d) -> p t d", t=NT)
        CTXT = view(CTXT_).rearrange("p (k t) -> p k t", k=KD)
        small = Region(SMALL_[0])

        def tiny(words):
            return view(small.take(words))

        eps_ln = tiny(1)
        eps_ttt = tiny(1)
        eps_rms = tiny(1)
        one = tiny(1)
        stats = tiny(TH * NT * 6).rearrange("p (t s) -> p t s", s=6)
        mv = tiny(TH * NT * 2).rearrange("p (t s) -> p t s", s=2)
        var = tiny(TH * NT)
        std = tiny(TH * NT)
        rstd = tiny(TH * NT)
        nmax = tiny(16)
        nbias = tiny(16)
        psums = tiny(16)
        rinv = tiny(16)
        a_neg = tiny(NBLK * NS)
        sum_sq = tiny(TH * NT)
        s_raw = tiny(NT * TH)
        s_gate = tiny(NT * TH)
        pos_f = tiny(B * KT)
        sel3 = tiny(NS).bitcast(BF16)
        assert small.at <= SMALL_[0] + SMALL_[1], small.at - SMALL_[0]

        ttt_w, ttt_all = views("ttt", TTTW_[0])

        wa = Region(wa_start)
        XS = view(wa.take(NBLK * B * PAD)).rearrange("p (m b t) -> p m b t", m=NBLK, b=B)
        YS = view((wa_start, NBLK * T)).rearrange("p (m t) -> p m t", m=NBLK)
        ZS = view(wa.take(NBLK * T)).rearrange("p (m t) -> p m t", m=NBLK)
        U = view(wa.take(NBLK * T)).rearrange("p (m t) -> p m t", m=NBLK)
        assert wa.at <= wb_start
        wb = Region(wb_start)
        DT = view(wb.take(NBLK * T)).rearrange("p (m t) -> p m t", m=NBLK)
        DTU = view(wb.take(NBLK * T)).rearrange("p (m t) -> p m t", m=NBLK)
        DTR = view(wb.take(T))
        assert wb.at <= c_start
        c1 = Region(c_start)
        w_inT = view(c1.take(KD * 2 * DI)).rearrange("p (k n) -> p k n", k=KD)
        mb_start = c1.take(pack_words("mamba"))[0]
        mb, mb_all = views("mamba", mb_start)
        loop = Region(c1.take(8 * T)[0])
        loop_words = (loop.at, 8 * T)
        DBU = view(loop.take(2 * T)).rearrange("p (i t) -> p i t", i=2)
        H = view(loop.take(2 * T)).rearrange("p (i t) -> p i t", i=2)
        HC = view(loop.take(2 * T)).rearrange("p (i t) -> p i t", i=2)
        CB = view(loop.take(2 * T)).rearrange("p (i t) -> p i t", i=2)
        SPZ = view((loop_words[0], NBLK * T)).rearrange("p (m t) -> p m t", m=NBLK)
        SPA = view((loop_words[0] + NBLK * T, NBLK * T)).rearrange("p (m t) -> p m t", m=NBLK)
        bc3 = view(c1.take(T // 2)).bitcast(BF16)
        bc_rest = view(c1.take(T))
        bc_mid = view(c1.take(T // 2)).bitcast(BF16)
        assert c1.at <= total, (c1.at, total)

        w_xT = mb["w_xT"].rearrange("p (m n) -> p m n", m=NBLK)
        w_outT = mb["w_outT"].rearrange("p (m n) -> p m n", m=NBLK)
        conv_w = mb["conv_w"].rearrange("p (m k) -> p m k", m=NBLK)
        a_log = mb["a_log"]
        N3 = 3 * 2 * NS

        c2 = Region(c_start)
        PR = view(c2.take(2 * 8 * L)).rearrange("p (i j m n) -> p i j m n", i=2, j=4, m=2)
        PT = view(c2.take(2 * 2 * L)).rearrange("p (i n m) -> p i n m", i=2, n=2)
        OT = view(c2.take(2 * P)).rearrange("p (i m c) -> p i m c", i=1, m=2)
        ffn, ffn_all = views("ffn", wa_start)
        fw1 = ffn["ffn1T"].rearrange("p (k n) -> p k n", k=KD)
        fw3 = ffn["ffn3T"].rearrange("p (k n) -> p k n", k=KD)
        fw2 = ffn["ffn2T"].rearrange("p (k d) -> p k d", k=NFB)
        fw2b = view((wa_start + pack_words("ffn"), NFB * D)).rearrange("p (k d) -> p k d", k=NFB)
        c3 = Region(c_start)
        HID = view(c3.take(NFB * T)).rearrange("p (k t) -> p k t", k=NFB)
        SG = view(c3.take(2 * 512)).rearrange("p (i t) -> p i t", i=2)
        w_qs = ttt_w["w_qs"].rearrange("p (k n) -> p k n", k=KD)
        w0T = ttt_w["w0T"].rearrange("p (h n) -> p h n", h=TH)
        w2T = ttt_w["w2T"].rearrange("p (h n) -> p h n", h=TH)
        w1T = ttt_w["w1T"].rearrange("p (h n) -> p h n", h=TH)
        w_oT = ttt_w["w_oT"].rearrange("p (h n) -> p h n", h=TH)
        c4 = Region(c_start)
        Q4 = view(c4.take(NT * D)).rearrange("p (t d) -> p t d", t=NT)
        SQ4 = view(c4.take(NT * D)).rearrange("p (t d) -> p t d", t=NT)
        QT4 = view(c4.take(TH * T)).rearrange("p (h b t) -> p h b t", h=TH, b=B)
        GH = view(c4.take(TH * T)).rearrange("p (h t) -> p h t", h=TH)
        SG4 = view(c4.take(2 * 512)).rearrange("p (i t) -> p i t", i=2)
        O4 = view(c4.take(NT * D)).rearrange("p (t d) -> p t d", t=NT)
        OT4 = view(c4.take(TH * T)).rearrange("p (h t) -> p h t", h=TH)
        assert c4.at <= total
        attn, attn_all = views("attn", wb_start)
        wqT = attn["wqT"].rearrange("p (k n) -> p k n", k=KD)
        wkT = attn["wkT"].rearrange("p (k n) -> p k n", k=KD)
        wvT = attn["wvT"].rearrange("p (k n) -> p k n", k=KD)
        woT = attn["woT"].rearrange("p (h n) -> p h n", h=QH)
        tab = Region(CTX_[0])
        KCOS = view(tab.take(KT * HD)).rearrange("p (t d) -> p t d", t=KT)
        KSIN = view(tab.take(KT * HD)).rearrange("p (t d) -> p t d", t=KT)
        QCOS = view(tab.take(2 * HD)).rearrange("p (t d) -> p t d", t=2)
        QSIN = view(tab.take(2 * HD)).rearrange("p (t d) -> p t d", t=2)
        assert tab.at <= CTX_[0] + CTX_[1]
        tmp5 = Region(TTTW_[0])
        RT1 = view(tmp5.take(2 * 512)).rearrange("p (i n) -> p i n", i=2)
        RAW5 = view(tmp5.take(2 * 512)).rearrange("p (i n) -> p i n", i=2)
        assert tmp5.at <= TTTW_[0] + TTTW_[1]
        c5 = Region(c_start)
        KTR = view(c5.take(KVH * 2 * L)).rearrange("p (h t) -> p h t", h=KVH)
        V5 = view(c5.take(KT * KVH * HD)).rearrange("p (t n) -> p t n", t=KT)
        QTR = view(c5.take(QH * L)).rearrange("p (h t) -> p h t", h=QH)
        AT = view(c5.take(QH * L)).rearrange("p (h t) -> p h t", h=QH)
        PR5 = view(c5.take(2 * 2 * 512)).rearrange("p (i m n) -> p i m n", i=2, m=2)
        ANG = view((c5.at - 2048, 3 * KT * ROPE)).rearrange("p (i t f) -> p i t f", i=3, t=KT)
        PT5 = view(c5.take(KT * L)).rearrange("p (k n) -> p k n", k=KT)
        RT2 = view(c5.take(512))
        SQ5 = view(c5.take(512))
        SINES = view(c5.take(3 * KT * ROPE)).rearrange("p (i t f) -> p i t f", i=3, t=KT)
        q_ss = view(c5.take(2 * QH))
        q_rs = view(c5.take(2 * QH))
        k_ss = view(c5.take(KT * KVH))
        k_rs = view(c5.take(KT * KVH))
        assert c5.at <= total, (c5.at, total)
        moe, moe_all = views("moe", wa_start)
        wa6 = moe["wa"].rearrange("p (k e) -> p k e", k=KD)
        wg6 = moe["wg"].rearrange("p (e k f) -> p e k f", e=NX, k=KD)
        w16 = moe["w1"].rearrange("p (e k f) -> p e k f", e=NX, k=KD)
        w26 = moe["w2"].rearrange("p (e d) -> p e d", e=NX)
        c6 = Region(c_start)
        AFF = view(c6.take(NT * NE)).rearrange("p (t e) -> p t e", t=NT)
        TOP = view(c6.take(NT * 8)).rearrange("p (t e) -> p t e", t=NT)
        TOPI = view(c6.take(NT * 8)).rearrange("p (t e) -> p t e", t=NT)
        PW = view(c6.take(NT * 2)).rearrange("p (t e) -> p t e", t=NT)
        PS = view(c6.take(NT))
        CMB = view(c6.take(NT * 2 * NS)).rearrange("p (t e) -> p t e", t=NT)
        PICK = view(c6.take(NT * NE)).rearrange("p (t e) -> p t e", t=NT)
        CT = view(c6.take(T))
        ct_rest = view(c6.take(T))
        ct_mid = view(c6.take(T // 2)).bitcast(BF16)
        ct3 = view(c6.take(T // 2)).bitcast(BF16)
        GE = view(c6.take(2 * 512)).rearrange("p (i t) -> p i t", i=2)
        YE = view(c6.take(2 * 512)).rearrange("p (i t) -> p i t", i=2)
        FT = view(c6.take(KD * T)).rearrange("p (k t) -> p k t", k=KD)
        assert c6.at <= total

        ld = {n: sem("loaded_" + n) for n in list(PACKS) + ["pos"]}
        consts_ready = sem("consts_ready")
        S = {n: sem(n) for n in SEMAPHORES.split()}

        block = ctx.enter_context(nc.Block())

        @block.sync
        def _(sp):
            sp.dma_start(arena[:, XT_[0]:XT_[0] + XT_[1]], dram["in"][:, 0:KD * T]).then_inc(ld["in"], 16)
            sp.dma_start(w_inT.rearrange("p k n -> p (k n)"), dram["in"][:, KD * T:]).then_inc(ld["in"], 16)
            sp.dma_start(mb_all, dram["mamba"]).then_inc(ld["mamba"], 16)
            sp.dma_start(ident, dram["ident"]).then_inc(ld["ident"], 16)
            sp.dma_start(arena[:, X_[0]:X_[0] + X_[1]], dram["x"]).then_inc(ld["x"], 16)
            sp.dma_start(arena[:, CTX_[0]:CTX_[0] + 2 * CTX_[1]], dram["ctx"]).then_inc(ld["ctx"], 16)
            sp.dma_start(ttt_all, dram["ttt"]).then_inc(ld["ttt"], 16)
            sp.dma_start(pos_i[:, :], dram["pos"]).then_inc(ld["pos"], 16)
            if LAST >= 3:
                sp.wait_ge(S["x_added"], NT)
                sp.dma_start(ffn_all, dram["ffn"]).then_inc(ld["ffn"], 16)
            if LAST >= 5:
                sp.dma_start(attn_all, dram["attn"]).then_inc(ld["attn"], 16)
            if LAST >= 6:
                sp.wait_ge(S["x_added"], 3 * NT)
                sp.dma_start(moe_all, dram["moe"]).then_inc(ld["moe"], 16)
            for i in range(NT):
                sp.wait_ge(S["x_ready"], NT * (LAST - 1) + i + 1)
                sp.dma_start(out[i * P:(i + 1) * P, :], X[:, i, :]).then_inc(S["stored"], 16)
            sp.wait_ge(S["stored"], 16 * NT)

        @block.tensor
        def _(pe):
            def turn_x(k):
                for i in range(NT):
                    pe.wait_ge(S["x_ready"], NT * (k - 1) + i + 1)
                    if i >= 2:
                        pe.wait_ge(S["xt_ready"], NT * (k - 2) + i - 1)
                    for f in range(KD):
                        mm = pe.transpose(psum[:, 6 + i % 2, f * P:(f + 1) * P], X[:, i, f * P:(f + 1) * P], ident)
                    mm.then_inc(S["xt_ps"], 1)
                pe.wait_ge(S["xt_ready"], NT * (k - 1))

            def mamba():
                pe.wait_ge(ld["in"], 32)
                for g in range(16):
                    m, n = g // 2, g % 2
                    if g >= 8:
                        pe.wait_ge(S["xs_copied"], g - 7)
                    for k in range(KD):
                        mm = pe.matmul(bank(g % 8), w_inT[:, k, m * P:(m + 1) * P], XT[:, k, n * 512:(n + 1) * 512],
                                       start=(k == 0), stop=(k == KD - 1))
                    mm.then_inc(S["proj_ps"], 1)
                pe.wait_ge(ld["mamba"], 16)
                pe.wait_ge(S["u_ready"], NBLK)
                pe.wait_ge(S["z_ready"], 8)
                for g in range(4):
                    n = g % 2
                    lo, width = (0, RANK) if g < 2 else (RANK, 2 * NS)
                    for m in range(NBLK):
                        mm = pe.matmul(psum[0:width, g, :], w_xT[:, m, lo:lo + width], U[:, m, n * 512:(n + 1) * 512],
                                       start=(m == 0), stop=(m == NBLK - 1))
                    mm.then_inc(S["dbl_ps"], 1)
                pe.wait_ge(S["dtr_copied"], 1)
                for m in range(NBLK):
                    if m == 3:
                        pe.wait_ge(S["bc_ready"], 2)
                    for n in range(2):
                        mm = pe.matmul(bank((4 + 2 * m) % 8 + n), mb["w_dtT"][:, m * P:(m + 1) * P],
                                       DTR[:, n * 512:(n + 1) * 512], start=True, stop=True)
                    mm.then_inc(S["dt_ps"], 1)
                pe.wait_ge(S["spz_ready"], NBLK)

                def sum_y(it):
                    m, s = it // NS, it % NS
                    pe.wait_ge(S["hc_ready"], it + 1)
                    if s == 0 and m > 0:
                        pe.wait_ge(S["y_used"], m)
                    for n in range(2):
                        mm = pe.matmul(bank(6 + n), ident, HC[:, it % 2, n * 512:(n + 1) * 512],
                                       start=(s == 0), stop=(s == NS - 1))
                    mm.then_inc(S["hc_summed"], 1)

                pe.wait_ge(S["bc_ready"], 2)
                pe.wait_ge(ld["ident"], 16)
                for it in range(NBLK * NS):
                    s = it % NS
                    if it > 0:
                        pe.wait_ge(S["dbu_ready"], it)
                    for n in range(2):
                        mm = pe.matmul(bank(n), sel3[0:N3, s:s + 1].broadcast_to([N3, P]), bc3[0:N3, n * 512:(n + 1) * 512],
                                       start=True, stop=True)
                    mm.then_inc(S["b_ps"], 1)
                    if it > 0:
                        pe.wait_ge(S["c_copied"], it)
                    for n in range(2):
                        mm = pe.matmul(bank(2 + n), sel3[0:N3, NS + s:NS + s + 1].broadcast_to([N3, P]),
                                       bc3[0:N3, n * 512:(n + 1) * 512], start=True, stop=True)
                    mm.then_inc(S["c_ps"], 1)
                    if it > 0:
                        sum_y(it - 1)
                sum_y(NBLK * NS - 1)
                pe.wait_ge(S["y_ready"], NBLK)
                for i in range(NT):
                    if i >= 4:
                        pe.wait_ge(S["x_added"], i - 3)
                    for m in range(NBLK):
                        mm = pe.matmul(psum[:, i % 4, 0:D], YS[:, m, i * P:(i + 1) * P], w_outT[:, m, :],
                                       start=(m == 0), stop=(m == NBLK - 1))
                    mm.then_inc(S["out_ps"], 1)

            def cross1():
                pe.wait_ge(ld["ctx"], 16)

                def scores(i):
                    pe.wait_ge(S["x_ready"], i + 1)
                    if i > 0:
                        pe.wait_ge(S["p_ready"], 8 * i)
                    for mt in range(2):
                        for j in range(4):
                            rows = slice(XR * j, XR * (j + 1))
                            mm = pe.matmul(psum[:, j, mt * L:(mt + 1) * L], X[rows, i, mt * P:(mt + 1) * P],
                                           CTX[rows, i, :], start=True, stop=True)
                    mm.then_inc(S["sc_ps"], 1)

                def turn_p(i, j):
                    g = 4 * i + j
                    pe.wait_ge(S["p_ready"], 8 * i + 2 * j + 2)
                    if g >= 2:
                        pe.wait_ge(S["pt_odd" if j % 2 else "pt_even"], g // 2)
                    for mt in range(2):
                        for nb in range(2):
                            mm = pe.transpose(psum[:, 4 + j % 2, nb * L + mt * P:nb * L + (mt + 1) * P],
                                              PR[:, i % 2, j, mt, nb * P:(nb + 1) * P], ident)
                    mm.then_inc(S["pt_ps"], 1)

                def weigh(i, j):
                    b, half = i // 2, i % 2
                    g = 4 * i + j
                    pe.wait_ge(S["pt_odd" if j % 2 else "pt_even"], g // 2 + 1)
                    if j == 0 and i > 0:
                        pe.wait_ge(S["ot_ready"], i)
                    col = b * L + half * P + XR * j
                    for mt in range(2):
                        for nb in range(2):
                            mm = pe.matmul(psum[:, 6, mt * P + XR * j:mt * P + XR * (j + 1)],
                                           PT[:, j % 2, nb, mt * P:(mt + 1) * P], CTXT[:, nb, col:col + XR],
                                           start=(nb == 0), stop=(nb == 1))
                    if j == 3:
                        mm.then_inc(S["o_ps"], 1)

                def turn_o(i):
                    pe.wait_ge(S["ot_ready"], i + 1)
                    if i > 0:
                        pe.wait_ge(S["x_added"], NT + i)
                    for mt in range(2):
                        mm = pe.transpose(psum[:, 7, mt * P:(mt + 1) * P], OT[:, 0, mt, :], ident)
                    mm.then_inc(S["out_ps"], 1)

                for i in range(NT + 1):
                    if i < NT:
                        scores(i)
                    if i >= 2:
                        turn_o(i - 2)
                    if i >= 1:
                        turn_p(i - 1, 0)
                        for j in range(4):
                            if j < 3:
                                turn_p(i - 1, j + 1)
                            weigh(i - 1, j)
                turn_o(NT - 1)

            def swiglu():
                pe.wait_ge(ld["ffn"], 16)
                pe.wait_ge(S["bf_ready"], 6)
                for g in range(4):
                    if g == 0:
                        pe.wait_ge(S["p_ready"], 8 * NT)
                    mm = pe.matmul(bank(g), ffn["hadamard"], fw2b[:, 2 * g:2 * g + 2, :].rearrange("p k d -> p (k d)"),
                                   start=True, stop=True)
                    mm.then_inc(S["had_ps"], 1)
                turn_x(2)
                pe.wait_ge(S["w2h_ready"], 4)
                for g in range(2 * NFB):
                    n, h = g // NFB, g % NFB
                    if g >= 2:
                        pe.wait_ge(S["hid_ready"], g - 1)
                    for w, b0 in ((fw1, 0), (fw3, 2)):
                        for k in range(KD):
                            mm = pe.matmul(bank(b0 + g % 2), w[:, k, h * P:(h + 1) * P], XT[:, k, n * 512:(n + 1) * 512],
                                           start=(k == 0), stop=(k == KD - 1))
                        mm.then_inc(S["up_ps"], 1)
                for i in range(NT):
                    pe.wait_ge(S["hid_ready"], NFB * (1 + i // 4))
                    if i >= 2:
                        pe.wait_ge(S["x_added"], 2 * NT + i - 1)
                    for h in range(NFB):
                        mm = pe.matmul(psum[:, 4 + i % 2, 0:D], HID[:, h, i * P:(i + 1) * P], fw2[:, h, :],
                                       start=(h == 0), stop=(h == NFB - 1))
                    mm.then_inc(S["out_ps"], 1)

            def ttt():
                pe.wait_ge(ld["ttt"], 16)
                turn_x(3)
                for i in range(NT):
                    if i >= 4:
                        pe.wait_ge(S["q4_copied"], i - 3)
                    for k in range(KD):
                        mm = pe.matmul(psum[:, i % 4, 0:D + TH], XT[:, k, i * P:(i + 1) * P], w_qs[:, k, :],
                                       start=(k == 0), stop=(k == KD - 1))
                    mm.then_inc(S["q4_ps"], 1)
                pe.wait_ge(S["q4_ready"], 1)
                for i in range(NT):
                    if i >= 2:
                        pe.wait_ge(S["qt4_copied"], i - 1)
                    for h in range(TH):
                        mm = pe.transpose(psum[:, 4 + i % 2, h * P:(h + 1) * P], Q4[:, i, h * P:(h + 1) * P], ident)
                    mm.then_inc(S["qt4_ps"], 1)
                pe.wait_ge(S["qt4_copied"], NT)
                for g in range(4):
                    h, n = g // 2, g % 2
                    if g >= 2:
                        pe.wait_ge(S["gh_ready"], g - 1)
                    rhs = QT4[:, h, 2 * n:2 * n + 2, :].rearrange("p b t -> p (b t)")
                    pe.matmul(bank(g % 2), w0T[:, h, :], rhs, start=True, stop=True).then_inc(S["f4_ps"], 1)
                    pe.matmul(bank(2 + g % 2), w2T[:, h, :], rhs, start=True, stop=True).then_inc(S["f4_ps"], 1)
                pe.wait_ge(S["gh_ready"], 4)
                for i in range(NT):
                    if i >= 2:
                        pe.wait_ge(S["o4_copied"], i - 1)
                    for h in range(TH):
                        mm = pe.matmul(psum[:, 4 + i % 2, h * P:(h + 1) * P], GH[:, h, i * P:(i + 1) * P], w1T[:, h, :],
                                       start=True, stop=True)
                    mm.then_inc(S["o4_ps"], 1)
                for i in range(NT):
                    pe.wait_ge(S["o4_normed"], i + 1)
                    if i >= 2:
                        pe.wait_ge(S["ot4_copied"], i - 1)
                    for h in range(TH):
                        mm = pe.transpose(psum[:, 6 + i % 2, h * P:(h + 1) * P], O4[:, i, h * P:(h + 1) * P], ident)
                    mm.then_inc(S["ot4_ps"], 1)
                for i in range(NT):
                    pe.wait_ge(S["ot4_copied"], i + 1)
                    if i >= 4:
                        pe.wait_ge(S["x_added"], 3 * NT + i - 3)
                    for h in range(TH):
                        mm = pe.matmul(psum[:, i % 4, 0:D], OT4[:, h, i * P:(i + 1) * P], w_oT[:, h, :],
                                       start=(h == 0), stop=(h == TH - 1))
                    mm.then_inc(S["out_ps"], 1)

            def cross2():
                pe.wait_ge(ld["attn"], 16)
                turn_x(4)
                for b in range(B):
                    def tile_T(t):
                        src, i = (CTXT, b * 2 + t) if t < 2 else (XT, b * 2 + t - 2)
                        return lambda k: src[:, k, i * P:(i + 1) * P]

                    def project(n, lhs, w, lo):
                        g = 12 * b + n
                        if g >= 2:
                            pe.wait_ge(S["kq_copied"], g - 1)
                        for k in range(KD):
                            mm = pe.matmul(bank(6 + n % 2), lhs(k), w[:, k, lo:lo + 512], start=(k == 0), stop=(k == KD - 1))
                        mm.then_inc(S["kq_ps"], 1)

                    def turn(n):
                        g = 12 * b + n
                        pe.wait_ge(S["rope_sum"], g + 1)
                        if g >= 2:
                            pe.wait_ge(S["tr_copied"], g - 1)
                        if n < KT:
                            pe.wait_ge(S["k_scaled"], KT * b + n + 1)
                        for h in range(4):
                            mm = pe.transpose(psum[:, 4 + n % 2, h * P:(h + 1) * P], RT1[:, n % 2, h * P:(h + 1) * P], ident)
                        mm.then_inc(S["tr_ps"], 1)

                    if b > 0:
                        pe.wait_ge(S["x_added"], 4 * NT + 2 * b)
                        pe.wait_ge(S["at_copied"], QH * b)
                        pe.wait_ge(S["pt5_copied"], 2 * QH * b)
                        pe.wait_ge(S["p5_ready"], 2 * QH * b)
                    for n in range(KT + 1):
                        if n < KT:
                            project(n, tile_T(n), wkT, 0)
                        if n >= 1:
                            turn(n - 1)
                    for t in range(KT):
                        if t == 0 and b > 0:
                            pe.wait_ge(S["at_ps"], QH * b)
                        lhs = tile_T(t)
                        for k in range(KD):
                            mm = pe.matmul(bank(t), lhs(k), wvT[:, k, :], start=(k == 0), stop=(k == KD - 1))
                        mm.then_inc(S["v_ps"], 1)
                    for n in range(KT, 13):
                        if n < 12:
                            c, t = divmod(n - KT, 2)
                            project(n, tile_T(2 + t), wqT, c * 512)
                        if n > KT:
                            turn(n - 1)
                    pe.wait_ge(S["tr_copied"], 12 * (b + 1))
                    pe.wait_ge(S["v_copied"], KT * (b + 1))

                    def scores(h):
                        g = QH * b + h
                        if h >= 2:
                            pe.wait_ge(S["p5_ready"], 2 * (g - 1))
                        for m in range(2):
                            mm = pe.matmul(bank(2 * (h % 2) + m), QTR[:, h, m * P:(m + 1) * P], KTR[:, h // 4, :],
                                           start=True, stop=True)
                            mm.then_inc(S["s5_ps"], 1)

                    def turn_p(h):
                        for m in range(2):
                            g = 2 * (QH * b + h) + m
                            pe.wait_ge(S["p5_normed"], g + 1)
                            if g >= 2:
                                pe.wait_ge(S["pt5_copied"], g - 1)
                            for kt in range(KT):
                                mm = pe.transpose(psum[:, 4 + m, kt * P:(kt + 1) * P],
                                                  PR5[:, h % 2, m, kt * P:(kt + 1) * P], ident)
                            mm.then_inc(S["pt5_ps"], 1)

                    def weigh(h):
                        g = QH * b + h
                        pe.wait_ge(S["pt5_copied"], 2 * (g + 1))
                        if h >= 1:
                            pe.wait_ge(S["at_copied"], g)
                        for kt in range(KT):
                            mm = pe.matmul(psum[:, 6, 0:L], V5[:, kt, (h // 4) * HD:(h // 4 + 1) * HD],
                                           PT5[:, kt, :], start=(kt == 0), stop=(kt == KT - 1))
                        mm.then_inc(S["at_ps"], 1)

                    scores(0)
                    scores(1)
                    for h in range(QH):
                        turn_p(h)
                        if h + 2 < QH:
                            scores(h + 2)
                        weigh(h)
                    pe.wait_ge(S["at_copied"], QH * (b + 1))
                    for m in range(2):
                        if m == 1:
                            pe.wait_ge(S["x_added"], 4 * NT + 2 * b + 1)
                        for h in range(QH):
                            mm = pe.matmul(psum[:, 7, 0:D], AT[:, h, m * P:(m + 1) * P], woT[:, h, :],
                                           start=(h == 0), stop=(h == QH - 1))
                        mm.then_inc(S["out_ps"], 1)

            def experts():
                pe.wait_ge(ld["moe"], 16)
                turn_x(5)
                for i in range(NT):
                    for k in range(KD):
                        mm = pe.matmul(psum[:, 0, i * NE:(i + 1) * NE], XT[:, k, i * P:(i + 1) * P], wa6[:, k, :],
                                       start=(k == 0), stop=(k == KD - 1))
                mm.then_inc(S["aff_ps"], 1)
                pe.wait_ge(S["cmb_ready"], 1)
                for i in range(NT):
                    mm = pe.transpose(psum[0:2 * NS, 4 + i // 4, (i % 4) * P:(i % 4 + 1) * P], CMB[:, i, :], ident)
                mm.then_inc(S["ct_ps"], 1)
                pe.wait_ge(S["ct_ready"], 2)

                def up(g):
                    n, e = g // NX, g % NX
                    if g >= 2:
                        pe.wait_ge(S["ye_ready"], g - 1)
                    for w, b0 in ((wg6, 2), (w16, 4)):
                        for k in range(KD):
                            mm = pe.matmul(bank(b0 + g % 2), w[:, e, k, :], XT[:, k, n * 512:(n + 1) * 512],
                                           start=(k == 0), stop=(k == KD - 1))
                        mm.then_inc(S["ge_ps"], 1)
                    if e < NE:
                        pe.matmul(bank(6 + g % 2), sel3[0:N3, e:e + 1].broadcast_to([N3, P]),
                                  ct3[0:N3, n * 512:(n + 1) * 512], start=True, stop=True).then_inc(S["cb_ps"], 1)

                def down(g):
                    n, e = g // NX, g % NX
                    if e == 0:
                        if n == 1:
                            pe.wait_ge(S["ft_copied"], 2)
                        for f in range(KD):
                            pe.matmul(bank(f), moe["b2"][0:NX, f * P:(f + 1) * P], CT[0:NX, n * 512:(n + 1) * 512],
                                      start=True, stop=False)
                    pe.wait_ge(S["ye_ready"], g + 1)
                    for f in range(KD):
                        mm = pe.matmul(bank(f), w26[:, e, f * P:(f + 1) * P], YE[:, g % 2, :],
                                       start=False, stop=(e == NX - 1))
                    mm.then_inc(S["ye_used"], 1)

                for g in range(2 * NX):
                    up(g)
                    if g > 0:
                        down(g - 1)
                down(2 * NX - 1)
                for i in range(NT):
                    pe.wait_ge(S["ft_copied"], 4)
                    if i >= 2:
                        pe.wait_ge(S["x_added"], 5 * NT + i - 1)
                    for f in range(KD):
                        mm = pe.transpose(psum[:, 6 + i % 2, f * P:(f + 1) * P], FT[:, f, i * P:(i + 1) * P], ident)
                    mm.then_inc(S["out_ps"], 1)

            for step, program in enumerate([mamba, cross1, swiglu, ttt, cross2, experts]):
                if LAST > step:
                    program()

        @block.scalar
        def _(act):
            def turn_x(k):
                for i in range(NT):
                    act.wait_ge(S["xt_ps"], NT * (k - 2) + i + 1)
                    act.activation(XT[:, :, i * P:(i + 1) * P], psum[:, 6 + i % 2, 0:D].rearrange("p (f t) -> p f t", f=KD),
                                   ACT.Copy).then_inc(S["xt_ready"], 1)

            def norm_std(k):
                act.wait_ge(S["ln_var"], NT * k)
                act.activation(std[:, 0:NT], mv[:, 0:NT, 1], ACT.Sqrt, bias=eps_ln).then_inc(S["ln_std"], 1)

            def mamba():
                for g in range(8, 16):
                    m, n = g // 2 - 4, g % 2
                    act.wait_ge(S["proj_ps"], g + 1)
                    act.activation(ZS[:, m, n * 512:(n + 1) * 512], bank(g % 8), ACT.Silu).then_inc(S["z_ready"], 1)
                for m in range(NBLK):
                    act.wait_ge(S["conv_done"], m + 1)
                    act.activation(U[:, m, :], U[:, m, :], ACT.Silu).then_inc(S["u_ready"], 1)
                act.wait_ge(S["dbl_ps"], 2)
                act.activation(DTR, bank(0, 2), ACT.Copy).then_inc(S["dtr_copied"], 1)
                act.activation(a_neg, a_log, ACT.Exp).then_inc(S["a_exp"], 1)
                for m in range(NBLK):
                    act.wait_ge(S["spz_ready"], m + 1)
                    act.activation(SPA[:, m, :], SPZ[:, m, :], ACT.Abs).then_inc(S["act_step"], 1)
                    act.wait_ge(S["act_step"], 2 * m + 1)
                    act.activation(SPA[:, m, :], SPA[:, m, :], ACT.Exp, scale=-1.0).then_inc(S["act_step"], 1)
                    act.wait_ge(S["act_step"], 2 * m + 2)
                    act.activation(SPA[:, m, :], SPA[:, m, :], ACT.Ln, bias=one).then_inc(S["spa_ready"], 1)
                act.wait_ge(S["dt_ready"], NBLK)
                act.wait_ge(S["a_ready"], 1)
                for it in range(NBLK * NS):
                    m, s = it // NS, it % NS
                    if it > 0:
                        act.wait_ge(S["h_ready"], it)
                    act.activation(bank(4, 2), DT[:, m, :], ACT.Exp, scale=a_neg[:, it:it + 1]).then_inc(S["da_ready"], 1)
                    act.wait_ge(S["c_ps"], it + 1)
                    if it >= 2:
                        act.wait_ge(S["hc_ready"], it - 1)
                    act.activation(CB[:, it % 2, :], bank(2, 2), ACT.Copy).then_inc(S["c_copied"], 1)
                norm_std(1)

            def cross1():
                for i in range(NT):
                    act.wait_ge(S["nbias_ready"], i + 1)
                    if i >= 2:
                        act.wait_ge(S["pt_ps"], 4 * (i - 1))
                    for j in range(4):
                        for mt in range(2):
                            c = 2 * j + mt
                            act.activation(PR[:, i % 2, j, mt, :], psum[:, j, mt * L:(mt + 1) * L], ACT.Exp,
                                           bias=nbias[:, 8 * (i % 2) + c:8 * (i % 2) + c + 1], scale=XSCALE,
                                           accum_out=psums[:, 8 * (i % 2) + c:8 * (i % 2) + c + 1]).then_inc(S["p_ready"], 1)
                    for j in (1, 3):
                        act.wait_ge(S["pt_ps"], 4 * i + j + 1)
                        act.activation(PT[:, 1, :, :].rearrange("p n m -> p (n m)"), bank(5), ACT.Copy)\
                           .then_inc(S["pt_odd"], 1)
                norm_std(2)

            def swiglu():
                for g in range(4):
                    act.wait_ge(S["had_ps"], g + 1)
                    act.activation(fw2[:, 2 * g:2 * g + 2, :].rearrange("p k d -> p (k d)"), bank(g), ACT.Copy,
                                   scale=float(FF) ** -0.5).then_inc(S["w2h_ready"], 1)
                turn_x(2)
                for g in range(2 * NFB):
                    act.wait_ge(S["up_ps"], 2 * g + 1)
                    if g >= 2:
                        act.wait_ge(S["hid_ready"], g - 1)
                    act.activation(SG[:, g % 2, :], bank(g % 2), ACT.Silu).then_inc(S["sg_ready"], 1)
                norm_std(3)

            def ttt():
                turn_x(3)
                for i in range(NT):
                    act.wait_ge(S["q4_ps"], i + 1)
                    act.activation(s_raw[:, TH * i:TH * (i + 1)], psum[:, i % 4, D:D + TH], ACT.Copy).then_inc(S["s4_copied"], 1)
                    act.activation(Q4[:, i, :], psum[:, i % 4, 0:D], ACT.Silu).then_inc(S["q4_copied"], 1)
                act.wait_ge(S["s4_raw"], 1)
                act.activation(s_gate, s_raw, ACT.Silu).then_inc(S["s4_ready"], 1)
                act.wait_ge(S["ss4_ready"], 1)
                act.activation(std, sum_sq, ACT.Sqrt).then_inc(S["ss4_std"], 1)
                for i in range(NT):
                    b, h = i // 2, i % 2
                    act.wait_ge(S["qt4_ps"], i + 1)
                    act.activation(QT4[:, h, b, :].rearrange("p (t h) -> p h t", h=TH),
                                   psum[:, 4 + i % 2, 0:D].rearrange("p (h t) -> p h t", h=TH), ACT.Copy)\
                       .then_inc(S["qt4_copied"], 1)
                for g in range(4):
                    act.wait_ge(S["f4_ps"], 2 * g + 1)
                    if g >= 2:
                        act.wait_ge(S["gh_ready"], g - 1)
                    act.activation(SG4[:, g % 2, :], bank(g % 2), ACT.Silu).then_inc(S["sg4_ready"], 1)
                for i in range(NT):
                    act.wait_ge(S["o4_ps"], i + 1)
                    act.activation(O4[:, i, :], psum[:, 4 + i % 2, 0:D], ACT.Copy).then_inc(S["o4_copied"], 1)
                act.wait_ge(S["o4_var"], TH * NT)
                act.activation(std, mv[:, :, 1], ACT.Sqrt, bias=eps_ttt).then_inc(S["o4_std"], 1)
                for i in range(NT):
                    act.wait_ge(S["ot4_ps"], i + 1)
                    act.activation(OT4[:, :, i * P:(i + 1) * P], psum[:, 6 + i % 2, 0:D].rearrange("p (h t) -> p h t", h=TH),
                                   ACT.Copy).then_inc(S["ot4_copied"], 1)
                norm_std(4)

            def cross2():
                turn_x(4)
                for b in range(B):
                    act.wait_ge(S["ang_ready"], 2 * (b + 1))
                    act.activation(SINES[:, 0, :, :], ANG[:, 0, :, :], ACT.Sin, scale=-1.0).then_inc(S["sines_ready"], 1)
                    act.activation(SINES[:, 1, :, :], ANG[:, 0, :, :], ACT.Sin).then_inc(S["sines_ready"], 1)
                    act.activation(SINES[:, 2, :, :], ANG[:, 2, :, :], ACT.Sin).then_inc(S["sines_ready"], 1)

                    def project(n):
                        g = 12 * b + n
                        act.wait_ge(S["kq_ps"], g + 1)
                        if g >= 2:
                            act.wait_ge(S["rope_sum"], g - 1)
                        act.activation(RAW5[:, n % 2, :], bank(6 + n % 2), ACT.Copy).then_inc(S["kq_copied"], 1)
                        act.wait_ge(S["kq_copied"], g + 1)
                        if g >= 1:
                            act.wait_ge(S["ss_ready"], g)
                        act.activation(SQ5, RAW5[:, n % 2, :], ACT.Square).then_inc(S["sq_ready"], 1)

                    def turn(n):
                        g = 12 * b + n
                        act.wait_ge(S["tr_ps"], g + 1)
                        got = bank(4 + n % 2).rearrange("p (h t) -> p h t", h=4)
                        if n < KT:
                            dst = KTR[:, :, n * P:(n + 1) * P]
                        else:
                            c, t = divmod(n - KT, 2)
                            dst = QTR[:, 4 * c:4 * c + 4, t * P:(t + 1) * P]
                        act.activation(dst, got, ACT.Copy).then_inc(S["tr_copied"], 1)

                    for n in range(KT + 1):
                        if n < KT:
                            project(n)
                            act.wait_ge(S["ss_ready"], 12 * b + n + 1)
                            act.activation(k_rs[:, KVH * n:KVH * (n + 1)], k_ss[:, KVH * n:KVH * (n + 1)], ACT.Sqrt,
                                           scale=1.0 / HD, bias=eps_rms).then_inc(S["rs_std"], 1)
                        if n >= 1:
                            turn(n - 1)
                    for t in range(KT):
                        act.wait_ge(S["v_ps"], KT * b + t + 1)
                        act.activation(V5[:, t, :], bank(t), ACT.Copy).then_inc(S["v_copied"], 1)
                    for n in range(KT, 13):
                        if n < 12:
                            project(n)
                        if n > KT:
                            turn(n - 1)
                    act.wait_ge(S["ss_ready"], 12 * (b + 1))
                    act.activation(q_rs, q_ss, ACT.Sqrt, scale=1.0 / HD, bias=eps_rms).then_inc(S["rs_std"], 1)

                    def probs(h):
                        for m in range(2):
                            g = 2 * (QH * b + h) + m
                            act.wait_ge(S["nb5_ready"], g + 1)
                            if h >= 2:
                                act.wait_ge(S["pt5_ps"], g - 3)
                            c = 2 * h + m
                            act.activation(PR5[:, h % 2, m, :], bank(2 * (h % 2) + m), ACT.Exp, scale=q_rs[:, c:c + 1],
                                           bias=nbias[:, g % 4:g % 4 + 1],
                                           accum_out=psums[:, g % 4:g % 4 + 1]).then_inc(S["p5_ready"], 1)

                    probs(0)
                    for h in range(QH):
                        for m in range(2):
                            g = 2 * (QH * b + h) + m
                            act.wait_ge(S["pt5_ps"], g + 1)
                            act.activation(PT5[:, :, m * P:(m + 1) * P], bank(4 + m).rearrange("p (k n) -> p k n", k=KT),
                                           ACT.Copy).then_inc(S["pt5_copied"], 1)
                        if h + 1 < QH:
                            probs(h + 1)
                norm_std(5)

            def experts():
                turn_x(5)
                act.wait_ge(S["aff_ps"], 1)
                act.activation(AFF.rearrange("p t e -> p (t e)"), psum[:, 0, 0:NT * NE], ACT.Exp, scale=-1.0)\
                   .then_inc(S["aff_exp"], 1)
                act.wait_ge(S["ct_ps"], 1)
                act.activation(CT[0:2 * NS, :], psum[0:2 * NS, 4:6, :].rearrange("p b n -> p (b n)"), ACT.Copy)\
                   .then_inc(S["ct_copied"], 1)
                for g in range(2 * NX):
                    e = g % NX
                    act.wait_ge(S["ge_ps"], 2 * g + 1)
                    if g >= 2:
                        act.wait_ge(S["ye_ready"], g - 1)
                    act.activation(GE[:, g % 2, :], bank(2 + g % 2), ACT.Gelu, bias=moe["gb"][:, e:e + 1])\
                       .then_inc(S["ge_ready"], 1)
                    if e == NX - 1:
                        n = g // NX
                        act.wait_ge(S["ye_used"], g + 1)
                        for f in range(KD):
                            act.activation(FT[:, f, n * 512:(n + 1) * 512], bank(f), ACT.Copy).then_inc(S["ft_copied"], 1)
                norm_std(6)

            act.wait_ge(consts_ready, 4)
            for step, program in enumerate([mamba, cross1, swiglu, ttt, cross2, experts]):
                if LAST > step:
                    program()

        @block.vector
        def _(dve):
            steps = [0]

            def step(instruction):
                steps[0] += 1
                instruction.then_inc(S["dve_step"], 1)

            def settle():
                dve.wait_ge(S["dve_step"], steps[0])

            def add_norm(k, source, twice=False):
                for i in range(NT):
                    dve.wait_ge(S["out_ps"], NT * (k - 1) + i + 1)
                    dve.scalar_tensor_tensor(out=X[:, i, :], in0=X[:, i, :], scalar=2.0 if twice else 1.0, in1=source(i),
                                             op0=ALU.mult, op1=ALU.add).then_inc(S["x_added"], 1)
                    dve.wait_ge(S["x_added"], NT * (k - 1) + i + 1)
                    step(dve.bn_stats(stats[:, i, :], X[:, i, :]))
                    settle()
                    dve.bn_aggr(mv[:, i, :], stats[:, i, :]).then_inc(S["ln_var"], 1)

            def apply_norm(k):
                dve.wait_ge(S["ln_std"], k)
                step(dve.reciprocal(rstd[:, 0:NT], std[:, 0:NT]))
                settle()
                for i in range(NT):
                    dve.tensor_scalar(X[:, i, :], X[:, i, :], mv[:, i, 0:1], rstd[:, i:i + 1], ALU.subtract, ALU.mult)\
                       .then_inc(S["x_ready"], 1)

            def three_parts(source, out3, rest, mid, rows, ready):
                step(dve.tensor_copy(out3[0:rows, :], source))
                settle()
                step(dve.tensor_tensor(rest[0:rows, :], source, out3[0:rows, :], ALU.subtract))
                settle()
                step(dve.tensor_copy(mid[0:rows, :], rest[0:rows, :]))
                settle()
                dve.tensor_tensor(out3[64:64 + rows, :], rest[0:rows, :], mid[0:rows, :], ALU.subtract).then_inc(ready, 1)
                dve.tensor_copy(out3[32:32 + rows, :], mid[0:rows, :]).then_inc(ready, 1)

            def mamba():
                step(dve.memset(XS[:, :, :, 0:DCONV - 1], 0.0))
                for g in range(8):
                    m, n = g // 2, g % 2
                    dve.wait_ge(S["proj_ps"], g + 1)
                    dve.tensor_copy(XS[:, m, 2 * n:2 * n + 2, DCONV - 1:], bank(g).rearrange("p (b t) -> p b t", b=2))\
                       .then_inc(S["xs_copied"], 1)
                dve.wait_ge(ld["mamba"], 16)
                step(dve.tensor_copy(sel3[0:N3, :], mb["sel3"][0:N3, :]))
                settle()
                for m in range(NBLK):
                    dve.wait_ge(S["xs_copied"], 2 * m + 2)
                    um = U[:, m, :].rearrange("p (b t) -> p b t", b=B)
                    step(dve.tensor_scalar(um, XS[:, m, :, 0:L], conv_w[:, m, 0:1], mb["conv_b"][:, m:m + 1], ALU.mult, ALU.add))
                    for k in range(1, DCONV):
                        settle()
                        tap = dve.scalar_tensor_tensor(out=um, in0=XS[:, m, :, k:k + L], scalar=conv_w[:, m, k:k + 1], in1=um,
                                                       op0=ALU.mult, op1=ALU.add)
                        if k < DCONV - 1:
                            step(tap)
                        else:
                            tap.then_inc(S["conv_done"], 1)
                dve.wait_ge(S["dbl_ps"], 4)
                three_parts(psum[0:2 * NS, 2:4, :].rearrange("p b n -> p (b n)"), bc3, bc_rest, bc_mid, 2 * NS,
                            S["bc_ready"])
                dve.wait_ge(S["a_exp"], 1)
                dve.tensor_scalar(a_neg, a_neg, -1.0, None, ALU.mult).then_inc(S["a_ready"], 1)

                def softplus_in(m):
                    dve.wait_ge(S["dt_ps"], m + 1)
                    dve.tensor_scalar(SPZ[:, m, :], bank((4 + 2 * m) % 8, 2), mb["b_dt"][:, m:m + 1], None, ALU.add)\
                       .then_inc(S["spz_ready"], 1)

                def softplus_out(m):
                    dve.wait_ge(S["spa_ready"], m + 1)
                    step(dve.scalar_tensor_tensor(out=DT[:, m, :], in0=SPZ[:, m, :], scalar=0.0, in1=SPA[:, m, :],
                                                  op0=ALU.max, op1=ALU.add))
                    settle()
                    step(dve.tensor_tensor(DTU[:, m, :], DT[:, m, :], U[:, m, :], ALU.mult))
                    settle()
                    dve.memset(DT[:, m, :].rearrange("p (b t) -> p b t", b=B)[:, :, 0:1], STEP0_DT).then_inc(S["dt_ready"], 1)

                softplus_in(0)
                for m in range(NBLK):
                    if m + 1 < NBLK:
                        softplus_in(m + 1)
                    softplus_out(m)
                dve.wait_ge(S["dt_ready"], NBLK)

                def input_term(it):
                    m = it // NS
                    dve.wait_ge(S["b_ps"], it + 1)
                    dve.tensor_tensor(DBU[:, it % 2, :], bank(0, 2), DTU[:, m, :], ALU.mult).then_inc(S["dbu_ready"], 1)

                def gate_y(m):
                    dve.wait_ge(S["hc_summed"], NS * (m + 1))
                    dve.scalar_tensor_tensor(out=YS[:, m, :], in0=U[:, m, :], scalar=mb["d_skip"][:, m:m + 1], in1=bank(6, 2),
                                             op0=ALU.mult, op1=ALU.add).then_inc(S["y_used"], 1)
                    dve.wait_ge(S["y_used"], m + 1)
                    dve.tensor_tensor(YS[:, m, :], YS[:, m, :], ZS[:, m, :], ALU.mult).then_inc(S["y_ready"], 1)

                n_it = NBLK * NS
                input_term(0)
                for it in range(n_it):
                    dve.wait_ge(S["da_ready"], it + 1)
                    dve.wait_ge(S["dbu_ready"], it + 1)
                    if it >= 2:
                        dve.wait_ge(S["hc_ready"], it - 1)
                    dve.tensor_tensor_scan(H[:, it % 2, :], bank(4, 2), DBU[:, it % 2, :], 0.0, ALU.mult, ALU.add)\
                       .then_inc(S["h_ready"], 1)
                    if it + 1 < n_it:
                        input_term(it + 1)
                    if it >= NS and it % NS == 0:
                        gate_y(it // NS - 1)
                gate_y(NBLK - 1)
                dve.wait_ge(ld["x"], 16)
                add_norm(1, lambda i: psum[:, i % 4, 0:D])
                apply_norm(1)

            def cross1():
                def bias(i):
                    dve.wait_ge(S["sc_ps"], i + 1)
                    c = slice(8 * (i % 2), 8 * (i % 2) + 8)
                    step(dve.tensor_reduce(nmax[:, c], psum[:, 0:4, :].rearrange("p b (m n) -> p (b m) n", m=2), AX.X,
                                           ALU.max, negate=True))
                    settle()
                    dve.tensor_scalar(nbias[:, c], nmax[:, c], XSCALE, None, ALU.mult).then_inc(S["nbias_ready"], 1)

                def add(i):
                    dve.wait_ge(S["out_ps"], NT + i + 1)
                    dve.tensor_tensor(X[:, i, :], X[:, i, :], psum[:, 7, 0:D], ALU.add).then_inc(S["x_added"], 1)
                    dve.wait_ge(S["x_added"], NT + i + 1)
                    step(dve.bn_stats(stats[:, i, :], X[:, i, :]))
                    settle()
                    dve.bn_aggr(mv[:, i, :], stats[:, i, :]).then_inc(S["ln_var"], 1)

                for i in range(NT + 1):
                    if i < NT:
                        bias(i)
                    if i >= 2:
                        add(i - 2)
                    if i == 0:
                        continue
                    t = i - 1
                    for j in (0, 2):
                        dve.wait_ge(S["pt_ps"], 4 * t + j + 1)
                        dve.tensor_copy(PT[:, 0, :, :].rearrange("p n m -> p (n m)"), bank(4)).then_inc(S["pt_even"], 1)
                    c = slice(8 * (t % 2), 8 * (t % 2) + 8)
                    dve.wait_ge(S["p_ready"], 8 * (t + 1))
                    step(dve.reciprocal(rinv[:, c], psums[:, c]))
                    settle()
                    dve.wait_ge(S["o_ps"], t + 1)
                    if t > 0:
                        dve.wait_ge(S["out_ps"], NT + t)
                    dve.tensor_tensor(OT[:, 0, :, :].rearrange("p m (j c) -> p m j c", j=4),
                                      psum[:, 6, 0:D].rearrange("p (m j c) -> p m j c", m=2, j=4),
                                      rinv[:, c].rearrange("p (j m) -> p m j", m=2).unsqueeze(3).broadcast_to([P, 2, 4, XR]),
                                      ALU.mult).then_inc(S["ot_ready"], 1)
                add(NT - 1)
                apply_norm(2)

            def swiglu():
                for g in range(2 * NFB):
                    n, h = g // NFB, g % NFB
                    dve.wait_ge(S["up_ps"], 2 * g + 2)
                    dve.wait_ge(S["sg_ready"], g + 1)
                    dve.tensor_tensor(HID[:, h, n * 512:(n + 1) * 512], SG[:, g % 2, :], bank(2 + g % 2), ALU.mult)\
                       .then_inc(S["hid_ready"], 1)
                add_norm(3, lambda i: psum[:, 4 + i % 2, 0:D])
                apply_norm(3)

            def ttt():
                dve.wait_ge(S["s4_copied"], NT)
                dve.wait_ge(ld["ttt"], 16)
                s3 = s_raw.rearrange("p (t h) -> p t h", h=TH)
                dve.tensor_tensor(s3, s3, ttt_w["b_s"].unsqueeze(1).broadcast_to([P, NT, TH]), ALU.add)\
                   .then_inc(S["s4_raw"], 1)
                dve.wait_ge(S["q4_copied"], NT)
                flat = Q4.rearrange("p t d -> p (t d)")
                sq = SQ4.rearrange("p t d -> p (t d)")
                heads = flat.rearrange("p (g d) -> p g d", d=THD)
                step(dve.tensor_tensor(sq, flat, flat, ALU.mult))
                settle()
                dve.tensor_reduce(sum_sq, sq.rearrange("p (g d) -> p g d", d=THD), AX.X, ALU.add).then_inc(S["ss4_ready"], 1)
                dve.wait_ge(S["ss4_std"], 1)
                step(dve.tensor_scalar(std, std, 1e-5, None, ALU.add))
                settle()
                step(dve.reciprocal(rstd, std))
                settle()
                dve.tensor_tensor(heads, heads, rstd.unsqueeze(2).broadcast_to([P, TH * NT, THD]), ALU.mult)\
                   .then_inc(S["q4_ready"], 1)
                for g in range(4):
                    h, n = g // 2, g % 2
                    dve.wait_ge(S["f4_ps"], 2 * g + 2)
                    dve.wait_ge(S["sg4_ready"], g + 1)
                    dve.tensor_tensor(GH[:, h, n * 512:(n + 1) * 512], SG4[:, g % 2, :], bank(2 + g % 2), ALU.mult)\
                       .then_inc(S["gh_ready"], 1)
                for i in range(NT):
                    dve.wait_ge(S["o4_copied"], i + 1)
                    for h in range(TH):
                        step(dve.bn_stats(stats[:, TH * i + h, :], O4[:, i, h * THD:(h + 1) * THD]))
                settle()
                for j in range(TH * NT):
                    dve.bn_aggr(mv[:, j, :], stats[:, j, :]).then_inc(S["o4_var"], 1)
                dve.wait_ge(S["o4_std"], 1)
                step(dve.reciprocal(rstd, std))
                settle()
                dve.wait_ge(S["s4_ready"], 1)
                for i in range(NT):
                    o = O4[:, i, :].rearrange("p (h d) -> p h d", h=TH)
                    for h in range(TH):
                        j = TH * i + h
                        step(dve.tensor_scalar(o[:, h, :], o[:, h, :], mv[:, j, 0:1], rstd[:, j:j + 1], ALU.subtract, ALU.mult))
                    settle()
                    step(dve.tensor_tensor(o, o, ttt_w["ln_g"].unsqueeze(1).broadcast_to([P, TH, THD]), ALU.mult))
                    settle()
                    step(dve.tensor_tensor(o, o, ttt_w["ln_b"].unsqueeze(1).broadcast_to([P, TH, THD]), ALU.add))
                    settle()
                    dve.tensor_tensor(o, o, s_gate[:, TH * i:TH * i + TH].unsqueeze(2).broadcast_to([P, TH, THD]), ALU.mult)\
                       .then_inc(S["o4_normed"], 1)
                add_norm(4, lambda i: psum[:, i % 4, 0:D])
                apply_norm(4)

            def cross2():
                dve.wait_ge(ld["pos"], 16)
                step(dve.tensor_copy(pos_f, pos_i[:, :]))
                dve.wait_ge(ld["attn"], 16)
                settle()
                for b in range(B):
                    x_, k_, c_ = ANG[:, 0, :, :], ANG[:, 1, :, :], ANG[:, 2, :, :]
                    if b > 0:
                        dve.wait_ge(S["pt5_ps"], 2 * QH * b)
                    for t in range(KT):
                        step(dve.tensor_scalar(x_[:, t, :], attn["inv_freq"], pos_f[:, KT * b + t:KT * b + t + 1], None, ALU.mult))
                    settle()
                    step(dve.tensor_scalar(k_, x_, float(1 / (2 * np.pi)), ROUND, ALU.mult, ALU.add))
                    settle()
                    step(dve.tensor_scalar(k_, k_, ROUND, None, ALU.subtract))
                    settle()
                    step(dve.scalar_tensor_tensor(out=x_, in0=k_, scalar=-TURN_HI, in1=x_, op0=ALU.mult, op1=ALU.add))
                    settle()
                    step(dve.scalar_tensor_tensor(out=x_, in0=k_, scalar=-TURN_LO, in1=x_, op0=ALU.mult, op1=ALU.add))
                    settle()
                    step(dve.tensor_scalar(c_, x_, float(np.pi / 2), None, ALU.add))
                    settle()
                    step(dve.tensor_scalar(k_, c_, float(np.pi), -float(2 * np.pi), ALU.is_gt, ALU.mult))
                    settle()
                    step(dve.tensor_tensor(c_, c_, k_, ALU.add))
                    settle()
                    dve.tensor_scalar(c_, c_, PI_MAX, -PI_MAX, ALU.min, ALU.max).then_inc(S["ang_ready"], 1)
                    dve.tensor_scalar(x_, x_, PI_MAX, -PI_MAX, ALU.min, ALU.max).then_inc(S["ang_ready"], 1)
                    dve.wait_ge(S["sines_ready"], 3 * (b + 1))

                    def tables(dst_cos, dst_sin, w, w_swap, t0, n):
                        halves = "p t (i f) -> p t i f"
                        step(dve.tensor_tensor(dst_cos.rearrange(halves, i=2),
                                               w.rearrange("p (i f) -> p i f", i=2).unsqueeze(1).broadcast_to([P, n, 2, ROPE]),
                                               SINES[:, 2, t0:t0 + n, :].unsqueeze(2).broadcast_to([P, n, 2, ROPE]), ALU.mult))
                        step(dve.tensor_tensor(dst_sin.rearrange(halves, i=2),
                                               w_swap.rearrange("p (i f) -> p i f", i=2).unsqueeze(1).broadcast_to([P, n, 2, ROPE]),
                                               SINES[:, 0:2, t0:t0 + n, :].rearrange("p i t f -> p t i f"), ALU.mult))

                    tables(KCOS, KSIN, attn["k_w"], attn["k_w_swap"], 0, KT)
                    tables(QCOS, QSIN, attn["q_w"], attn["q_w_swap"], CTXT_TILES, 2)
                    settle()

                    def rope(n):
                        g = 12 * b + n
                        if n < KT:
                            cos, sin, ss = KCOS[:, n, :], KSIN[:, n, :], k_ss[:, KVH * n:KVH * (n + 1)]
                        else:
                            c, t = divmod(n - KT, 2)
                            cos, sin = QCOS[:, t, :], QSIN[:, t, :]
                            ss = q_ss.rearrange("p (h m) -> p h m", m=2)[:, 4 * c:4 * c + 4, t]
                        raw = RAW5[:, n % 2, :].rearrange("p (h i f) -> p h i f", h=4, i=2)
                        dve.wait_ge(S["kq_copied"], g + 1)
                        if g >= 2:
                            dve.wait_ge(S["tr_ps"], g - 1)
                        dve.tensor_tensor(RT1[:, n % 2, :].rearrange("p (h d) -> p h d", h=4),
                                          RAW5[:, n % 2, :].rearrange("p (h d) -> p h d", h=4),
                                          cos.unsqueeze(1).broadcast_to([P, 4, HD]), ALU.mult).then_inc(S["t1_ready"], 1)
                        if g >= 1:
                            dve.wait_ge(S["rope_sum"], g)
                        for i in range(2):
                            dve.tensor_tensor(RT2.rearrange("p (h i f) -> p h i f", h=4, i=2)[:, :, i, :], raw[:, :, 1 - i, :],
                                              sin[:, i * ROPE:(i + 1) * ROPE].unsqueeze(1).broadcast_to([P, 4, ROPE]),
                                              ALU.mult).then_inc(S["t1_ready"], 1)
                        dve.wait_ge(S["sq_ready"], g + 1)
                        dve.tensor_reduce(ss, SQ5.rearrange("p (h d) -> p h d", h=4), AX.X, ALU.add).then_inc(S["ss_ready"], 1)

                    for n in range(12):
                        rope(n)
                        if n < KT:
                            dve.wait_ge(S["rs_std"], (KT + 1) * b + n + 1)
                            kr = k_rs[:, KVH * n:KVH * (n + 1)]
                            dve.reciprocal(kr, kr).then_inc(S["krs_ready"], 1)
                    dve.wait_ge(S["rs_std"], (KT + 1) * (b + 1))
                    step(dve.reciprocal(q_rs, q_rs))
                    settle()
                    step(dve.tensor_scalar(q_rs, q_rs, ASCALE, None, ALU.mult))
                    settle()

                    def bias(h):
                        for m in range(2):
                            g = 2 * (QH * b + h) + m
                            dve.wait_ge(S["s5_ps"], g + 1)
                            step(dve.tensor_reduce(nmax[:, g % 4:g % 4 + 1], bank(2 * (h % 2) + m), AX.X, ALU.max, negate=True))
                            settle()
                            dve.tensor_tensor(nbias[:, g % 4:g % 4 + 1], nmax[:, g % 4:g % 4 + 1],
                                              q_rs[:, 2 * h + m:2 * h + m + 1], ALU.mult).then_inc(S["nb5_ready"], 1)

                    def inverse(h):
                        for m in range(2):
                            g = 2 * (QH * b + h) + m
                            dve.wait_ge(S["p5_ready"], g + 1)
                            step(dve.reciprocal(rinv[:, g % 4:g % 4 + 1], psums[:, g % 4:g % 4 + 1]))
                            settle()
                            dve.tensor_scalar(PR5[:, h % 2, m, :], PR5[:, h % 2, m, :], rinv[:, g % 4:g % 4 + 1], None, ALU.mult)\
                               .then_inc(S["p5_normed"], 1)

                    bias(0)
                    for h in range(QH):
                        if h + 1 < QH:
                            bias(h + 1)
                        inverse(h)
                        if h >= 1:
                            dve.wait_ge(S["at_ps"], QH * b + h)
                            dve.tensor_copy(AT[:, h - 1, :], psum[:, 6, 0:L]).then_inc(S["at_copied"], 1)
                    dve.wait_ge(S["at_ps"], QH * (b + 1))
                    dve.tensor_copy(AT[:, QH - 1, :], psum[:, 6, 0:L]).then_inc(S["at_copied"], 1)
                    for m in range(2):
                        i = 2 * b + m
                        dve.wait_ge(S["out_ps"], 4 * NT + i + 1)
                        dve.tensor_tensor(X[:, i, :], X[:, i, :], psum[:, 7, 0:D], ALU.add).then_inc(S["x_added"], 1)
                        dve.wait_ge(S["x_added"], 4 * NT + i + 1)
                        step(dve.bn_stats(stats[:, i, :], X[:, i, :]))
                        settle()
                        dve.bn_aggr(mv[:, i, :], stats[:, i, :]).then_inc(S["ln_var"], 1)
                apply_norm(5)

            def experts():
                dve.wait_ge(S["aff_exp"], 1)
                step(dve.tensor_scalar(AFF, AFF, 1.0, None, ALU.add))
                step(dve.memset(CMB, 0.0))
                settle()
                step(dve.reciprocal(AFF, AFF))
                settle()
                for i in range(NT):
                    step(dve.max(TOP[:, i, :], AFF[:, i, :]))
                settle()
                for i in range(NT):
                    step(dve.max_index(top_i[:, i, :], TOP[:, i, :], AFF[:, i, :]))
                step(dve.tensor_tensor(PS, TOP[:, :, 0], TOP[:, :, 1], ALU.add))
                settle()
                step(dve.tensor_copy(TOPI, top_i[:, :, :]))
                step(dve.reciprocal(PS, PS))
                settle()
                step(dve.tensor_tensor(PW, TOP[:, :, 0:2], PS.unsqueeze(2).broadcast_to([P, NT, 2]), ALU.mult))
                settle()
                steps_e = moe["iota"].unsqueeze(1).broadcast_to([P, NT, NE])
                for c in range(2):
                    step(dve.tensor_tensor(PICK, steps_e, TOPI[:, :, c:c + 1].broadcast_to([P, NT, NE]), ALU.is_equal))
                    settle()
                    step(dve.tensor_tensor(PICK, PICK, PW[:, :, c:c + 1].broadcast_to([P, NT, NE]), ALU.mult))
                    settle()
                    step(dve.tensor_tensor(CMB[:, :, 0:NE], CMB[:, :, 0:NE], PICK, ALU.add))
                    settle()
                dve.memset(CMB[:, :, NE:NX], 1.0).then_inc(S["cmb_ready"], 1)
                dve.wait_ge(S["ct_copied"], 1)
                three_parts(CT[0:2 * NS, :], ct3, ct_rest, ct_mid, 2 * NS, S["ct_ready"])
                for g in range(2 * NX):
                    n, e = g // NX, g % NX
                    dve.wait_ge(S["ge_ps"], 2 * g + 2)
                    dve.wait_ge(S["ge_ready"], g + 1)
                    if g >= 2:
                        dve.wait_ge(S["ye_used"], g - 1)
                    y = dve.scalar_tensor_tensor(out=YE[:, g % 2, :], in0=bank(4 + g % 2), scalar=moe["b1"][:, e:e + 1],
                                                 in1=GE[:, g % 2, :], op0=ALU.add, op1=ALU.mult)
                    if e < NE:
                        step(y)
                        settle()
                        dve.wait_ge(S["cb_ps"], n * NE + e + 1)
                        dve.tensor_tensor(YE[:, g % 2, :], YE[:, g % 2, :], bank(6 + g % 2), ALU.mult).then_inc(S["ye_ready"], 1)
                    else:
                        y.then_inc(S["ye_ready"], 1)
                add_norm(6, lambda i: psum[:, 6 + i % 2, 0:D], twice=True)
                apply_norm(6)

            dve.memset(eps_ln, LN_EPS).then_inc(consts_ready, 1)
            dve.memset(eps_ttt, TTT_EPS).then_inc(consts_ready, 1)
            dve.memset(eps_rms, RMS_EPS).then_inc(consts_ready, 1)
            dve.memset(one, 1.0).then_inc(consts_ready, 1)
            for k, program in enumerate([mamba, cross1, swiglu, ttt, cross2, experts]):
                if LAST > k:
                    program()

        @block.gpsimd
        def _(pool):
            def mamba():
                for it in range(NBLK * NS):
                    pool.wait_ge(S["h_ready"], it + 1)
                    pool.wait_ge(S["c_copied"], it + 1)
                    if it >= 2:
                        pool.wait_ge(S["hc_summed"], it - 1)
                    pool.tensor_tensor(HC[:, it % 2, :], H[:, it % 2, :], CB[:, it % 2, :], ALU.mult)\
                        .then_inc(S["hc_ready"], 1)

            def swiglu():
                pool.wait_ge(ld["ffn"], 16)
                for n, (src, dst) in enumerate(((fw2, fw2b), (fw2b, fw2), (fw2, fw2b))):
                    h = 1 << n
                    a = src.rearrange("p (g i h) d -> p g i (h d)", i=2, h=h)
                    o = dst.rearrange("p (g i h) d -> p g i (h d)", i=2, h=h)
                    if n > 0:
                        pool.wait_ge(S["bf_ready"], 2 * n)
                    pool.tensor_tensor(o[:, :, 0, :], a[:, :, 0, :], a[:, :, 1, :], ALU.add).then_inc(S["bf_ready"], 1)
                    pool.tensor_tensor(o[:, :, 1, :], a[:, :, 0, :], a[:, :, 1, :], ALU.subtract).then_inc(S["bf_ready"], 1)

            def cross2():
                for b in range(B):
                    for n in range(12):
                        g = 12 * b + n
                        pool.wait_ge(S["t1_ready"], 3 * (g + 1))
                        pool.tensor_tensor(RT1[:, n % 2, :], RT1[:, n % 2, :], RT2, ALU.add).then_inc(S["rope_sum"], 1)
                        if n < KT:
                            pool.wait_ge(S["krs_ready"], KT * b + n + 1)
                            pool.wait_ge(S["rope_sum"], g + 1)
                            k3 = RT1[:, n % 2, :].rearrange("p (h d) -> p h d", h=KVH)
                            pool.tensor_tensor(k3, k3, k_rs[:, KVH * n:KVH * (n + 1)].unsqueeze(2).broadcast_to([P, KVH, HD]),
                                               ALU.mult).then_inc(S["k_scaled"], 1)

            if LAST >= 1:
                mamba()
            if LAST >= 3:
                swiglu()
            if LAST >= 5:
                cross2()


def _columns(w):
    k, n = w.shape
    return w.reshape(k // P, P, n).transpose(1, 0, 2)


def _rows(v):
    return np.broadcast_to(v.reshape(1, -1), (P, v.size))


def _hadamard(n):
    h = np.ones((1, 1), np.float32)
    while h.shape[0] < n:
        h = np.concatenate([np.concatenate([h, h], 1), np.concatenate([h, -h], 1)], 0)
    return h


def _few(w):
    return np.concatenate([w, np.zeros((P - w.shape[0], w.shape[1]), w.dtype)], 0)


def kernel(**inputs):
    import concourse.bacc as _bacc
    from concourse.bass_utils import run_bass_kernel_spmd as _run

    a = {k: np.asarray(v) for k, v in inputs.items()}
    x2 = a["x"].reshape(T, D)
    ctx2 = a["ctx_2048"].reshape(T, D)
    qkv = a["L1_attn_W_qkv"].reshape(D, TH, 3, THD)
    experts = {k: np.concatenate([a["L1_ffn_r" + k], a["L1_ffn_s" + k]], 0) for k in ("g", "gb", "w1", "b1", "w2", "b2")}
    swap = lambda v: np.concatenate([v[ROPE:], v[:ROPE]])
    eye = np.eye(P, dtype=np.float32)
    parts = {
        "xT": _columns(x2.T), "w_inT": _columns(a["L0_attn_W_in"].T),
        "w_xT": _columns(a["L0_attn_W_x"].T), "w_dtT": a["L0_attn_W_dt"].T, "w_outT": _columns(a["L0_attn_W_out"].T),
        "conv_w": _columns(a["L0_attn_conv_w"]), "conv_b": _columns(a["L0_attn_conv_b"][:, None]),
        "b_dt": _columns(a["L0_attn_b_dt"][:, None]), "a_log": _columns(a["L0_attn_A_log"]),
        "d_skip": _columns(a["L0_attn_D"][:, None]), "ident": eye,
        "sel3": _few(np.tile(eye[:2 * NS, :2 * NS], (3, 1))),
        "x": _columns(x2), "ctx": _columns(ctx2), "ctxT": _columns(ctx2.T),
        "w_qs": _columns(np.concatenate([qkv[:, :, 0].reshape(D, TH * THD), a["L1_attn_W_s"]], 1)),
        "w0T": a["L1_attn_w0"].transpose(2, 0, 1), "w2T": a["L1_attn_w2"].transpose(2, 0, 1),
        "w1T": a["L1_attn_w1"].transpose(2, 0, 1), "w_oT": _columns(a["L1_attn_W_o"]),
        "ln_g": _rows(a["L1_attn_ln_g"]), "ln_b": _rows(a["L1_attn_ln_b"]), "b_s": _rows(a["L1_attn_b_s"]),
        "ffn1T": _columns(a["L0_ffn_W1"].T), "ffn3T": _columns(a["L0_ffn_W3"].T),
        "ffn2T": _columns(a["L0_ffn_W2"].T), "hadamard": _hadamard(P),
        "wqT": _columns(a["L1_xattn_Wq"].T), "wkT": _columns(a["L1_xattn_Wk"].T),
        "wvT": _columns(a["L1_xattn_Wv"].T), "woT": _columns(a["L1_xattn_Wo"].T),
        "q_w": _rows(a["L1_xattn_q_norm_w"]), "q_w_swap": _rows(swap(a["L1_xattn_q_norm_w"])),
        "k_w": _rows(a["L1_xattn_k_norm_w"]), "k_w_swap": _rows(swap(a["L1_xattn_k_norm_w"])),
        "inv_freq": _rows((1.0 / np.float32(10000.0) ** (np.arange(0, HD, 2, dtype=np.float32) / HD)).astype(np.float32)),
        "wa": _columns(a["L1_ffn_wa"]),
        "wg": experts["g"].reshape(NX, KD, P, EF).transpose(2, 0, 1, 3),
        "w1": experts["w1"].reshape(NX, KD, P, EF).transpose(2, 0, 1, 3),
        "w2": experts["w2"].transpose(1, 0, 2), "gb": experts["gb"].T, "b1": experts["b1"].T,
        "b2": _few(experts["b2"]), "iota": _rows(np.arange(NE, dtype=np.float32)),
    }
    arrays = {}
    for name, inside in PACKS.items():
        arrays["in_" + name] = np.ascontiguousarray(
            np.concatenate([parts[p].reshape(P, w) for p, w in inside], 1))
    pos = np.concatenate([a["pos_BxS2"].reshape(B, CTXT_TILES, P), a["itok_BxS_4096_4607"].reshape(B, CTXT_TILES, P)], 1)
    arrays["in_pos"] = np.ascontiguousarray(pos.reshape(B * KT, P).T.astype(np.int32))

    nc = _bacc.Bacc("TRN2", target_bir_lowering=False, num_devices=1)
    aps = {k[3:]: nc.dram_tensor(k, v.shape, mybir.dt.from_np(v.dtype), kind="ExternalInput").ap()
           for k, v in arrays.items()}
    out = nc.dram_tensor("out_x", (T, D), F32, kind="ExternalOutput").ap()
    decoder(nc, aps, out)
    r = _run(nc, [arrays], core_ids=[0])
    return r.results[0]["out_x"].reshape(B, L, D)
```

```python
from contextlib import ExitStack

import numpy as np

import concourse.bass as bass
from concourse import mybir

F32 = mybir.dt.float32
BF16 = mybir.dt.bfloat16
I32 = mybir.dt.int32
U32 = mybir.dt.uint32
ALU = mybir.AluOpType
ACT = mybir.ActivationFunctionType
AX = mybir.AxisListType

P = 128
B, L, D = 4, 256, 256
T = B * L
NT = T // P
KD = D // P
LN_EPS = 1e-5

DI, NS, DCONV, RANK = 512, 16, 4, 128
NBLK = DI // P
PAD = L + DCONV - 1
STEP0_DT = 1e28

XH = 8
XR = L // XH
XSCALE = float(1.0 / np.sqrt(np.float32(XR)))

FF = 1024
NFB = FF // P

TH, THD = 2, 128
TTT_EPS = 1e-6
L2_EPS = 1e-5
TINY = 1e-30

QH, KVH, HD = 16, 4, 128
CTXT_TILES = L // P
KT = 2 * CTXT_TILES
ROPE = HD // 2
ASCALE = float(np.float32(1.0 / np.sqrt(HD).astype(np.float32)))
RMS_EPS = 1e-6
EARLY = KT + 3

NE, NSH, EF = 16, 2, 128
NX = NE + NSH



class Region:

    def __init__(self, start):
        self.at = start

    def take(self, words):
        start, self.at = self.at, self.at + words
        return start, words


PACKS = {
    "in": [("xT", KD * T), ("w_inT", KD * 2 * DI)],
    "mamba": [("w_xT", NBLK * (RANK + 2 * NS)), ("w_dtT", DI), ("w_outT", NBLK * D), ("conv_w", NBLK * DCONV),
              ("conv_b", NBLK), ("b_dt", NBLK), ("a_log", NBLK * NS), ("d_skip", NBLK),
              ("sel3", 2 * NS)],
    "ident": [("ident", P)],
    "x": [("x", NT * D)],
    "ctx": [("ctx", NT * D), ("ctxT", KD * T)],
    "ttt": [("w_qs", KD * (TH * THD + TH)), ("w0T", TH * P), ("w2T", TH * P), ("w1T", TH * P), ("w_oT", TH * D),
            ("ln_g", P), ("ln_b", P), ("b_s", TH)],
    "ffn": [("ffn1T", KD * FF), ("ffn3T", KD * FF), ("ffn2T", NFB * D), ("hadamard", P)],
    "attn": [("wqT", KD * QH * HD), ("wkT", KD * KVH * HD), ("wvT", KD * KVH * HD), ("woT", QH * D),
             ("q_w", HD), ("q_w_swap", HD), ("k_w", HD), ("k_w_swap", HD), ("inv_freq", ROPE)],
    "moe": [("wa", KD * NE), ("wg", NX * KD * EF), ("w1", NX * KD * EF), ("w2", NX * D), ("gb", NX), ("b1", NX),
            ("b2", D), ("iota", NE)],
}


def pack_words(name):
    return sum(w for _, w in PACKS[name])

ROUND = float(1.5 * 2 ** 23)
TURN_HI = 6.28125
TURN_LO = float(2 * np.pi - TURN_HI)
PI_MAX = 3.1415925

ROOT_GUESS = float(0x5f3759df)

DT_BANKS = (4, 6, 0, 4)

SEMAPHORES = """
    x_added x_ready stored xt_ready xt_ps xs_copied proj_ps u_ready z_ready dbl_ps dt_ps dtr_copied spz_ready
    hc_ready y_used hc_summed bc_ready dbu_ready b_ps c_copied c_ps y_ready out_ps p_ready sc_ps p_normed
    pt_copied pt_ps bf_ready had_ps w2h_ready hid_ready up_ps q4_copied q4_ps q4_ready qt4_copied qt4_ps gh_ready
    f4_ps o4_copied o4_ps o4_normed ot4_copied ot4_ps tr_copied kq_copied at_copied kq_ps pt5_copied rope_sum
    k_scaled tr_ps v_ps p5_ready v_copied s5_ps p5_normed pt5_ps at_ps aff_ps cmb_ready ct_ps ct_ready ye_ready
    ge_ps cb_ps ft_copied ye_used conv_done a_exp spe_used act_step spl_ready a_ready dt_ready h_ready da_ready
    nbias_ready sg_ready s4_copied s4_raw s4_ready sg4_ready ang_ready sines_ready ss_ready sq_ready nb5_ready
    aff_exp ct_copied ge_ready dve_step ln_var ln_rstd ss4_ready norm4_ready o4_var o4_rstd krs_ready t1_ready
    qrs_ready pool_step
"""

LAST = 6


def decoder(nc: bass.Bass, dram, out: bass.AP):
    with ExitStack() as ctx:
        def sem(name):
            return ctx.enter_context(nc.semaphore(name))

        kept = Region(0)
        X_ = kept.take(NT * D)
        XT_ = kept.take(KD * T)
        CTX_ = kept.take(NT * D)
        CTXT_ = kept.take(KD * T)
        IDENT_ = kept.take(P)
        SMALL_ = kept.take(512)
        TTTW_ = kept.take(pack_words("ttt"))
        wa_start = kept.at
        wb_start = wa_start + max(pack_words("moe"), pack_words("ffn") + NFB * D)
        c_start = wb_start + pack_words("attn")
        total = c_start + 17248

        arena = ctx.enter_context(nc.sbuf_tensor("arena", [P, total], F32))
        psum = ctx.enter_context(nc.psum_tensor("psum", [P, 8, 512], F32))
        pos_i = ctx.enter_context(nc.sbuf_tensor("pos_i", [P, B * KT], I32))
        top_i = ctx.enter_context(nc.sbuf_tensor("top_i", [P, NT, 8], U32))

        def view(span, parts=P):
            return arena[0:parts, span[0]:span[0] + span[1]]

        def views(name, start):
            r = Region(start)
            got = {part: view(r.take(w)) for part, w in PACKS[name]}
            return got, arena[:, start:start + pack_words(name)]

        def bank(b, n=1):
            return psum[:, b:b + n, :].rearrange("p b n -> p (b n)")

        X = view(X_).rearrange("p (t d) -> p t d", t=NT)
        XT = view(XT_).rearrange("p (k t) -> p k t", k=KD)
        ident = view(IDENT_)
        CTX = view(CTX_).rearrange("p (t d) -> p t d", t=NT)
        CTXT = view(CTXT_).rearrange("p (k t) -> p k t", k=KD)
        small = Region(SMALL_[0])

        def tiny(words):
            return view(small.take(words))

        one = tiny(1)
        stats = tiny(TH * NT * 6).rearrange("p (t s) -> p t s", s=6)
        mv = tiny(TH * NT * 2).rearrange("p (t s) -> p t s", s=2)
        var = tiny(TH * NT)
        std = tiny(TH * NT)
        rstd = tiny(TH * NT)
        root_tmp = tiny(3 * TH * NT)
        root_k = tiny(3 * KVH)
        nmax = tiny(16)
        nbias = tiny(16)
        psums = tiny(16)
        rinv = tiny(16)
        a_neg = tiny(NBLK * NS)
        sum_sq = tiny(TH * NT)
        s_raw = tiny(NT * TH)
        s_gate = tiny(NT * TH)
        pos_f = tiny(B * KT)
        sel3 = tiny(NS).bitcast(BF16)
        assert small.at <= SMALL_[0] + SMALL_[1], small.at - SMALL_[0]

        ttt_w, ttt_all = views("ttt", TTTW_[0])

        wa = Region(wa_start)
        XS = view(wa.take(NBLK * B * PAD)).rearrange("p (m b t) -> p m b t", m=NBLK, b=B)
        YS = view((wa_start, NBLK * T)).rearrange("p (m t) -> p m t", m=NBLK)
        ZS = view(wa.take(NBLK * T)).rearrange("p (m t) -> p m t", m=NBLK)
        U = view(wa.take(NBLK * T)).rearrange("p (m t) -> p m t", m=NBLK)
        assert wa.at <= wb_start
        wb = Region(wb_start)
        DT = view(wb.take(NBLK * T)).rearrange("p (m t) -> p m t", m=NBLK)
        DTU = view(wb.take(NBLK * T)).rearrange("p (m t) -> p m t", m=NBLK)
        DTR = view(wb.take(T))
        assert wb.at <= c_start
        c1 = Region(c_start)
        w_inT = view(c1.take(KD * 2 * DI)).rearrange("p (k n) -> p k n", k=KD)
        mb_start = c1.take(pack_words("mamba"))[0]
        mb, mb_all = views("mamba", mb_start)
        loop = Region(c1.take(9 * T)[0])
        DBU = view(loop.take(2 * T)).rearrange("p (i t) -> p i t", i=2)
        H = view(loop.take(2 * T)).rearrange("p (i t) -> p i t", i=2)
        HC = view(loop.take(3 * T)).rearrange("p (i t) -> p i t", i=3)
        CB = view(loop.take(2 * T)).rearrange("p (i t) -> p i t", i=2)
        SPZ = view((wa_start, NBLK * T)).rearrange("p (m t) -> p m t", m=NBLK)
        SPE = view(c1.take(T))
        bc3 = view(c1.take(T // 2)).bitcast(BF16)
        bc_rest = view(c1.take(T))
        bc_mid = view(c1.take(T // 2)).bitcast(BF16)
        assert c1.at <= total, (c1.at, total)

        w_xT = mb["w_xT"].rearrange("p (m n) -> p m n", m=NBLK)
        w_outT = mb["w_outT"].rearrange("p (m n) -> p m n", m=NBLK)
        conv_w = mb["conv_w"].rearrange("p (m k) -> p m k", m=NBLK)
        a_log = mb["a_log"]
        N3 = 3 * 2 * NS

        c2 = Region(c_start)
        PR = view(c2.take(2 * 8 * L)).rearrange("p (i j m n) -> p i j m n", i=2, j=4, m=2)
        PT = view(c2.take(2 * 2 * L)).rearrange("p (i n m) -> p i n m", i=2, n=2)
        OT = view(c2.take(2 * P)).rearrange("p (i m c) -> p i m c", i=1, m=2)
        ffn, ffn_all = views("ffn", wa_start)
        fw1 = ffn["ffn1T"].rearrange("p (k n) -> p k n", k=KD)
        fw3 = ffn["ffn3T"].rearrange("p (k n) -> p k n", k=KD)
        fw2 = ffn["ffn2T"].rearrange("p (k d) -> p k d", k=NFB)
        fw2b = view((wa_start + pack_words("ffn"), NFB * D)).rearrange("p (k d) -> p k d", k=NFB)
        c3 = Region(c_start)
        HID = view(c3.take(NFB * T)).rearrange("p (k t) -> p k t", k=NFB)
        SG = view(c3.take(2 * 512)).rearrange("p (i t) -> p i t", i=2)
        w_qs = ttt_w["w_qs"].rearrange("p (k n) -> p k n", k=KD)
        w0T = ttt_w["w0T"].rearrange("p (h n) -> p h n", h=TH)
        w2T = ttt_w["w2T"].rearrange("p (h n) -> p h n", h=TH)
        w1T = ttt_w["w1T"].rearrange("p (h n) -> p h n", h=TH)
        w_oT = ttt_w["w_oT"].rearrange("p (h n) -> p h n", h=TH)
        c4 = Region(c_start)
        Q4 = view(c4.take(NT * D)).rearrange("p (t d) -> p t d", t=NT)
        SQ4 = view(c4.take(NT * D)).rearrange("p (t d) -> p t d", t=NT)
        QT4 = view(c4.take(TH * T)).rearrange("p (h b t) -> p h b t", h=TH, b=B)
        GH = view(c4.take(TH * T)).rearrange("p (h t) -> p h t", h=TH)
        SG4 = view(c4.take(2 * 512)).rearrange("p (i t) -> p i t", i=2)
        O4 = view(c4.take(NT * D)).rearrange("p (t d) -> p t d", t=NT)
        OT4 = view(c4.take(TH * T)).rearrange("p (h t) -> p h t", h=TH)
        assert c4.at <= total
        attn, attn_all = views("attn", wb_start)
        wqT = attn["wqT"].rearrange("p (k n) -> p k n", k=KD)
        wkT = attn["wkT"].rearrange("p (k n) -> p k n", k=KD)
        wvT = attn["wvT"].rearrange("p (k n) -> p k n", k=KD)
        woT = attn["woT"].rearrange("p (h n) -> p h n", h=QH)
        tab = Region(CTX_[0])
        KCOS = view(tab.take(KT * HD)).rearrange("p (t d) -> p t d", t=KT)
        KSIN = view(tab.take(KT * HD)).rearrange("p (t d) -> p t d", t=KT)
        QCOS = view(tab.take(2 * HD)).rearrange("p (t d) -> p t d", t=2)
        QSIN = view(tab.take(2 * HD)).rearrange("p (t d) -> p t d", t=2)
        assert tab.at <= CTX_[0] + CTX_[1]
        tmp5 = Region(TTTW_[0])
        RT1 = view(tmp5.take(2 * 512)).rearrange("p (i n) -> p i n", i=2)
        RAW5 = view(tmp5.take(2 * 512)).rearrange("p (i n) -> p i n", i=2)
        assert tmp5.at <= TTTW_[0] + TTTW_[1]
        c5 = Region(c_start)
        KTR = view(c5.take(KVH * 2 * L)).rearrange("p (h t) -> p h t", h=KVH)
        V5 = view(c5.take(KT * KVH * HD)).rearrange("p (t n) -> p t n", t=KT)
        QTR = view(c5.take(QH * L)).rearrange("p (h t) -> p h t", h=QH)
        AT = view(c5.take(QH * L)).rearrange("p (h t) -> p h t", h=QH)
        PR5 = view(c5.take(2 * 2 * 512)).rearrange("p (i m n) -> p i m n", i=2, m=2)
        PT5 = view(c5.take(KT * L)).rearrange("p (k n) -> p k n", k=KT)
        RT2 = view(c5.take(512))
        SQ5 = view(c5.take(512))
        ANG = view((c5.at - 1024, 3 * KT * ROPE)).rearrange("p (i t f) -> p i t f", i=3, t=KT)
        SINES = view(c5.take(3 * KT * ROPE)).rearrange("p (i t f) -> p i t f", i=3, t=KT)
        q_ss = view(c5.take(2 * QH))
        q_rs = view(c5.take(2 * QH))
        k_ss = view(c5.take(KT * KVH))
        k_rs = view(c5.take(KT * KVH))
        assert c5.at <= total, (c5.at, total)
        moe, moe_all = views("moe", wa_start)
        wa6 = moe["wa"].rearrange("p (k e) -> p k e", k=KD)
        wg6 = moe["wg"].rearrange("p (e k f) -> p e k f", e=NX, k=KD)
        w16 = moe["w1"].rearrange("p (e k f) -> p e k f", e=NX, k=KD)
        w26 = moe["w2"].rearrange("p (e d) -> p e d", e=NX)
        c6 = Region(c_start)
        AFF = view(c6.take(NT * NE)).rearrange("p (t e) -> p t e", t=NT)
        TOP = view(c6.take(NT * 8)).rearrange("p (t e) -> p t e", t=NT)
        TOPI = view(c6.take(NT * 8)).rearrange("p (t e) -> p t e", t=NT)
        PW = view(c6.take(NT * 2)).rearrange("p (t e) -> p t e", t=NT)
        PS = view(c6.take(NT))
        CMB = view(c6.take(NT * 2 * NS)).rearrange("p (t e) -> p t e", t=NT)
        PICK = view(c6.take(NT * NE)).rearrange("p (t e) -> p t e", t=NT)
        CT = view(c6.take(T))
        ct_rest = view(c6.take(T))
        ct_mid = view(c6.take(T // 2)).bitcast(BF16)
        ct3 = view(c6.take(T // 2)).bitcast(BF16)
        GE = view(c6.take(2 * 512)).rearrange("p (i t) -> p i t", i=2)
        YE = view(c6.take(2 * 512)).rearrange("p (i t) -> p i t", i=2)
        FT = view(c6.take(KD * T)).rearrange("p (k t) -> p k t", k=KD)
        assert c6.at <= total

        ld = {n: sem("loaded_" + n) for n in list(PACKS) + ["pos"]}
        consts_ready = sem("consts_ready")
        S = {n: sem(n) for n in SEMAPHORES.split()}

        block = ctx.enter_context(nc.Block())

        @block.sync
        def _(sp):
            sp.dma_start(arena[:, XT_[0]:XT_[0] + XT_[1]], dram["in"][:, 0:KD * T]).then_inc(ld["in"], 16)
            sp.dma_start(w_inT.rearrange("p k n -> p (k n)"), dram["in"][:, KD * T:]).then_inc(ld["in"], 16)
            sp.dma_start(mb_all, dram["mamba"]).then_inc(ld["mamba"], 16)
            sp.dma_start(ident, dram["ident"]).then_inc(ld["ident"], 16)
            sp.dma_start(arena[:, X_[0]:X_[0] + X_[1]], dram["x"]).then_inc(ld["x"], 16)
            sp.dma_start(arena[:, CTX_[0]:CTX_[0] + 2 * CTX_[1]], dram["ctx"]).then_inc(ld["ctx"], 16)
            sp.dma_start(ttt_all, dram["ttt"]).then_inc(ld["ttt"], 16)
            sp.dma_start(pos_i[:, :], dram["pos"]).then_inc(ld["pos"], 16)
            if LAST >= 3:
                sp.wait_ge(S["x_added"], NT)
                sp.dma_start(ffn_all, dram["ffn"]).then_inc(ld["ffn"], 16)
            if LAST >= 5:
                sp.dma_start(attn_all, dram["attn"]).then_inc(ld["attn"], 16)
            if LAST >= 6:
                sp.wait_ge(S["x_added"], 3 * NT)
                sp.dma_start(moe_all, dram["moe"]).then_inc(ld["moe"], 16)
            for i in range(NT):
                sp.wait_ge(S["x_ready"], NT * (LAST - 1) + i + 1)
                sp.dma_start(out[i * P:(i + 1) * P, :], X[:, i, :]).then_inc(S["stored"], 16)
            sp.wait_ge(S["stored"], 16 * NT)

        @block.tensor
        def _(pe):
            def turn_x(k):
                for i in range(NT):
                    pe.wait_ge(S["x_ready"], NT * (k - 1) + i + 1)
                    if i >= 2:
                        pe.wait_ge(S["xt_ready"], NT * (k - 2) + i - 1)
                    for f in range(KD):
                        mm = pe.transpose(psum[:, 6 + i % 2, f * P:(f + 1) * P], X[:, i, f * P:(f + 1) * P], ident)
                    mm.then_inc(S["xt_ps"], 1)
                pe.wait_ge(S["xt_ready"], NT * (k - 1))

            def mamba():
                pe.wait_ge(ld["in"], 32)
                for g in range(16):
                    m, n = g // 2, g % 2
                    if g >= 8:
                        pe.wait_ge(S["xs_copied"], g - 7)
                    for k in range(KD):
                        mm = pe.matmul(bank(g % 8), w_inT[:, k, m * P:(m + 1) * P], XT[:, k, n * 512:(n + 1) * 512],
                                       start=(k == 0), stop=(k == KD - 1))
                    mm.then_inc(S["proj_ps"], 1)
                pe.wait_ge(ld["mamba"], 16)
                pe.wait_ge(S["u_ready"], NBLK)
                pe.wait_ge(S["z_ready"], 8)
                def project_u(g):
                    n = g % 2
                    lo, width = (0, RANK) if g < 2 else (RANK, 2 * NS)
                    for m in range(NBLK):
                        mm = pe.matmul(psum[0:width, g, :], w_xT[:, m, lo:lo + width], U[:, m, n * 512:(n + 1) * 512],
                                       start=(m == 0), stop=(m == NBLK - 1))
                    mm.then_inc(S["dbl_ps"], 1)

                def project_dt(m):
                    for n in range(2):
                        mm = pe.matmul(bank(DT_BANKS[m] + n), mb["w_dtT"][:, m * P:(m + 1) * P],
                                       DTR[:, n * 512:(n + 1) * 512], start=True, stop=True)
                    mm.then_inc(S["dt_ps"], 1)

                for g in range(4):
                    project_u(g)
                pe.wait_ge(S["dtr_copied"], 1)
                for m in range(NBLK):
                    if m == 3:
                        pe.wait_ge(S["spz_ready"], 1)
                    project_dt(m)
                pe.wait_ge(S["spz_ready"], NBLK)

                def sum_y(it):
                    m, s = it // NS, it % NS
                    pe.wait_ge(S["hc_ready"], it + 1)
                    if s == 0 and m > 0:
                        pe.wait_ge(S["y_used"], m)
                    for n in range(2):
                        mm = pe.matmul(bank(6 + n), ident, HC[:, it % 3, n * 512:(n + 1) * 512],
                                       start=(s == 0), stop=(s == NS - 1))
                    mm.then_inc(S["hc_summed"], 1)

                pe.wait_ge(S["bc_ready"], 2)
                pe.wait_ge(ld["ident"], 16)
                for it in range(NBLK * NS):
                    s = it % NS
                    if it > 0:
                        pe.wait_ge(S["dbu_ready"], it)
                    for n in range(2):
                        mm = pe.matmul(bank(n), sel3[0:N3, s:s + 1].broadcast_to([N3, P]), bc3[0:N3, n * 512:(n + 1) * 512],
                                       start=True, stop=True)
                    mm.then_inc(S["b_ps"], 1)
                    if it > 0:
                        pe.wait_ge(S["c_copied"], it)
                    for n in range(2):
                        mm = pe.matmul(bank(2 + n), sel3[0:N3, NS + s:NS + s + 1].broadcast_to([N3, P]),
                                       bc3[0:N3, n * 512:(n + 1) * 512], start=True, stop=True)
                    mm.then_inc(S["c_ps"], 1)
                    if it > 1:
                        sum_y(it - 2)
                sum_y(NBLK * NS - 2)
                sum_y(NBLK * NS - 1)
                pe.wait_ge(S["y_ready"], NBLK)
                for i in range(NT):
                    if i >= 2:
                        pe.wait_ge(S["x_added"], i - 1)
                    for m in range(NBLK):
                        mm = pe.matmul(psum[:, 4 + i % 2, 0:D], YS[:, m, i * P:(i + 1) * P], w_outT[:, m, :],
                                       start=(m == 0), stop=(m == NBLK - 1))
                    mm.then_inc(S["out_ps"], 1)

            def cross1():
                pe.wait_ge(ld["ctx"], 16)

                def scores(u):
                    i, r = u // 2, u % 2
                    pe.wait_ge(S["x_ready"], i + 1)
                    if u >= 2:
                        pe.wait_ge(S["p_ready"], 4 * (u - 1))
                    for mt in range(2):
                        for j in (2 * r, 2 * r + 1):
                            rows = slice(XR * j, XR * (j + 1))
                            mm = pe.matmul(psum[:, 2 * r + j % 2, mt * L:(mt + 1) * L], X[rows, i, mt * P:(mt + 1) * P],
                                           CTX[rows, i, :], start=True, stop=True)
                    mm.then_inc(S["sc_ps"], 1)

                def turn_p(u, odd):
                    i, j = u // 2, 2 * (u % 2) + odd
                    if odd == 0:
                        pe.wait_ge(S["p_normed"], 4 * (u + 1))
                    if u >= 1:
                        pe.wait_ge(S["pt_copied"], 2 * u - 1 + odd)
                    for mt in range(2):
                        for nb in range(2):
                            mm = pe.transpose(psum[:, 4 + odd, nb * L + mt * P:nb * L + (mt + 1) * P],
                                              PR[:, i % 2, j, mt, nb * P:(nb + 1) * P], ident)
                    mm.then_inc(S["pt_ps"], 1)

                def weigh(u, odd):
                    i, j = u // 2, 2 * (u % 2) + odd
                    pe.wait_ge(S["pt_copied"], 2 * u + odd + 1)
                    if j == 0 and i >= 2:
                        pe.wait_ge(S["x_added"], NT + i - 1)
                    col = i * P + XR * j
                    for nb in range(2):
                        mm = pe.matmul(psum[XR * j:XR * (j + 1), 6 + i % 2, 0:D], CTXT[:, nb, col:col + XR],
                                       PT[:, odd, nb, :], start=(nb == 0), stop=(nb == 1))
                    if j == 3:
                        mm.then_inc(S["out_ps"], 1)

                scores(0)
                scores(1)
                pe.wait_ge(S["x_added"], NT)
                for u in range(2 * NT):
                    turn_p(u, 0)
                    turn_p(u, 1)
                    if u + 2 < 2 * NT:
                        scores(u + 2)
                    weigh(u, 0)
                    weigh(u, 1)
                pe.wait_ge(S["x_added"], 2 * NT)

            def swiglu():
                pe.wait_ge(ld["ffn"], 16)
                pe.wait_ge(S["bf_ready"], 6)
                for g in range(4):
                    if g == 0:
                        pe.wait_ge(S["p_ready"], 8 * NT)
                    mm = pe.matmul(bank(g), ffn["hadamard"], fw2b[:, 2 * g:2 * g + 2, :].rearrange("p k d -> p (k d)"),
                                   start=True, stop=True)
                    mm.then_inc(S["had_ps"], 1)
                turn_x(2)
                pe.wait_ge(S["w2h_ready"], 4)
                for g in range(2 * NFB):
                    n, h = g // NFB, g % NFB
                    if g >= 2:
                        pe.wait_ge(S["hid_ready"], g - 1)
                    for w, b0 in ((fw1, 0), (fw3, 2)):
                        for k in range(KD):
                            mm = pe.matmul(bank(b0 + g % 2), w[:, k, h * P:(h + 1) * P], XT[:, k, n * 512:(n + 1) * 512],
                                           start=(k == 0), stop=(k == KD - 1))
                        mm.then_inc(S["up_ps"], 1)
                for i in range(NT):
                    pe.wait_ge(S["hid_ready"], NFB * (1 + i // 4))
                    if i >= 2:
                        pe.wait_ge(S["x_added"], 2 * NT + i - 1)
                    for h in range(NFB):
                        mm = pe.matmul(psum[:, 4 + i % 2, 0:D], HID[:, h, i * P:(i + 1) * P], fw2[:, h, :],
                                       start=(h == 0), stop=(h == NFB - 1))
                    mm.then_inc(S["out_ps"], 1)

            def ttt():
                pe.wait_ge(ld["ttt"], 16)
                turn_x(3)
                for i in range(NT):
                    if i >= 4:
                        pe.wait_ge(S["q4_copied"], i - 3)
                    for k in range(KD):
                        mm = pe.matmul(psum[:, i % 4, 0:D + TH], XT[:, k, i * P:(i + 1) * P], w_qs[:, k, :],
                                       start=(k == 0), stop=(k == KD - 1))
                    mm.then_inc(S["q4_ps"], 1)
                pe.wait_ge(S["q4_ready"], 1)
                for i in range(NT):
                    if i >= 2:
                        pe.wait_ge(S["qt4_copied"], i - 1)
                    for h in range(TH):
                        mm = pe.transpose(psum[:, 4 + i % 2, h * P:(h + 1) * P], Q4[:, i, h * P:(h + 1) * P], ident)
                    mm.then_inc(S["qt4_ps"], 1)
                pe.wait_ge(S["qt4_copied"], NT)
                for g in range(4):
                    h, n = g // 2, g % 2
                    if g >= 2:
                        pe.wait_ge(S["gh_ready"], g - 1)
                    rhs = QT4[:, h, 2 * n:2 * n + 2, :].rearrange("p b t -> p (b t)")
                    pe.matmul(bank(g % 2), w0T[:, h, :], rhs, start=True, stop=True).then_inc(S["f4_ps"], 1)
                    pe.matmul(bank(2 + g % 2), w2T[:, h, :], rhs, start=True, stop=True).then_inc(S["f4_ps"], 1)
                pe.wait_ge(S["gh_ready"], 4)
                for i in range(NT):
                    if i >= 2:
                        pe.wait_ge(S["o4_copied"], i - 1)
                    for h in range(TH):
                        mm = pe.matmul(psum[:, 4 + i % 2, h * P:(h + 1) * P], GH[:, h, i * P:(i + 1) * P], w1T[:, h, :],
                                       start=True, stop=True)
                    mm.then_inc(S["o4_ps"], 1)
                for i in range(NT):
                    pe.wait_ge(S["o4_normed"], i + 1)
                    if i >= 2:
                        pe.wait_ge(S["ot4_copied"], i - 1)
                    for h in range(TH):
                        mm = pe.transpose(psum[:, 6 + i % 2, h * P:(h + 1) * P], O4[:, i, h * P:(h + 1) * P], ident)
                    mm.then_inc(S["ot4_ps"], 1)
                for i in range(NT):
                    pe.wait_ge(S["ot4_copied"], i + 1)
                    if i >= 4:
                        pe.wait_ge(S["x_added"], 3 * NT + i - 3)
                    for h in range(TH):
                        mm = pe.matmul(psum[:, i % 4, 0:D], OT4[:, h, i * P:(i + 1) * P], w_oT[:, h, :],
                                       start=(h == 0), stop=(h == TH - 1))
                    mm.then_inc(S["out_ps"], 1)

            def cross2():
                pe.wait_ge(ld["attn"], 16)
                turn_x(4)
                for b in range(B + 1):
                    def project(n):
                        g = 12 * b + n
                        c, t = divmod(n - KT, 2)
                        src, i, w, lo = (XT, b * 2 + t, wqT, c * 512) if n >= KT else \
                            (CTXT, b * 2 + n, wkT, 0) if n < CTXT_TILES else (XT, b * 2 + n - CTXT_TILES, wkT, 0)
                        if n >= EARLY:
                            pe.wait_ge(S["tr_copied"], g)
                        elif g >= 2:
                            pe.wait_ge(S["kq_copied"], g - 1)
                        if n == 0 and b > 0:
                            pe.wait_ge(S["at_copied"], QH * b)
                        if n == 1 and b > 0:
                            pe.wait_ge(S["tr_copied"], g - 1)
                        for k in range(KD):
                            mm = pe.matmul(bank(7 if n >= EARLY else 6 + n % 2), src[:, k, i * P:(i + 1) * P],
                                           w[:, k, lo:lo + 512], start=(k == 0), stop=(k == KD - 1))
                        mm.then_inc(S["kq_ps"], 1)

                    def turn(n):
                        g = 12 * b + n
                        if n == 0 and b > 0:
                            pe.wait_ge(S["pt5_copied"], 2 * QH * b)
                        pe.wait_ge(S["rope_sum"], g + 1)
                        if g >= 2:
                            pe.wait_ge(S["tr_copied"], g - 1)
                        if n < KT:
                            pe.wait_ge(S["k_scaled"], KT * b + n + 1)
                        for h in range(4):
                            mm = pe.transpose(psum[:, 7 if n >= EARLY else 4 + n % 2, h * P:(h + 1) * P],
                                              RT1[:, n % 2, h * P:(h + 1) * P], ident)
                        mm.then_inc(S["tr_ps"], 1)

                    def values(t, wait):
                        src, i = (CTXT, b * 2 + t) if t < CTXT_TILES else (XT, b * 2 + t - CTXT_TILES)
                        if wait:
                            pe.wait_ge(S["x_added"], 4 * NT + 2 * b)
                        for k in range(KD):
                            mm = pe.matmul(bank(t), src[:, k, i * P:(i + 1) * P], wvT[:, k, :],
                                           start=(k == 0), stop=(k == KD - 1))
                        mm.then_inc(S["v_ps"], 1)

                    def output(m):
                        if m == 0:
                            pe.wait_ge(S["at_copied"], QH * b)
                            pe.wait_ge(S["p5_ready"], 2 * QH * b)
                        for h in range(QH):
                            mm = pe.matmul(psum[:, m, 0:D], AT[:, h, m * P:(m + 1) * P], woT[:, h, :],
                                           start=(h == 0), stop=(h == QH - 1))
                        mm.then_inc(S["out_ps"], 1)

                    if b == B:
                        output(0)
                        output(1)
                        break
                    project(0)
                    project(1)
                    if b > 0:
                        output(0)
                    turn(0)
                    project(2)
                    turn(1)
                    project(3)
                    if b > 0:
                        output(1)
                    turn(2)
                    project(4)
                    turn(3)
                    project(5)
                    values(2, False)
                    values(3, False)
                    turn(4)
                    project(6)
                    values(0, b > 0)
                    values(1, b > 0)
                    turn(5)
                    turn(6)

                    def scores(h):
                        g = QH * b + h
                        if h == 0:
                            pe.wait_ge(S["v_copied"], KT * (b + 1))
                        if h % 4 == 0:
                            pe.wait_ge(S["tr_copied"], 12 * b + 6 + h // 2)
                        if h >= 2:
                            pe.wait_ge(S["p5_ready"], 2 * (g - 1))
                        for m in range(2):
                            mm = pe.matmul(bank(2 * (h % 2) + m), QTR[:, h, m * P:(m + 1) * P], KTR[:, h // 4, :],
                                           start=True, stop=True)
                            mm.then_inc(S["s5_ps"], 1)

                    def turn_p(h):
                        if h == 0:
                            pe.wait_ge(S["tr_copied"], 12 * b + EARLY)
                        for m in range(2):
                            g = 2 * (QH * b + h) + m
                            pe.wait_ge(S["p5_normed"], g + 1)
                            if g >= 2:
                                pe.wait_ge(S["pt5_copied"], g - 1)
                            for kt in range(KT):
                                mm = pe.transpose(psum[:, 4 + m, kt * P:(kt + 1) * P],
                                                  PR5[:, h % 2, m, kt * P:(kt + 1) * P], ident)
                            mm.then_inc(S["pt5_ps"], 1)

                    def weigh(h):
                        g = QH * b + h
                        pe.wait_ge(S["pt5_copied"], 2 * (g + 1))
                        if h >= 1:
                            pe.wait_ge(S["at_copied"], g)
                        for kt in range(KT):
                            mm = pe.matmul(psum[:, 6, 0:L], V5[:, kt, (h // 4) * HD:(h // 4 + 1) * HD],
                                           PT5[:, kt, :], start=(kt == 0), stop=(kt == KT - 1))
                        mm.then_inc(S["at_ps"], 1)

                    scores(0)
                    scores(1)
                    for h in range(QH):
                        turn_p(h)
                        if h + 2 < QH:
                            scores(h + 2)
                        weigh(h)
                        n = EARLY + h // 2
                        if n < 12:
                            if h % 2 == 0:
                                project(n)
                            else:
                                turn(n)

            def experts():
                pe.wait_ge(ld["moe"], 16)
                turn_x(5)
                for i in range(NT):
                    for k in range(KD):
                        mm = pe.matmul(psum[:, 0, i * NE:(i + 1) * NE], XT[:, k, i * P:(i + 1) * P], wa6[:, k, :],
                                       start=(k == 0), stop=(k == KD - 1))
                mm.then_inc(S["aff_ps"], 1)
                pe.wait_ge(S["cmb_ready"], 1)
                for i in range(NT):
                    mm = pe.transpose(psum[0:2 * NS, 4 + i // 4, (i % 4) * P:(i % 4 + 1) * P], CMB[:, i, :], ident)
                mm.then_inc(S["ct_ps"], 1)
                pe.wait_ge(S["ct_ready"], 2)

                def up(g):
                    n, e = g // NX, g % NX
                    if g >= 2:
                        pe.wait_ge(S["ye_ready"], g - 1)
                    for w, b0 in ((wg6, 2), (w16, 4)):
                        for k in range(KD):
                            mm = pe.matmul(bank(b0 + g % 2), w[:, e, k, :], XT[:, k, n * 512:(n + 1) * 512],
                                           start=(k == 0), stop=(k == KD - 1))
                        mm.then_inc(S["ge_ps"], 1)
                    if e < NE:
                        pe.matmul(bank(6 + g % 2), sel3[0:N3, e:e + 1].broadcast_to([N3, P]),
                                  ct3[0:N3, n * 512:(n + 1) * 512], start=True, stop=True).then_inc(S["cb_ps"], 1)

                def down(g):
                    n, e = g // NX, g % NX
                    if e == 0:
                        if n == 1:
                            pe.wait_ge(S["ft_copied"], 2)
                        for f in range(KD):
                            pe.matmul(bank(f), moe["b2"][0:NX, f * P:(f + 1) * P], CT[0:NX, n * 512:(n + 1) * 512],
                                      start=True, stop=False)
                    pe.wait_ge(S["ye_ready"], g + 1)
                    for f in range(KD):
                        mm = pe.matmul(bank(f), w26[:, e, f * P:(f + 1) * P], YE[:, g % 2, :],
                                       start=False, stop=(e == NX - 1))
                    mm.then_inc(S["ye_used"], 1)

                for g in range(2 * NX):
                    up(g)
                    if g > 0:
                        down(g - 1)
                down(2 * NX - 1)
                for i in range(NT):
                    pe.wait_ge(S["ft_copied"], 4)
                    if i >= 2:
                        pe.wait_ge(S["x_added"], 5 * NT + i - 1)
                    for f in range(KD):
                        mm = pe.transpose(psum[:, 6 + i % 2, f * P:(f + 1) * P], FT[:, f, i * P:(i + 1) * P], ident)
                    mm.then_inc(S["out_ps"], 1)

            for step, program in enumerate([mamba, cross1, swiglu, ttt, cross2, experts]):
                if LAST > step:
                    program()

        @block.scalar
        def _(act):
            def turn_x(k):
                for i in range(NT):
                    act.wait_ge(S["xt_ps"], NT * (k - 2) + i + 1)
                    act.activation(XT[:, :, i * P:(i + 1) * P], psum[:, 6 + i % 2, 0:D].rearrange("p (f t) -> p f t", f=KD),
                                   ACT.Copy).then_inc(S["xt_ready"], 1)

            def mamba():
                for g in range(8, 16):
                    m, n = g // 2 - 4, g % 2
                    act.wait_ge(S["proj_ps"], g + 1)
                    act.activation(ZS[:, m, n * 512:(n + 1) * 512], bank(g % 8), ACT.Silu).then_inc(S["z_ready"], 1)
                for m in range(NBLK):
                    act.wait_ge(S["conv_done"], m + 1)
                    act.activation(U[:, m, :], U[:, m, :], ACT.Silu).then_inc(S["u_ready"], 1)
                act.wait_ge(S["dbl_ps"], 2)
                act.activation(DTR, bank(0, 2), ACT.Copy).then_inc(S["dtr_copied"], 1)
                act.activation(a_neg, a_log, ACT.Exp).then_inc(S["a_exp"], 1)
                def softplus(m):
                    act.wait_ge(S["spz_ready"], m + 1)
                    if m > 0:
                        act.wait_ge(S["spe_used"], m)
                    act.activation(SPE, SPZ[:, m, :], ACT.Abs).then_inc(S["act_step"], 1)
                    act.wait_ge(S["act_step"], 2 * m + 1)
                    act.activation(SPE, SPE, ACT.Exp, scale=-1.0).then_inc(S["act_step"], 1)
                    act.wait_ge(S["act_step"], 2 * m + 2)
                    act.activation(DTU[:, m, :], SPE, ACT.Ln, bias=one).then_inc(S["spl_ready"], 1)

                softplus(0)
                act.wait_ge(S["a_ready"], 1)
                for it in range(NBLK * NS):
                    m, s = it // NS, it % NS
                    if s == 0:
                        act.wait_ge(S["dt_ready"], m + 1)
                    if it > 0:
                        act.wait_ge(S["h_ready"], it)
                    act.activation(bank(4, 2), DT[:, m, :], ACT.Exp, scale=a_neg[:, it:it + 1]).then_inc(S["da_ready"], 1)
                    act.wait_ge(S["c_ps"], it + 1)
                    if it >= 2:
                        act.wait_ge(S["hc_ready"], it - 1)
                    act.activation(CB[:, it % 2, :], bank(2, 2), ACT.Copy).then_inc(S["c_copied"], 1)
                    if s == 2 and m + 1 < NBLK:
                        softplus(m + 1)

            def cross1():
                def exps(u):
                    i, r = u // 2, u % 2
                    act.wait_ge(S["nbias_ready"], u + 1)
                    if u >= 4:
                        act.wait_ge(S["pt_ps"], 2 * (u - 3))
                    for j in (2 * r, 2 * r + 1):
                        for mt in range(2):
                            c = 8 * (i % 2) + 2 * j + mt
                            act.activation(PR[:, i % 2, j, mt, :], psum[:, 2 * r + j % 2, mt * L:(mt + 1) * L], ACT.Exp,
                                           bias=nbias[:, c:c + 1], scale=XSCALE,
                                           accum_out=psums[:, c:c + 1]).then_inc(S["p_ready"], 1)

                exps(0)
                for u in range(2 * NT):
                    if u + 1 < 2 * NT:
                        exps(u + 1)
                    for odd in range(2):
                        act.wait_ge(S["pt_ps"], 2 * u + odd + 1)
                        act.activation(PT[:, odd, :, :].rearrange("p n m -> p (n m)"), bank(4 + odd), ACT.Copy)\
                           .then_inc(S["pt_copied"], 1)

            def swiglu():
                for g in range(4):
                    act.wait_ge(S["had_ps"], g + 1)
                    act.activation(fw2[:, 2 * g:2 * g + 2, :].rearrange("p k d -> p (k d)"), bank(g), ACT.Copy,
                                   scale=float(FF) ** -0.5).then_inc(S["w2h_ready"], 1)
                turn_x(2)
                for g in range(2 * NFB):
                    act.wait_ge(S["up_ps"], 2 * g + 1)
                    if g >= 2:
                        act.wait_ge(S["hid_ready"], g - 1)
                    act.activation(SG[:, g % 2, :], bank(g % 2), ACT.Silu).then_inc(S["sg_ready"], 1)

            def ttt():
                turn_x(3)
                for i in range(NT):
                    act.wait_ge(S["q4_ps"], i + 1)
                    act.activation(s_raw[:, TH * i:TH * (i + 1)], psum[:, i % 4, D:D + TH], ACT.Copy).then_inc(S["s4_copied"], 1)
                    act.activation(Q4[:, i, :], psum[:, i % 4, 0:D], ACT.Silu).then_inc(S["q4_copied"], 1)
                act.wait_ge(S["s4_raw"], 1)
                act.activation(s_gate, s_raw, ACT.Silu).then_inc(S["s4_ready"], 1)
                for i in range(NT):
                    b, h = i // 2, i % 2
                    act.wait_ge(S["qt4_ps"], i + 1)
                    act.activation(QT4[:, h, b, :].rearrange("p (t h) -> p h t", h=TH),
                                   psum[:, 4 + i % 2, 0:D].rearrange("p (h t) -> p h t", h=TH), ACT.Copy)\
                       .then_inc(S["qt4_copied"], 1)
                for g in range(4):
                    act.wait_ge(S["f4_ps"], 2 * g + 1)
                    if g >= 2:
                        act.wait_ge(S["gh_ready"], g - 1)
                    act.activation(SG4[:, g % 2, :], bank(g % 2), ACT.Silu).then_inc(S["sg4_ready"], 1)
                for i in range(NT):
                    act.wait_ge(S["o4_ps"], i + 1)
                    act.activation(O4[:, i, :], psum[:, 4 + i % 2, 0:D], ACT.Copy).then_inc(S["o4_copied"], 1)
                for i in range(NT):
                    act.wait_ge(S["ot4_ps"], i + 1)
                    act.activation(OT4[:, :, i * P:(i + 1) * P], psum[:, 6 + i % 2, 0:D].rearrange("p (h t) -> p h t", h=TH),
                                   ACT.Copy).then_inc(S["ot4_copied"], 1)

            def cross2():
                turn_x(4)

                def sines(b):
                    act.wait_ge(S["ang_ready"], 2 * (b + 1))
                    act.activation(SINES[:, 0, :, :], ANG[:, 0, :, :], ACT.Sin, scale=-1.0).then_inc(S["sines_ready"], 1)
                    act.activation(SINES[:, 1, :, :], ANG[:, 0, :, :], ACT.Sin).then_inc(S["sines_ready"], 1)
                    act.activation(SINES[:, 2, :, :], ANG[:, 2, :, :], ACT.Sin).then_inc(S["sines_ready"], 1)

                sines(0)
                for b in range(B):
                    def project(n):
                        g = 12 * b + n
                        act.wait_ge(S["kq_ps"], g + 1)
                        if g >= 2:
                            act.wait_ge(S["rope_sum"], g - 1)
                        act.activation(RAW5[:, n % 2, :], bank(7 if n >= EARLY else 6 + n % 2), ACT.Copy)\
                           .then_inc(S["kq_copied"], 1)

                    def square(n):
                        g = 12 * b + n
                        act.wait_ge(S["kq_copied"], g + 1)
                        if g >= 1:
                            act.wait_ge(S["ss_ready"], g)
                        act.activation(SQ5, RAW5[:, n % 2, :], ACT.Square).then_inc(S["sq_ready"], 1)

                    def turn(n):
                        act.wait_ge(S["tr_ps"], 12 * b + n + 1)
                        got = bank(7 if n >= EARLY else 4 + n % 2).rearrange("p (h t) -> p h t", h=4)
                        if n < KT:
                            dst = KTR[:, :, n * P:(n + 1) * P]
                        else:
                            c, t = divmod(n - KT, 2)
                            dst = QTR[:, 4 * c:4 * c + 4, t * P:(t + 1) * P]
                        act.activation(dst, got, ACT.Copy).then_inc(S["tr_copied"], 1)

                    def values(n, t):
                        act.wait_ge(S["v_ps"], KT * b + n + 1)
                        act.activation(V5[:, t, :], bank(t), ACT.Copy).then_inc(S["v_copied"], 1)

                    project(0)
                    square(0)
                    for n in range(1, EARLY):
                        project(n)
                        square(n)
                        if n == 6:
                            values(0, 2)
                            values(1, 3)
                        turn(n - 1)
                    values(2, 0)
                    values(3, 1)
                    turn(EARLY - 1)

                    def probs(h):
                        for m in range(2):
                            g = 2 * (QH * b + h) + m
                            act.wait_ge(S["nb5_ready"], g + 1)
                            if h >= 2:
                                act.wait_ge(S["pt5_ps"], g - 3)
                            c = 2 * h + m
                            act.activation(PR5[:, h % 2, m, :], bank(2 * (h % 2) + m), ACT.Exp, scale=q_rs[:, c:c + 1],
                                           bias=nbias[:, g % 4:g % 4 + 1],
                                           accum_out=psums[:, g % 4:g % 4 + 1]).then_inc(S["p5_ready"], 1)

                    probs(0)
                    for h in range(QH):
                        n = EARLY + (h - 1) // 2
                        if h >= 1 and n < 12:
                            if h % 2 == 1:
                                project(n)
                            else:
                                turn(n)
                        for m in range(2):
                            g = 2 * (QH * b + h) + m
                            act.wait_ge(S["pt5_ps"], g + 1)
                            act.activation(PT5[:, :, m * P:(m + 1) * P], bank(4 + m).rearrange("p (k n) -> p k n", k=KT),
                                           ACT.Copy).then_inc(S["pt5_copied"], 1)
                        if h + 1 < QH:
                            probs(h + 1)
                        if h % 2 == 1 and n < 12:
                            square(n)
                        if h == 12 and b + 1 < B:
                            sines(b + 1)

            def experts():
                turn_x(5)
                act.wait_ge(S["aff_ps"], 1)
                act.activation(AFF.rearrange("p t e -> p (t e)"), psum[:, 0, 0:NT * NE], ACT.Exp, scale=-1.0)\
                   .then_inc(S["aff_exp"], 1)
                act.wait_ge(S["ct_ps"], 1)
                act.activation(CT[0:2 * NS, :], psum[0:2 * NS, 4:6, :].rearrange("p b n -> p (b n)"), ACT.Copy)\
                   .then_inc(S["ct_copied"], 1)
                for g in range(2 * NX):
                    e = g % NX
                    act.wait_ge(S["ge_ps"], 2 * g + 1)
                    if g >= 2:
                        act.wait_ge(S["ye_ready"], g - 1)
                    act.activation(GE[:, g % 2, :], bank(2 + g % 2), ACT.Gelu, bias=moe["gb"][:, e:e + 1])\
                       .then_inc(S["ge_ready"], 1)
                    if e == NX - 1:
                        n = g // NX
                        act.wait_ge(S["ye_used"], g + 1)
                        for f in range(KD):
                            act.activation(FT[:, f, n * 512:(n + 1) * 512], bank(f), ACT.Copy).then_inc(S["ft_copied"], 1)

            act.wait_ge(consts_ready, 1)
            for step, program in enumerate([mamba, cross1, swiglu, ttt, cross2, experts]):
                if LAST > step:
                    program()

        @block.vector
        def _(dve):
            steps = [0]

            def step(instruction):
                steps[0] += 1
                instruction.then_inc(S["dve_step"], 1)

            def settle():
                dve.wait_ge(S["dve_step"], steps[0])

            def spread(k, i):
                dve.wait_ge(S["x_added"], NT * (k - 1) + i + 1)
                step(dve.bn_stats(stats[:, i, :], X[:, i, :]))
                settle()
                dve.bn_aggr(mv[:, i, :], stats[:, i, :]).then_inc(S["ln_var"], 1)

            def apply_norm(k, i):
                dve.wait_ge(S["ln_rstd"], NT * (k - 1) + i + 1)
                dve.tensor_scalar(X[:, i, :], X[:, i, :], mv[:, i, 0:1], rstd[:, i:i + 1], ALU.subtract, ALU.mult)\
                   .then_inc(S["x_ready"], 1)

            def add_norm(k, source, twice=False, leave_last=False):
                for i in range(NT):
                    dve.wait_ge(S["out_ps"], NT * (k - 1) + i + 1)
                    dve.scalar_tensor_tensor(out=X[:, i, :], in0=X[:, i, :], scalar=2.0 if twice else 1.0, in1=source(i),
                                             op0=ALU.mult, op1=ALU.add).then_inc(S["x_added"], 1)
                    spread(k, i)
                    if i >= 1:
                        apply_norm(k, i - 1)
                if not leave_last:
                    apply_norm(k, NT - 1)

            def three_parts(source, out3, rest, mid, rows, ready):
                step(dve.tensor_copy(out3[0:rows, :], source))
                settle()
                step(dve.tensor_tensor(rest[0:rows, :], source, out3[0:rows, :], ALU.subtract))
                settle()
                step(dve.tensor_copy(mid[0:rows, :], rest[0:rows, :]))
                settle()
                dve.tensor_tensor(out3[64:64 + rows, :], rest[0:rows, :], mid[0:rows, :], ALU.subtract).then_inc(ready, 1)
                dve.tensor_copy(out3[32:32 + rows, :], mid[0:rows, :]).then_inc(ready, 1)

            def mamba():
                step(dve.memset(XS[:, :, :, 0:DCONV - 1], 0.0))
                for g in range(8):
                    m, n = g // 2, g % 2
                    dve.wait_ge(S["proj_ps"], g + 1)
                    dve.tensor_copy(XS[:, m, 2 * n:2 * n + 2, DCONV - 1:], bank(g).rearrange("p (b t) -> p b t", b=2))\
                       .then_inc(S["xs_copied"], 1)
                dve.wait_ge(ld["mamba"], 16)
                step(dve.tensor_copy(sel3[0:N3, :], mb["sel3"][0:N3, :]))
                settle()
                for m in range(NBLK):
                    dve.wait_ge(S["xs_copied"], 2 * m + 2)
                    um = U[:, m, :].rearrange("p (b t) -> p b t", b=B)
                    step(dve.tensor_scalar(um, XS[:, m, :, 0:L], conv_w[:, m, 0:1], mb["conv_b"][:, m:m + 1], ALU.mult, ALU.add))
                    for k in range(1, DCONV):
                        settle()
                        tap = dve.scalar_tensor_tensor(out=um, in0=XS[:, m, :, k:k + L], scalar=conv_w[:, m, k:k + 1], in1=um,
                                                       op0=ALU.mult, op1=ALU.add)
                        if k < DCONV - 1:
                            step(tap)
                        else:
                            tap.then_inc(S["conv_done"], 1)
                def softplus_in(m):
                    dve.wait_ge(S["dt_ps"], m + 1)
                    dve.tensor_scalar(SPZ[:, m, :], bank(DT_BANKS[m], 2), mb["b_dt"][:, m:m + 1], None, ALU.add)\
                       .then_inc(S["spz_ready"], 1)

                def softplus_out(m):
                    dve.wait_ge(S["act_step"], 2 * m + 2)
                    step(dve.tensor_scalar(DT[:, m, :], SPE, 1.0, 1.0, ALU.add, ALU.subtract))
                    settle()
                    step(dve.tensor_tensor(DT[:, m, :], SPE, DT[:, m, :], ALU.subtract))
                    dve.wait_ge(S["spl_ready"], m + 1)
                    dve.scalar_tensor_tensor(out=SPZ[:, m, :], in0=SPZ[:, m, :], scalar=0.0, in1=DTU[:, m, :],
                                             op0=ALU.max, op1=ALU.add).then_inc(S["spe_used"], 1)
                    settle()
                    dve.wait_ge(S["spe_used"], m + 1)
                    step(dve.tensor_tensor(DT[:, m, :], SPZ[:, m, :], DT[:, m, :], ALU.add))
                    settle()
                    step(dve.tensor_tensor(DTU[:, m, :], DT[:, m, :], U[:, m, :], ALU.mult))
                    settle()
                    dve.memset(DT[:, m, :].rearrange("p (b t) -> p b t", b=B)[:, :, 0:1], STEP0_DT).then_inc(S["dt_ready"], 1)

                softplus_in(0)
                softplus_in(1)
                three_parts(psum[0:2 * NS, 2:4, :].rearrange("p b n -> p (b n)"), bc3, bc_rest, bc_mid, 2 * NS,
                            S["bc_ready"])
                softplus_in(2)
                softplus_in(3)
                dve.wait_ge(S["a_exp"], 1)
                dve.tensor_scalar(a_neg, a_neg, -1.0, None, ALU.mult).then_inc(S["a_ready"], 1)
                softplus_out(0)

                def input_term(it):
                    m = it // NS
                    dve.wait_ge(S["b_ps"], it + 1)
                    dve.tensor_tensor(DBU[:, it % 2, :], bank(0, 2), DTU[:, m, :], ALU.mult).then_inc(S["dbu_ready"], 1)

                def gate_y(m):
                    dve.wait_ge(S["hc_summed"], NS * (m + 1))
                    dve.scalar_tensor_tensor(out=YS[:, m, :], in0=U[:, m, :], scalar=mb["d_skip"][:, m:m + 1], in1=bank(6, 2),
                                             op0=ALU.mult, op1=ALU.add).then_inc(S["y_used"], 1)
                    dve.wait_ge(S["y_used"], m + 1)
                    dve.tensor_tensor(YS[:, m, :], YS[:, m, :], ZS[:, m, :], ALU.mult).then_inc(S["y_ready"], 1)

                n_it = NBLK * NS
                input_term(0)
                for it in range(n_it):
                    dve.wait_ge(S["da_ready"], it + 1)
                    dve.wait_ge(S["dbu_ready"], it + 1)
                    if it >= 2:
                        dve.wait_ge(S["hc_ready"], it - 1)
                    dve.tensor_tensor_scan(H[:, it % 2, :], bank(4, 2), DBU[:, it % 2, :], 0.0, ALU.mult, ALU.add)\
                       .then_inc(S["h_ready"], 1)
                    if it + 1 < n_it:
                        input_term(it + 1)
                    if it >= NS and it % NS == 1:
                        gate_y(it // NS - 1)
                    if it % NS == 4 and it // NS + 1 < NBLK:
                        softplus_out(it // NS + 1)
                gate_y(NBLK - 1)
                dve.wait_ge(ld["x"], 16)
                add_norm(1, lambda i: psum[:, 4 + i % 2, 0:D], leave_last=LAST > 1)

            def cross1():
                def bias(u):
                    c = slice(8 * (u // 2 % 2) + 4 * (u % 2), 8 * (u // 2 % 2) + 4 * (u % 2) + 4)
                    dve.wait_ge(S["sc_ps"], u + 1)
                    step(dve.tensor_reduce(nmax[:, c], psum[:, 2 * (u % 2):2 * (u % 2) + 2, :]
                                           .rearrange("p b (m n) -> p (b m) n", m=2), AX.X, ALU.max, negate=True))
                    settle()
                    dve.tensor_scalar(nbias[:, c], nmax[:, c], XSCALE, None, ALU.mult).then_inc(S["nbias_ready"], 1)

                def normalise(u):
                    i, r = u // 2, u % 2
                    c0 = 8 * (i % 2) + 4 * r
                    dve.wait_ge(S["p_ready"], 4 * (u + 1))
                    step(dve.reciprocal(rinv[:, c0:c0 + 4], psums[:, c0:c0 + 4]))
                    settle()
                    for c in range(4):
                        p = PR[:, i % 2, 2 * r + c // 2, c % 2, :]
                        dve.tensor_scalar(p, p, rinv[:, c0 + c:c0 + c + 1], None, ALU.mult).then_inc(S["p_normed"], 1)

                def add(i):
                    dve.wait_ge(S["out_ps"], NT + i + 1)
                    dve.tensor_tensor(X[:, i, :], X[:, i, :], psum[:, 6 + i % 2, 0:D], ALU.add).then_inc(S["x_added"], 1)
                    spread(2, i)

                bias(0)
                normalise(0)
                apply_norm(1, NT - 1)
                for u in range(2 * NT):
                    if u + 1 < 2 * NT:
                        bias(u + 1)
                        normalise(u + 1)
                    if u % 2 == 0 and u >= 2:
                        add(u // 2 - 1)
                    if u % 2 == 1 and u >= 3:
                        apply_norm(2, u // 2 - 1)
                add(NT - 1)
                apply_norm(2, NT - 1)

            def swiglu():
                for g in range(2 * NFB):
                    n, h = g // NFB, g % NFB
                    dve.wait_ge(S["up_ps"], 2 * g + 2)
                    dve.wait_ge(S["sg_ready"], g + 1)
                    dve.tensor_tensor(HID[:, h, n * 512:(n + 1) * 512], SG[:, g % 2, :], bank(2 + g % 2), ALU.mult)\
                       .then_inc(S["hid_ready"], 1)
                add_norm(3, lambda i: psum[:, 4 + i % 2, 0:D])

            def ttt():
                dve.wait_ge(S["s4_copied"], NT)
                dve.wait_ge(ld["ttt"], 16)
                s3 = s_raw.rearrange("p (t h) -> p t h", h=TH)
                dve.tensor_tensor(s3, s3, ttt_w["b_s"].unsqueeze(1).broadcast_to([P, NT, TH]), ALU.add)\
                   .then_inc(S["s4_raw"], 1)
                dve.wait_ge(S["q4_copied"], NT)
                flat = Q4.rearrange("p t d -> p (t d)")
                sq = SQ4.rearrange("p t d -> p (t d)")
                heads = flat.rearrange("p (g d) -> p g d", d=THD)
                step(dve.tensor_tensor(sq, flat, flat, ALU.mult))
                settle()
                dve.tensor_reduce(sum_sq, sq.rearrange("p (g d) -> p g d", d=THD), AX.X, ALU.add).then_inc(S["ss4_ready"], 1)
                dve.wait_ge(S["norm4_ready"], 1)
                step(dve.reciprocal(rstd, std))
                settle()
                dve.tensor_tensor(heads, heads, rstd.unsqueeze(2).broadcast_to([P, TH * NT, THD]), ALU.mult)\
                   .then_inc(S["q4_ready"], 1)
                for g in range(4):
                    h, n = g // 2, g % 2
                    dve.wait_ge(S["f4_ps"], 2 * g + 2)
                    dve.wait_ge(S["sg4_ready"], g + 1)
                    dve.tensor_tensor(GH[:, h, n * 512:(n + 1) * 512], SG4[:, g % 2, :], bank(2 + g % 2), ALU.mult)\
                       .then_inc(S["gh_ready"], 1)
                for i in range(NT):
                    dve.wait_ge(S["o4_copied"], i + 1)
                    for h in range(TH):
                        step(dve.bn_stats(stats[:, TH * i + h, :], O4[:, i, h * THD:(h + 1) * THD]))
                settle()
                for j in range(TH * NT):
                    dve.bn_aggr(mv[:, j, :], stats[:, j, :]).then_inc(S["o4_var"], 1)
                dve.wait_ge(S["o4_rstd"], 1)
                dve.wait_ge(S["s4_ready"], 1)
                for i in range(NT):
                    o = O4[:, i, :].rearrange("p (h d) -> p h d", h=TH)
                    for h in range(TH):
                        j = TH * i + h
                        step(dve.tensor_scalar(o[:, h, :], o[:, h, :], mv[:, j, 0:1], rstd[:, j:j + 1], ALU.subtract, ALU.mult))
                    settle()
                    step(dve.tensor_tensor(o, o, ttt_w["ln_g"].unsqueeze(1).broadcast_to([P, TH, THD]), ALU.mult))
                    settle()
                    step(dve.tensor_tensor(o, o, ttt_w["ln_b"].unsqueeze(1).broadcast_to([P, TH, THD]), ALU.add))
                    settle()
                    dve.tensor_tensor(o, o, s_gate[:, TH * i:TH * i + TH].unsqueeze(2).broadcast_to([P, TH, THD]), ALU.mult)\
                       .then_inc(S["o4_normed"], 1)
                add_norm(4, lambda i: psum[:, i % 4, 0:D])

            def cross2():
                dve.wait_ge(ld["pos"], 16)
                step(dve.tensor_copy(pos_f, pos_i[:, :]))
                dve.wait_ge(ld["attn"], 16)
                settle()

                def angles(b):
                    x_, k_, c_ = ANG[:, 0, :, :], ANG[:, 1, :, :], ANG[:, 2, :, :]
                    for t in range(KT):
                        step(dve.tensor_scalar(x_[:, t, :], attn["inv_freq"], pos_f[:, KT * b + t:KT * b + t + 1], None, ALU.mult))
                    settle()
                    step(dve.tensor_scalar(k_, x_, float(1 / (2 * np.pi)), ROUND, ALU.mult, ALU.add))
                    settle()
                    step(dve.tensor_scalar(k_, k_, ROUND, None, ALU.subtract))
                    settle()
                    step(dve.scalar_tensor_tensor(out=x_, in0=k_, scalar=-TURN_HI, in1=x_, op0=ALU.mult, op1=ALU.add))
                    settle()
                    step(dve.scalar_tensor_tensor(out=x_, in0=k_, scalar=-TURN_LO, in1=x_, op0=ALU.mult, op1=ALU.add))
                    settle()
                    step(dve.tensor_scalar(c_, x_, float(np.pi / 2), None, ALU.add))
                    settle()
                    step(dve.tensor_scalar(k_, c_, float(np.pi), -float(2 * np.pi), ALU.is_gt, ALU.mult))
                    settle()
                    step(dve.tensor_tensor(c_, c_, k_, ALU.add))
                    settle()
                    dve.tensor_scalar(c_, c_, PI_MAX, -PI_MAX, ALU.min, ALU.max).then_inc(S["ang_ready"], 1)
                    dve.tensor_scalar(x_, x_, PI_MAX, -PI_MAX, ALU.min, ALU.max).then_inc(S["ang_ready"], 1)

                def tables(b):
                    def table(dst_cos, dst_sin, w, w_swap, t0, n):
                        halves = "p t (i f) -> p t i f"
                        step(dve.tensor_tensor(dst_cos.rearrange(halves, i=2),
                                               w.rearrange("p (i f) -> p i f", i=2).unsqueeze(1).broadcast_to([P, n, 2, ROPE]),
                                               SINES[:, 2, t0:t0 + n, :].unsqueeze(2).broadcast_to([P, n, 2, ROPE]), ALU.mult))
                        step(dve.tensor_tensor(dst_sin.rearrange(halves, i=2),
                                               w_swap.rearrange("p (i f) -> p i f", i=2).unsqueeze(1).broadcast_to([P, n, 2, ROPE]),
                                               SINES[:, 0:2, t0:t0 + n, :].rearrange("p i t f -> p t i f"), ALU.mult))

                    dve.wait_ge(S["sines_ready"], 3 * (b + 1))
                    table(KCOS, KSIN, attn["k_w"], attn["k_w_swap"], 0, KT)
                    table(QCOS, QSIN, attn["q_w"], attn["q_w_swap"], CTXT_TILES, 2)
                    settle()

                def root_of_keys(n, g):
                    kr = k_rs[:, KVH * n:KVH * (n + 1)]
                    arg, half, t = root_k[:, 0:KVH], root_k[:, KVH:2 * KVH], root_k[:, 2 * KVH:3 * KVH]
                    dve.wait_ge(S["ss_ready"], g + 1)
                    step(dve.tensor_scalar(arg, k_ss[:, KVH * n:KVH * (n + 1)], 1.0 / HD, RMS_EPS, ALU.mult, ALU.add))
                    settle()
                    step(dve.tensor_scalar(half, arg, -0.5, None, ALU.mult))
                    step(dve.tensor_scalar(kr.bitcast(I32), arg.bitcast(I32), -0.5, ROOT_GUESS, ALU.mult, ALU.add))
                    settle()
                    for it in range(3):
                        step(dve.tensor_tensor(t, kr, kr, ALU.mult))
                        settle()
                        step(dve.tensor_tensor(t, t, half, ALU.mult))
                        settle()
                        last = dve.scalar_tensor_tensor(out=kr, in0=t, scalar=1.5, in1=kr, op0=ALU.add, op1=ALU.mult)
                        if it < 2:
                            step(last)
                            settle()
                    last.then_inc(S["krs_ready"], 1)

                def add(i):
                    dve.wait_ge(S["out_ps"], 4 * NT + i + 1)
                    dve.tensor_tensor(X[:, i, :], X[:, i, :], psum[:, i % 2, 0:D], ALU.add).then_inc(S["x_added"], 1)
                    spread(5, i)

                angles(0)
                tables(0)
                for b in range(B):
                    def rope(n):
                        g = 12 * b + n
                        if n < KT:
                            cos, sin, ss = KCOS[:, n, :], KSIN[:, n, :], k_ss[:, KVH * n:KVH * (n + 1)]
                        else:
                            c, t = divmod(n - KT, 2)
                            cos, sin = QCOS[:, t, :], QSIN[:, t, :]
                            ss = q_ss.rearrange("p (h m) -> p h m", m=2)[:, 4 * c:4 * c + 4, t]
                        raw = RAW5[:, n % 2, :].rearrange("p (h i f) -> p h i f", h=4, i=2)
                        dve.wait_ge(S["kq_copied"], g + 1)
                        if g >= 2:
                            dve.wait_ge(S["tr_ps"], g - 1)
                        dve.tensor_tensor(RT1[:, n % 2, :].rearrange("p (h d) -> p h d", h=4),
                                          RAW5[:, n % 2, :].rearrange("p (h d) -> p h d", h=4),
                                          cos.unsqueeze(1).broadcast_to([P, 4, HD]), ALU.mult).then_inc(S["t1_ready"], 1)
                        if g >= 1:
                            dve.wait_ge(S["rope_sum"], g)
                        for i in range(2):
                            dve.tensor_tensor(RT2.rearrange("p (h i f) -> p h i f", h=4, i=2)[:, :, i, :], raw[:, :, 1 - i, :],
                                              sin[:, i * ROPE:(i + 1) * ROPE].unsqueeze(1).broadcast_to([P, 4, ROPE]),
                                              ALU.mult).then_inc(S["t1_ready"], 1)
                        dve.wait_ge(S["sq_ready"], g + 1)
                        dve.tensor_reduce(ss, SQ5.rearrange("p (h d) -> p h d", h=4), AX.X, ALU.add).then_inc(S["ss_ready"], 1)

                    for n in range(EARLY):
                        rope(n)
                        if n < KT:
                            root_of_keys(n, 12 * b + n)
                        if b > 0 and n in (1, 3):
                            add(2 * (b - 1) + n // 2)

                    def bias(h):
                        if h % 4 == 0:
                            dve.wait_ge(S["qrs_ready"], 4 * b + h // 4 + 1)
                        for m in range(2):
                            g = 2 * (QH * b + h) + m
                            dve.wait_ge(S["s5_ps"], g + 1)
                            step(dve.tensor_reduce(nmax[:, g % 4:g % 4 + 1], bank(2 * (h % 2) + m), AX.X, ALU.max, negate=True))
                            settle()
                            dve.tensor_tensor(nbias[:, g % 4:g % 4 + 1], nmax[:, g % 4:g % 4 + 1],
                                              q_rs[:, 2 * h + m:2 * h + m + 1], ALU.mult).then_inc(S["nb5_ready"], 1)

                    def inverse(h):
                        for m in range(2):
                            g = 2 * (QH * b + h) + m
                            dve.wait_ge(S["p5_ready"], g + 1)
                            step(dve.reciprocal(rinv[:, g % 4:g % 4 + 1], psums[:, g % 4:g % 4 + 1]))
                            settle()
                            dve.tensor_scalar(PR5[:, h % 2, m, :], PR5[:, h % 2, m, :], rinv[:, g % 4:g % 4 + 1], None, ALU.mult)\
                               .then_inc(S["p5_normed"], 1)

                    bias(0)
                    for h in range(QH):
                        if h + 1 < QH:
                            bias(h + 1)
                        inverse(h)
                        if h >= 1:
                            dve.wait_ge(S["at_ps"], QH * b + h)
                            dve.tensor_copy(AT[:, h - 1, :], psum[:, 6, 0:L]).then_inc(S["at_copied"], 1)
                        if h % 2 == 1 and EARLY + h // 2 < 12:
                            rope(EARLY + h // 2)
                        if h == 3 and b > 0:
                            apply_norm(5, 2 * b - 2)
                            apply_norm(5, 2 * b - 1)
                        if h == 11 and b + 1 < B:
                            angles(b + 1)
                        if h == 14 and b + 1 < B:
                            tables(b + 1)
                    dve.wait_ge(S["at_ps"], QH * (b + 1))
                    dve.tensor_copy(AT[:, QH - 1, :], psum[:, 6, 0:L]).then_inc(S["at_copied"], 1)
                add(NT - 2)
                add(NT - 1)
                apply_norm(5, NT - 2)
                apply_norm(5, NT - 1)

            def experts():
                dve.wait_ge(S["aff_exp"], 1)
                step(dve.tensor_scalar(AFF, AFF, 1.0, None, ALU.add))
                step(dve.memset(CMB, 0.0))
                settle()
                step(dve.reciprocal(AFF, AFF))
                settle()
                for i in range(NT):
                    step(dve.max(TOP[:, i, :], AFF[:, i, :]))
                settle()
                for i in range(NT):
                    step(dve.max_index(top_i[:, i, :], TOP[:, i, :], AFF[:, i, :]))
                step(dve.tensor_tensor(PS, TOP[:, :, 0], TOP[:, :, 1], ALU.add))
                settle()
                step(dve.tensor_copy(TOPI, top_i[:, :, :]))
                step(dve.reciprocal(PS, PS))
                settle()
                step(dve.tensor_tensor(PW, TOP[:, :, 0:2], PS.unsqueeze(2).broadcast_to([P, NT, 2]), ALU.mult))
                settle()
                steps_e = moe["iota"].unsqueeze(1).broadcast_to([P, NT, NE])
                for c in range(2):
                    step(dve.tensor_tensor(PICK, steps_e, TOPI[:, :, c:c + 1].broadcast_to([P, NT, NE]), ALU.is_equal))
                    settle()
                    step(dve.tensor_tensor(PICK, PICK, PW[:, :, c:c + 1].broadcast_to([P, NT, NE]), ALU.mult))
                    settle()
                    step(dve.tensor_tensor(CMB[:, :, 0:NE], CMB[:, :, 0:NE], PICK, ALU.add))
                    settle()
                dve.memset(CMB[:, :, NE:NX], 1.0).then_inc(S["cmb_ready"], 1)
                dve.wait_ge(S["ct_copied"], 1)
                three_parts(CT[0:2 * NS, :], ct3, ct_rest, ct_mid, 2 * NS, S["ct_ready"])
                for g in range(2 * NX):
                    n, e = g // NX, g % NX
                    dve.wait_ge(S["ge_ps"], 2 * g + 2)
                    dve.wait_ge(S["ge_ready"], g + 1)
                    if g >= 2:
                        dve.wait_ge(S["ye_used"], g - 1)
                    y = dve.scalar_tensor_tensor(out=YE[:, g % 2, :], in0=bank(4 + g % 2), scalar=moe["b1"][:, e:e + 1],
                                                 in1=GE[:, g % 2, :], op0=ALU.add, op1=ALU.mult)
                    if e < NE:
                        step(y)
                        settle()
                        dve.wait_ge(S["cb_ps"], n * NE + e + 1)
                        dve.tensor_tensor(YE[:, g % 2, :], YE[:, g % 2, :], bank(6 + g % 2), ALU.mult).then_inc(S["ye_ready"], 1)
                    else:
                        y.then_inc(S["ye_ready"], 1)
                add_norm(6, lambda i: psum[:, 6 + i % 2, 0:D], twice=True)

            dve.memset(one, 1.0).then_inc(consts_ready, 1)
            for k, program in enumerate([mamba, cross1, swiglu, ttt, cross2, experts]):
                if LAST > k:
                    program()

        @block.gpsimd
        def _(pool):
            pool_steps = [0]

            def step(instruction):
                pool_steps[0] += 1
                instruction.then_inc(S["pool_step"], 1)
                pool.wait_ge(S["pool_step"], pool_steps[0])

            def inverse_root(out, v, scale, shift, at_least=False):
                n = v.shape[-1]
                arg, half, t = root_tmp[:, 0:n], root_tmp[:, 16:16 + n], root_tmp[:, 32:32 + n]
                step(pool.tensor_scalar(arg, v, scale, shift, ALU.mult, ALU.max if at_least else ALU.add))
                pool_steps[0] += 1
                pool.tensor_scalar(half, arg, -0.5, None, ALU.mult).then_inc(S["pool_step"], 1)
                step(pool.tensor_scalar(out.bitcast(I32), arg.bitcast(I32), -0.5, ROOT_GUESS, ALU.mult, ALU.add))
                for it in range(3):
                    if n == 1:
                        step(pool.tensor_scalar(t, out, out, half, ALU.mult, ALU.mult))
                        last = pool.tensor_scalar(out, t, 1.5, out, ALU.add, ALU.mult)
                        if it < 2:
                            step(last)
                        continue
                    step(pool.tensor_tensor(t, out, out, ALU.mult))
                    step(pool.tensor_tensor(t, t, half, ALU.mult))
                    step(pool.tensor_scalar(t, t, 1.5, None, ALU.add))
                    last = pool.tensor_tensor(out, out, t, ALU.mult)
                    if it < 2:
                        step(last)
                return last

            def rstd_tile(k, i):
                pool.wait_ge(S["ln_var"], NT * (k - 1) + i + 1)
                inverse_root(rstd[:, i:i + 1], mv[:, i, 1:2], 1.0, LN_EPS).then_inc(S["ln_rstd"], 1)

            def rstd_tiles(k):
                for i in range(NT):
                    rstd_tile(k, i)

            def ttt():
                pool.wait_ge(S["ss4_ready"], 1)
                step(inverse_root(rstd, sum_sq, 1.0, TINY, at_least=True))
                step(pool.tensor_tensor(std, rstd, sum_sq, ALU.mult))
                pool.tensor_scalar(std, std, L2_EPS, None, ALU.add).then_inc(S["norm4_ready"], 1)
                pool.wait_ge(S["o4_var"], TH * NT)
                inverse_root(rstd, mv[:, :, 1], 1.0, TTT_EPS).then_inc(S["o4_rstd"], 1)

            def mamba():
                for it in range(NBLK * NS):
                    pool.wait_ge(S["h_ready"], it + 1)
                    pool.wait_ge(S["c_copied"], it + 1)
                    if it >= 3:
                        pool.wait_ge(S["hc_summed"], it - 2)
                    pool.tensor_tensor(HC[:, it % 3, :], H[:, it % 2, :], CB[:, it % 2, :], ALU.mult)\
                        .then_inc(S["hc_ready"], 1)

            def swiglu():
                for i in range(3):
                    rstd_tile(2, i)
                pool.wait_ge(ld["ffn"], 16)
                for n, (src, dst) in enumerate(((fw2, fw2b), (fw2b, fw2), (fw2, fw2b))):
                    h = 1 << n
                    a = src.rearrange("p (g i h) d -> p g i (h d)", i=2, h=h)
                    o = dst.rearrange("p (g i h) d -> p g i (h d)", i=2, h=h)
                    if n > 0:
                        pool.wait_ge(S["bf_ready"], 2 * n)
                    pool.tensor_tensor(o[:, :, 0, :], a[:, :, 0, :], a[:, :, 1, :], ALU.add).then_inc(S["bf_ready"], 1)
                    pool.tensor_tensor(o[:, :, 1, :], a[:, :, 0, :], a[:, :, 1, :], ALU.subtract).then_inc(S["bf_ready"], 1)
                    rstd_tile(2, 3 + n)
                for i in range(6, NT):
                    rstd_tile(2, i)

            def cross2():
                for b in range(B):
                    for n in range(12):
                        g = 12 * b + n
                        pool.wait_ge(S["t1_ready"], 3 * (g + 1))
                        pool.tensor_tensor(RT1[:, n % 2, :], RT1[:, n % 2, :], RT2, ALU.add).then_inc(S["rope_sum"], 1)
                        if n < KT:
                            pool.wait_ge(S["krs_ready"], KT * b + n + 1)
                            pool.wait_ge(S["rope_sum"], g + 1)
                            k3 = RT1[:, n % 2, :].rearrange("p (h d) -> p h d", h=KVH)
                            pool.tensor_tensor(k3, k3, k_rs[:, KVH * n:KVH * (n + 1)].unsqueeze(2).broadcast_to([P, KVH, HD]),
                                               ALU.mult).then_inc(S["k_scaled"], 1)
                        elif n % 2 == 1:
                            c = (n - KT) // 2
                            pool.wait_ge(S["ss_ready"], g + 1)
                            q = q_rs[:, 8 * c:8 * c + 8]
                            step(inverse_root(q, q_ss[:, 8 * c:8 * c + 8], 1.0 / HD, RMS_EPS))
                            pool.tensor_scalar(q, q, ASCALE, None, ALU.mult).then_inc(S["qrs_ready"], 1)
                        if n == EARLY - 1 and b > 0:
                            rstd_tile(5, 2 * b - 2)
                            rstd_tile(5, 2 * b - 1)
                rstd_tile(5, NT - 2)
                rstd_tile(5, NT - 1)

            mamba()
            rstd_tiles(1)
            if LAST == 2:
                rstd_tiles(2)
            if LAST >= 3:
                swiglu()
                rstd_tiles(3)
            if LAST >= 4:
                ttt()
                rstd_tiles(4)
            if LAST >= 5:
                cross2()
            if LAST >= 6:
                rstd_tiles(6)


def _columns(w):
    k, n = w.shape
    return w.reshape(k // P, P, n).transpose(1, 0, 2)


def _rows(v):
    return np.broadcast_to(v.reshape(1, -1), (P, v.size))


def _hadamard(n):
    h = np.ones((1, 1), np.float32)
    while h.shape[0] < n:
        h = np.concatenate([np.concatenate([h, h], 1), np.concatenate([h, -h], 1)], 0)
    return h


def _few(w):
    return np.concatenate([w, np.zeros((P - w.shape[0], w.shape[1]), w.dtype)], 0)


def kernel(**inputs):
    import concourse.bacc as _bacc
    from concourse.bass_utils import run_bass_kernel_spmd as _run

    a = {k: np.asarray(v) for k, v in inputs.items()}
    x2 = a["x"].reshape(T, D)
    ctx2 = a["ctx_2048"].reshape(T, D)
    qkv = a["L1_attn_W_qkv"].reshape(D, TH, 3, THD)
    experts = {k: np.concatenate([a["L1_ffn_r" + k], a["L1_ffn_s" + k]], 0) for k in ("g", "gb", "w1", "b1", "w2", "b2")}
    swap = lambda v: np.concatenate([v[ROPE:], v[:ROPE]])
    eye = np.eye(P, dtype=np.float32)
    parts = {
        "xT": _columns(x2.T), "w_inT": _columns(a["L0_attn_W_in"].T),
        "w_xT": _columns(a["L0_attn_W_x"].T), "w_dtT": a["L0_attn_W_dt"].T, "w_outT": _columns(a["L0_attn_W_out"].T),
        "conv_w": _columns(a["L0_attn_conv_w"]), "conv_b": _columns(a["L0_attn_conv_b"][:, None]),
        "b_dt": _columns(a["L0_attn_b_dt"][:, None]), "a_log": _columns(a["L0_attn_A_log"]),
        "d_skip": _columns(a["L0_attn_D"][:, None]), "ident": eye,
        "sel3": _few(np.tile(eye[:2 * NS, :2 * NS], (3, 1))),
        "x": _columns(x2), "ctx": _columns(ctx2), "ctxT": _columns(ctx2.T),
        "w_qs": _columns(np.concatenate([qkv[:, :, 0].reshape(D, TH * THD), a["L1_attn_W_s"]], 1)),
        "w0T": a["L1_attn_w0"].transpose(2, 0, 1), "w2T": a["L1_attn_w2"].transpose(2, 0, 1),
        "w1T": a["L1_attn_w1"].transpose(2, 0, 1), "w_oT": _columns(a["L1_attn_W_o"]),
        "ln_g": _rows(a["L1_attn_ln_g"]), "ln_b": _rows(a["L1_attn_ln_b"]), "b_s": _rows(a["L1_attn_b_s"]),
        "ffn1T": _columns(a["L0_ffn_W1"].T), "ffn3T": _columns(a["L0_ffn_W3"].T),
        "ffn2T": _columns(a["L0_ffn_W2"].T), "hadamard": _hadamard(P),
        "wqT": _columns(a["L1_xattn_Wq"].T), "wkT": _columns(a["L1_xattn_Wk"].T),
        "wvT": _columns(a["L1_xattn_Wv"].T), "woT": _columns(a["L1_xattn_Wo"].T),
        "q_w": _rows(a["L1_xattn_q_norm_w"]), "q_w_swap": _rows(swap(a["L1_xattn_q_norm_w"])),
        "k_w": _rows(a["L1_xattn_k_norm_w"]), "k_w_swap": _rows(swap(a["L1_xattn_k_norm_w"])),
        "inv_freq": _rows((1.0 / np.float32(10000.0) ** (np.arange(0, HD, 2, dtype=np.float32) / HD)).astype(np.float32)),
        "wa": _columns(a["L1_ffn_wa"]),
        "wg": experts["g"].reshape(NX, KD, P, EF).transpose(2, 0, 1, 3),
        "w1": experts["w1"].reshape(NX, KD, P, EF).transpose(2, 0, 1, 3),
        "w2": experts["w2"].transpose(1, 0, 2), "gb": experts["gb"].T, "b1": experts["b1"].T,
        "b2": _few(experts["b2"]), "iota": _rows(np.arange(NE, dtype=np.float32)),
    }
    arrays = {}
    for name, inside in PACKS.items():
        arrays["in_" + name] = np.ascontiguousarray(
            np.concatenate([parts[p].reshape(P, w) for p, w in inside], 1))
    pos = np.concatenate([a["pos_BxS2"].reshape(B, CTXT_TILES, P), a["itok_BxS_4096_4607"].reshape(B, CTXT_TILES, P)], 1)
    arrays["in_pos"] = np.ascontiguousarray(pos.reshape(B * KT, P).T.astype(np.int32))

    nc = _bacc.Bacc("TRN2", target_bir_lowering=False, num_devices=1)
    aps = {k[3:]: nc.dram_tensor(k, v.shape, mybir.dt.from_np(v.dtype), kind="ExternalInput").ap()
           for k, v in arrays.items()}
    out = nc.dram_tensor("out_x", (T, D), F32, kind="ExternalOutput").ap()
    decoder(nc, aps, out)
    r = _run(nc, [arrays], core_ids=[0])
    return r.results[0]["out_x"].reshape(B, L, D)
```

```python
from contextlib import ExitStack

import numpy as np

import concourse.bass as bass
from concourse import mybir

F32 = mybir.dt.float32
BF16 = mybir.dt.bfloat16
I32 = mybir.dt.int32
U32 = mybir.dt.uint32
ALU = mybir.AluOpType
ACT = mybir.ActivationFunctionType
AX = mybir.AxisListType

P = 128
B, L, D = 4, 256, 256
T = B * L
NT = T // P
KD = D // P
LN_EPS = 1e-5

DI, NS, DCONV, RANK = 512, 16, 4, 128
NBLK = DI // P
PAD = L + DCONV - 1
STEP0_DT = 1e28

XH = 8
XR = L // XH
XSCALE = float(1.0 / np.sqrt(np.float32(XR)))

FF = 1024
NFB = FF // P

TH, THD = 2, 128
TTT_EPS = 1e-6
L2_EPS = 1e-5
TINY = 1e-30

QH, KVH, HD = 16, 4, 128
CTXT_TILES = L // P
KT = 2 * CTXT_TILES
ROPE = HD // 2
ASCALE = float(np.float32(1.0 / np.sqrt(HD).astype(np.float32)))
RMS_EPS = 1e-6
EARLY = KT + 3

NE, NSH, EF = 16, 2, 128
NX = NE + NSH
EXPERTS = list(range(NE, NX)) + list(range(NE))



class Region:

    def __init__(self, start):
        self.at = start

    def take(self, words):
        start, self.at = self.at, self.at + words
        return start, words


PACKS = {
    "in": [("xT", KD * T), ("w_inT", KD * 2 * DI)],
    "mamba": [("w_xT", NBLK * (RANK + 2 * NS)), ("w_dtT", DI), ("w_outT", NBLK * D), ("conv_w", NBLK * DCONV),
              ("conv_b", NBLK), ("b_dt", NBLK), ("a_log", NBLK * NS), ("d_skip", NBLK),
              ("sel3", 2 * NS)],
    "ident": [("ident", P)],
    "x": [("x", NT * D)],
    "ctx": [("ctx", NT * D), ("ctxT", KD * T)],
    "ttt": [("w_qs", KD * (TH * THD + TH)), ("w0T", TH * P), ("w2T", TH * P), ("w1T", TH * P), ("w_oT", TH * D),
            ("ln_g", P), ("ln_b", P), ("b_s", TH)],
    "ffn": [("ffn1T", KD * FF), ("ffn3T", KD * FF), ("ffn2T", NFB * D), ("hadamard", P)],
    "attn": [("wqT", KD * QH * HD), ("wkT", KD * KVH * HD), ("wvT", KD * KVH * HD), ("woT", QH * D),
             ("q_w", HD), ("q_w_swap", HD), ("k_w", HD), ("k_w_swap", HD), ("inv_freq", ROPE)],
    "moe": [("wa", KD * NE), ("wg", NX * KD * EF), ("w1", NX * KD * EF), ("w2", NX * D), ("gb", NX), ("b1", NX),
            ("b2", D), ("iota", NE)],
}


def pack_words(name):
    return sum(w for _, w in PACKS[name])

ROUND = float(1.5 * 2 ** 23)
TURN_HI = 6.28125
TURN_LO = float(2 * np.pi - TURN_HI)
PI_MAX = 3.1415925

ROOT_GUESS = float(0x5f3759df)

DT_BANKS = (4, 6, 0, 4)

SEMAPHORES = """
    x_added x_ready stored xt_ready xt_ps xs_copied proj_ps u_ready z_ready dbl_ps dt_ps dtr_copied spz_ready
    hc_ready y_used hc_summed bc_ready dbu_ready b_ps c_copied c_ps y_ready out_ps p_ready sc_ps p_normed
    pt_copied pt_ps bf_ready had_ps w2h_ready hid_ready up_ps q4_copied q4_ps q4_ready qt4_copied qt4_ps gh_ready
    f4_ps o4_copied o4_ps o4_normed ot4_copied ot4_ps tr_copied kq_copied at_copied kq_ps pt5_copied rope_sum
    k_scaled tr_ps v_ps p5_ready v_copied s5_ps p5_normed pt5_ps at_ps aff_ps ye_ready ge_ps ct_ready cb_ps
    ft_copied aff_exp ye_used cmb_ready ct_ps conv_done a_exp spe_used act_step spl_ready a_ready dt_ready h_ready
    da_ready nbias_ready ang_ready sines_ready sg_ready s4_copied sg4_ready s4_raw s4_ready ss_ready nb5_ready
    ge_ready ct_copied dve_step ln_var ln_rstd pos_ready o4_scaled t1_ready krs_ready qrs_ready pool_step
"""



def decoder(nc: bass.Bass, dram, out: bass.AP):
    with ExitStack() as ctx:
        def sem(name):
            return ctx.enter_context(nc.semaphore(name))

        kept = Region(0)
        X_ = kept.take(NT * D)
        XT_ = kept.take(KD * T)
        CTX_ = kept.take(NT * D)
        CTXT_ = kept.take(KD * T)
        IDENT_ = kept.take(P)
        SMALL_ = kept.take(512)
        TTTW_ = kept.take(pack_words("ttt"))
        wa_start = kept.at
        wb_start = wa_start + max(pack_words("moe"), pack_words("ffn") + NFB * D)
        c_start = wb_start + pack_words("attn")
        total = c_start + 17248

        arena = ctx.enter_context(nc.sbuf_tensor("arena", [P, total], F32))
        psum = ctx.enter_context(nc.psum_tensor("psum", [P, 8, 512], F32))
        pos_i = ctx.enter_context(nc.sbuf_tensor("pos_i", [P, B * KT], I32))
        top_i = ctx.enter_context(nc.sbuf_tensor("top_i", [P, NT, 8], U32))

        def view(span, parts=P):
            return arena[0:parts, span[0]:span[0] + span[1]]

        def views(name, start):
            r = Region(start)
            got = {part: view(r.take(w)) for part, w in PACKS[name]}
            return got, arena[:, start:start + pack_words(name)]

        def bank(b, n=1):
            return psum[:, b:b + n, :].rearrange("p b n -> p (b n)")

        X = view(X_).rearrange("p (t d) -> p t d", t=NT)
        XT = view(XT_).rearrange("p (k t) -> p k t", k=KD)
        ident = view(IDENT_)
        CTX = view(CTX_).rearrange("p (t d) -> p t d", t=NT)
        CTXT = view(CTXT_).rearrange("p (k t) -> p k t", k=KD)
        small = Region(SMALL_[0])

        def tiny(words):
            return view(small.take(words))

        one = tiny(1)
        stats = tiny(TH * NT * 6).rearrange("p (t s) -> p t s", s=6)
        mv = tiny(TH * NT * 2).rearrange("p (t s) -> p t s", s=2)
        std = tiny(TH * NT)
        rstd = tiny(TH * NT)
        root_tmp = tiny(3 * TH * NT)
        root_v = tiny(3 * 8)
        nmax = tiny(16)
        nbias = tiny(16)
        psums = tiny(16)
        rinv = tiny(16)
        a_neg = tiny(NBLK * NS)
        sum_sq = tiny(TH * NT)
        s_raw = tiny(NT * TH)
        s_gate = tiny(NT * TH)
        pos_f = tiny(B * KT)
        sel3 = tiny(NS).bitcast(BF16)
        assert small.at <= SMALL_[0] + SMALL_[1], small.at - SMALL_[0]

        ttt_w, ttt_all = views("ttt", TTTW_[0])

        wa = Region(wa_start)
        XS = view(wa.take(NBLK * B * PAD)).rearrange("p (m b t) -> p m b t", m=NBLK, b=B)
        YS = view((wa_start, NBLK * T)).rearrange("p (m t) -> p m t", m=NBLK)
        ZS = view(wa.take(NBLK * T)).rearrange("p (m t) -> p m t", m=NBLK)
        U = view(wa.take(NBLK * T)).rearrange("p (m t) -> p m t", m=NBLK)
        assert wa.at <= wb_start
        wb = Region(wb_start)
        DT = view(wb.take(NBLK * T)).rearrange("p (m t) -> p m t", m=NBLK)
        DTU = view(wb.take(NBLK * T)).rearrange("p (m t) -> p m t", m=NBLK)
        DTR = view(wb.take(T))
        assert wb.at <= c_start
        c1 = Region(c_start)
        w_inT = view(c1.take(KD * 2 * DI)).rearrange("p (k n) -> p k n", k=KD)
        mb_start = c1.take(pack_words("mamba"))[0]
        mb, mb_all = views("mamba", mb_start)
        loop = Region(c1.take(9 * T)[0])
        DBU = view(loop.take(2 * T)).rearrange("p (i t) -> p i t", i=2)
        H = view(loop.take(2 * T)).rearrange("p (i t) -> p i t", i=2)
        HC = view(loop.take(3 * T)).rearrange("p (i t) -> p i t", i=3)
        CB = view(loop.take(2 * T)).rearrange("p (i t) -> p i t", i=2)
        SPZ = view((wa_start, NBLK * T)).rearrange("p (m t) -> p m t", m=NBLK)
        SPE = view(c1.take(T))
        bc3 = view(c1.take(T // 2)).bitcast(BF16)
        bc_rest = view(c1.take(T))
        bc_mid = view(c1.take(T // 2)).bitcast(BF16)
        assert c1.at <= total, (c1.at, total)

        w_xT = mb["w_xT"].rearrange("p (m n) -> p m n", m=NBLK)
        w_outT = mb["w_outT"].rearrange("p (m n) -> p m n", m=NBLK)
        conv_w = mb["conv_w"].rearrange("p (m k) -> p m k", m=NBLK)
        a_log = mb["a_log"]
        N3 = 3 * 2 * NS

        c2 = Region(c_start)
        PR = view(c2.take(2 * 8 * L)).rearrange("p (i j m n) -> p i j m n", i=2, j=4, m=2)
        PT = view(c2.take(2 * 2 * L)).rearrange("p (i n m) -> p i n m", i=2, n=2)
        ffn, ffn_all = views("ffn", wa_start)
        fw1 = ffn["ffn1T"].rearrange("p (k n) -> p k n", k=KD)
        fw3 = ffn["ffn3T"].rearrange("p (k n) -> p k n", k=KD)
        fw2 = ffn["ffn2T"].rearrange("p (k d) -> p k d", k=NFB)
        fw2b = view((wa_start + pack_words("ffn"), NFB * D)).rearrange("p (k d) -> p k d", k=NFB)
        c3 = Region(c_start)
        HID = view(c3.take(NFB * T)).rearrange("p (k t) -> p k t", k=NFB)
        SG = view(c3.take(2 * 512)).rearrange("p (i t) -> p i t", i=2)
        w_qs = ttt_w["w_qs"].rearrange("p (k n) -> p k n", k=KD)
        w0T = ttt_w["w0T"].rearrange("p (h n) -> p h n", h=TH)
        w2T = ttt_w["w2T"].rearrange("p (h n) -> p h n", h=TH)
        w1T = ttt_w["w1T"].rearrange("p (h n) -> p h n", h=TH)
        w_oT = ttt_w["w_oT"].rearrange("p (h n) -> p h n", h=TH)
        c4 = Region(c_start)
        Q4 = view(c4.take(NT * D)).rearrange("p (t d) -> p t d", t=NT)
        SQ4 = view(c4.take(NT * D)).rearrange("p (t d) -> p t d", t=NT)
        QT4 = view(c4.take(TH * T)).rearrange("p (h b t) -> p h b t", h=TH, b=B)
        GH = view(c4.take(TH * T)).rearrange("p (h t) -> p h t", h=TH)
        SG4 = view(c4.take(2 * 512)).rearrange("p (i t) -> p i t", i=2)
        O4 = view(c4.take(NT * D)).rearrange("p (t d) -> p t d", t=NT)
        OT4 = view(c4.take(TH * T)).rearrange("p (h t) -> p h t", h=TH)
        assert c4.at <= total
        attn, attn_all = views("attn", wb_start)
        wqT = attn["wqT"].rearrange("p (k n) -> p k n", k=KD)
        wkT = attn["wkT"].rearrange("p (k n) -> p k n", k=KD)
        wvT = attn["wvT"].rearrange("p (k n) -> p k n", k=KD)
        woT = attn["woT"].rearrange("p (h n) -> p h n", h=QH)
        tab = Region(CTX_[0])
        KCOS = view(tab.take(KT * HD)).rearrange("p (t d) -> p t d", t=KT)
        KSIN = view(tab.take(KT * HD)).rearrange("p (t d) -> p t d", t=KT)
        QCOS = view(tab.take(2 * HD)).rearrange("p (t d) -> p t d", t=2)
        QSIN = view(tab.take(2 * HD)).rearrange("p (t d) -> p t d", t=2)
        assert tab.at <= CTX_[0] + CTX_[1]
        tmp5 = Region(TTTW_[0])
        RT1 = view(tmp5.take(2 * 512)).rearrange("p (i n) -> p i n", i=2)
        RAW5 = view(tmp5.take(2 * 512)).rearrange("p (i n) -> p i n", i=2)
        assert tmp5.at <= TTTW_[0] + TTTW_[1]
        c5 = Region(c_start)
        KTR = view(c5.take(KVH * 2 * L)).rearrange("p (h t) -> p h t", h=KVH)
        V5 = view(c5.take(KT * KVH * HD)).rearrange("p (t n) -> p t n", t=KT)
        QTR = view(c5.take(QH * L)).rearrange("p (h t) -> p h t", h=QH)
        AT = view(c5.take(QH * L)).rearrange("p (h t) -> p h t", h=QH)
        PR5 = view(c5.take(2 * 2 * 512)).rearrange("p (i m n) -> p i m n", i=2, m=2)
        PT5 = view(c5.take(KT * L)).rearrange("p (k n) -> p k n", k=KT)
        RT2 = view(c5.take(512))
        SQ5 = view(c5.take(512))
        ANG = view((c5.at - 1024, 3 * KT * ROPE)).rearrange("p (i t f) -> p i t f", i=3, t=KT)
        SINES = view(c5.take(3 * KT * ROPE)).rearrange("p (i t f) -> p i t f", i=3, t=KT)
        q_ss = view(c5.take(2 * QH))
        q_rs = view(c5.take(2 * QH))
        k_ss = view(c5.take(KT * KVH))
        k_rs = view(c5.take(KT * KVH))
        assert c5.at <= total, (c5.at, total)
        moe, moe_all = views("moe", wa_start)
        wa6 = moe["wa"].rearrange("p (k e) -> p k e", k=KD)
        wg6 = moe["wg"].rearrange("p (e k f) -> p e k f", e=NX, k=KD)
        w16 = moe["w1"].rearrange("p (e k f) -> p e k f", e=NX, k=KD)
        w26 = moe["w2"].rearrange("p (e d) -> p e d", e=NX)
        c6 = Region(c_start)
        AFF = view(c6.take(NT * NE)).rearrange("p (t e) -> p t e", t=NT)
        TOP = view(c6.take(NT * 8)).rearrange("p (t e) -> p t e", t=NT)
        TOPI = view(c6.take(NT * 8)).rearrange("p (t e) -> p t e", t=NT)
        PW = view(c6.take(NT * 2)).rearrange("p (t e) -> p t e", t=NT)
        PS = view(c6.take(NT))
        CMB = view(c6.take(NT * 2 * NS)).rearrange("p (t e) -> p t e", t=NT)
        PICK = view(c6.take(NT * NE)).rearrange("p (t e) -> p t e", t=NT)
        CT = view(c6.take(T))
        ct_rest = view(c6.take(T))
        ct_mid = view(c6.take(T // 2)).bitcast(BF16)
        ct3 = view(c6.take(T // 2)).bitcast(BF16)
        GE = view(c6.take(2 * 512)).rearrange("p (i t) -> p i t", i=2)
        YE = view(c6.take(2 * 512)).rearrange("p (i t) -> p i t", i=2)
        FT = view(c6.take(KD * T)).rearrange("p (k t) -> p k t", k=KD)
        assert c6.at <= total

        ld = {n: sem("loaded_" + n) for n in list(PACKS) + ["pos", "in_x1", "in_z"]}
        consts_ready = sem("consts_ready")
        S = {n: sem(n) for n in SEMAPHORES.split()}

        block = ctx.enter_context(nc.Block())

        @block.sync
        def _(sp):
            x_in = dram["in"][:, 0:KD * T].rearrange("p (k t) -> p k t", k=KD)
            w_in = dram["in"][:, KD * T:].rearrange("p (k n) -> p k n", k=KD)
            sp.dma_start(XT[:, :, 0:512], x_in[:, :, 0:512]).then_inc(ld["in"], 16)
            sp.dma_start(w_inT[:, :, 0:DI], w_in[:, :, 0:DI]).then_inc(ld["in"], 16)
            sp.dma_start(XT[:, :, 512:], x_in[:, :, 512:]).then_inc(ld["in_x1"], 16)
            sp.dma_start(w_inT[:, :, DI:], w_in[:, :, DI:]).then_inc(ld["in_z"], 16)
            sp.dma_start(mb_all, dram["mamba"]).then_inc(ld["mamba"], 16)
            sp.dma_start(ident, dram["ident"]).then_inc(ld["ident"], 16)
            sp.dma_start(arena[:, X_[0]:X_[0] + X_[1]], dram["x"]).then_inc(ld["x"], 16)
            sp.dma_start(arena[:, CTX_[0]:CTX_[0] + 2 * CTX_[1]], dram["ctx"]).then_inc(ld["ctx"], 16)
            sp.dma_start(ttt_all, dram["ttt"]).then_inc(ld["ttt"], 16)
            sp.dma_start(pos_i[:, :], dram["pos"]).then_inc(ld["pos"], 16)
            sp.wait_ge(S["x_added"], NT)
            sp.dma_start(ffn_all, dram["ffn"]).then_inc(ld["ffn"], 16)
            sp.dma_start(attn_all, dram["attn"]).then_inc(ld["attn"], 16)
            sp.wait_ge(S["x_added"], 3 * NT)
            sp.dma_start(moe_all, dram["moe"]).then_inc(ld["moe"], 16)
            for i in range(NT):
                sp.wait_ge(S["x_ready"], 5 * NT + i + 1)
                sp.dma_start(out[i * P:(i + 1) * P, :], X[:, i, :]).then_inc(S["stored"], 16)
            sp.wait_ge(S["stored"], 16 * NT)

        @block.tensor
        def _(pe):
            def turn_x(k, tiles=range(NT), bank0=6):
                for i in tiles:
                    pe.wait_ge(S["x_ready"], NT * (k - 1) + i + 1)
                    if i >= 2:
                        pe.wait_ge(S["xt_ready"], NT * (k - 2) + i - 1)
                    for f in range(KD):
                        mm = pe.transpose(psum[:, bank0 + i % 2, f * P:(f + 1) * P], X[:, i, f * P:(f + 1) * P], ident)
                    mm.then_inc(S["xt_ps"], 1)
                pe.wait_ge(S["xt_ready"], NT * (k - 2) + i + 1)

            def mamba():
                pe.wait_ge(ld["in"], 32)
                for g in range(16):
                    m, n = g // 2, g % 2
                    if g == 1:
                        pe.wait_ge(ld["in_x1"], 16)
                    if g == 8:
                        pe.wait_ge(ld["in_z"], 16)
                    if g >= 8:
                        pe.wait_ge(S["xs_copied"], g - 7)
                    for k in range(KD):
                        mm = pe.matmul(bank(g % 8), w_inT[:, k, m * P:(m + 1) * P], XT[:, k, n * 512:(n + 1) * 512],
                                       start=(k == 0), stop=(k == KD - 1))
                    mm.then_inc(S["proj_ps"], 1)
                pe.wait_ge(ld["mamba"], 16)
                pe.wait_ge(S["u_ready"], NBLK)
                pe.wait_ge(S["z_ready"], 4)
                def project_u(g):
                    n = g % 2
                    lo, width = (0, RANK) if g < 2 else (RANK, 2 * NS)
                    for m in range(NBLK):
                        mm = pe.matmul(psum[0:width, g, :], w_xT[:, m, lo:lo + width], U[:, m, n * 512:(n + 1) * 512],
                                       start=(m == 0), stop=(m == NBLK - 1))
                    mm.then_inc(S["dbl_ps"], 1)

                def project_dt(m):
                    for n in range(2):
                        mm = pe.matmul(bank(DT_BANKS[m] + n), mb["w_dtT"][:, m * P:(m + 1) * P],
                                       DTR[:, n * 512:(n + 1) * 512], start=True, stop=True)
                    mm.then_inc(S["dt_ps"], 1)

                for g in range(3):
                    project_u(g)
                pe.wait_ge(S["dtr_copied"], 1)
                pe.wait_ge(S["z_ready"], 8)
                project_dt(0)
                project_u(3)
                project_dt(1)
                project_dt(2)
                pe.wait_ge(S["spz_ready"], 1)
                project_dt(3)
                pe.wait_ge(S["spz_ready"], NBLK)

                def sum_y(it):
                    m, s = it // NS, it % NS
                    pe.wait_ge(S["hc_ready"], it + 1)
                    if s == 0 and m > 0:
                        pe.wait_ge(S["y_used"], m)
                    for n in range(2):
                        mm = pe.matmul(bank(6 + n), ident, HC[:, it % 3, n * 512:(n + 1) * 512],
                                       start=(s == 0), stop=(s == NS - 1))
                    mm.then_inc(S["hc_summed"], 1)

                pe.wait_ge(S["bc_ready"], 2)
                pe.wait_ge(ld["ident"], 16)
                for it in range(NBLK * NS):
                    s = it % NS
                    if it > 0:
                        pe.wait_ge(S["dbu_ready"], it)
                    for n in range(2):
                        mm = pe.matmul(bank(n), sel3[0:N3, s:s + 1].broadcast_to([N3, P]), bc3[0:N3, n * 512:(n + 1) * 512],
                                       start=True, stop=True)
                    mm.then_inc(S["b_ps"], 1)
                    if it > 0:
                        pe.wait_ge(S["c_copied"], it)
                    for n in range(2):
                        mm = pe.matmul(bank(2 + n), sel3[0:N3, NS + s:NS + s + 1].broadcast_to([N3, P]),
                                       bc3[0:N3, n * 512:(n + 1) * 512], start=True, stop=True)
                    mm.then_inc(S["c_ps"], 1)
                    if it > 1:
                        sum_y(it - 2)
                sum_y(NBLK * NS - 2)
                sum_y(NBLK * NS - 1)
                pe.wait_ge(S["y_ready"], NBLK)
                for i in range(NT):
                    if i >= 2:
                        pe.wait_ge(S["x_added"], i - 1)
                    for m in range(NBLK):
                        mm = pe.matmul(psum[:, 4 + i % 2, 0:D], YS[:, m, i * P:(i + 1) * P], w_outT[:, m, :],
                                       start=(m == 0), stop=(m == NBLK - 1))
                    mm.then_inc(S["out_ps"], 1)

            def cross1():
                pe.wait_ge(ld["ctx"], 16)

                def scores(u):
                    i, r = u // 2, u % 2
                    pe.wait_ge(S["x_ready"], i + 1)
                    if u >= 2:
                        pe.wait_ge(S["p_ready"], 4 * (u - 1))
                    for mt in range(2):
                        for j in (2 * r, 2 * r + 1):
                            rows = slice(XR * j, XR * (j + 1))
                            mm = pe.matmul(psum[:, 2 * r + j % 2, mt * L:(mt + 1) * L], X[rows, i, mt * P:(mt + 1) * P],
                                           CTX[rows, i, :], start=True, stop=True)
                    mm.then_inc(S["sc_ps"], 1)

                def turn_p(u, odd):
                    i, j = u // 2, 2 * (u % 2) + odd
                    pe.wait_ge(S["p_normed"], 4 * u + 2 * odd + 2)
                    if u >= 1:
                        pe.wait_ge(S["pt_copied"], 2 * u - 1 + odd)
                    for mt in range(2):
                        for nb in range(2):
                            mm = pe.transpose(psum[:, 4 + odd, nb * L + mt * P:nb * L + (mt + 1) * P],
                                              PR[:, i % 2, j, mt, nb * P:(nb + 1) * P], ident)
                    mm.then_inc(S["pt_ps"], 1)

                def weigh(u, odd):
                    i, j = u // 2, 2 * (u % 2) + odd
                    pe.wait_ge(S["pt_copied"], 2 * u + odd + 1)
                    if j == 0 and i >= 2:
                        pe.wait_ge(S["x_added"], NT + i - 1)
                    col = i * P + XR * j
                    for nb in range(2):
                        mm = pe.matmul(psum[XR * j:XR * (j + 1), 6 + i % 2, 0:D], CTXT[:, nb, col:col + XR],
                                       PT[:, odd, nb, :], start=(nb == 0), stop=(nb == 1))
                    if j == 3:
                        mm.then_inc(S["out_ps"], 1)

                scores(0)
                scores(1)
                pe.wait_ge(S["x_added"], NT)
                for u in range(2 * NT):
                    turn_p(u, 0)
                    turn_p(u, 1)
                    if u + 2 < 2 * NT:
                        scores(u + 2)
                    weigh(u, 0)
                    weigh(u, 1)
                pe.wait_ge(S["x_added"], 2 * NT)

            def swiglu():
                pe.wait_ge(ld["ffn"], 16)
                pe.wait_ge(S["bf_ready"], 6)
                for g in range(4):
                    if g == 0:
                        pe.wait_ge(S["p_ready"], 8 * NT)
                    mm = pe.matmul(bank(g), ffn["hadamard"], fw2b[:, 2 * g:2 * g + 2, :].rearrange("p k d -> p (k d)"),
                                   start=True, stop=True)
                    mm.then_inc(S["had_ps"], 1)
                turn_x(2, range(NT - 1))
                pe.wait_ge(S["w2h_ready"], 4)
                for g in range(2 * NFB):
                    n, h = g // NFB, g % NFB
                    if g == 2:
                        turn_x(2, [NT - 1])
                    if g >= 2:
                        pe.wait_ge(S["hid_ready"], g - 1)
                    for w, b0 in ((fw1, 0), (fw3, 2)):
                        for k in range(KD):
                            mm = pe.matmul(bank(b0 + g % 2), w[:, k, h * P:(h + 1) * P], XT[:, k, n * 512:(n + 1) * 512],
                                           start=(k == 0), stop=(k == KD - 1))
                        mm.then_inc(S["up_ps"], 1)
                for i in range(NT):
                    pe.wait_ge(S["hid_ready"], NFB * (1 + i // 4))
                    if i >= 2:
                        pe.wait_ge(S["x_added"], 2 * NT + i - 1)
                    for h in range(NFB):
                        mm = pe.matmul(psum[:, 4 + i % 2, 0:D], HID[:, h, i * P:(i + 1) * P], fw2[:, h, :],
                                       start=(h == 0), stop=(h == NFB - 1))
                    mm.then_inc(S["out_ps"], 1)

            def ttt():
                pe.wait_ge(ld["ttt"], 16)
                turn_x(3, range(NT - 1))
                for i in range(NT):
                    if i == NT - 1:
                        turn_x(3, [i])
                    if i >= 4:
                        pe.wait_ge(S["q4_copied"], i - 3)
                    for k in range(KD):
                        mm = pe.matmul(psum[:, i % 4, 0:D + TH], XT[:, k, i * P:(i + 1) * P], w_qs[:, k, :],
                                       start=(k == 0), stop=(k == KD - 1))
                    mm.then_inc(S["q4_ps"], 1)

                def turn_q(n):
                    pe.wait_ge(S["q4_ready"], n + 1)
                    for i in range(4 * n, 4 * n + 4):
                        if i >= 2:
                            pe.wait_ge(S["qt4_copied"], i - 1)
                        for h in range(TH):
                            mm = pe.transpose(psum[:, 4 + i % 2, h * P:(h + 1) * P], Q4[:, i, h * P:(h + 1) * P], ident)
                        mm.then_inc(S["qt4_ps"], 1)

                def fast_weights(n):
                    pe.wait_ge(S["qt4_copied"], 4 * n + 4)
                    if n == 0:
                        pe.wait_ge(S["q4_copied"], NT)
                    for h in range(TH):
                        g = 2 * n + h
                        if g >= 2:
                            pe.wait_ge(S["gh_ready"], g - 1)
                        rhs = QT4[:, h, 2 * n:2 * n + 2, :].rearrange("p b t -> p (b t)")
                        pe.matmul(bank(g % 2), w0T[:, h, :], rhs, start=True, stop=True).then_inc(S["f4_ps"], 1)
                        pe.matmul(bank(2 + g % 2), w2T[:, h, :], rhs, start=True, stop=True).then_inc(S["f4_ps"], 1)

                def down(n):
                    pe.wait_ge(S["gh_ready"], 2 * n + 2)
                    if n == 0:
                        pe.wait_ge(S["qt4_copied"], NT)
                    for i in range(4 * n, 4 * n + 4):
                        if i >= 2:
                            pe.wait_ge(S["o4_copied"], i - 1)
                        for h in range(TH):
                            mm = pe.matmul(psum[:, 4 + i % 2, h * P:(h + 1) * P], GH[:, h, i * P:(i + 1) * P], w1T[:, h, :],
                                           start=True, stop=True)
                        mm.then_inc(S["o4_ps"], 1)

                def turn_o(i):
                    pe.wait_ge(S["o4_normed"], i + 1)
                    if i >= 2:
                        pe.wait_ge(S["ot4_copied"], i - 1)
                    for h in range(TH):
                        mm = pe.transpose(psum[:, 6 + i % 2, h * P:(h + 1) * P], O4[:, i, h * P:(h + 1) * P], ident)
                    mm.then_inc(S["ot4_ps"], 1)

                def output(i):
                    pe.wait_ge(S["ot4_copied"], i + 1)
                    if i >= 4:
                        pe.wait_ge(S["x_added"], 3 * NT + i - 3)
                    for h in range(TH):
                        mm = pe.matmul(psum[:, i % 4, 0:D], OT4[:, h, i * P:(i + 1) * P], w_oT[:, h, :],
                                       start=(h == 0), stop=(h == TH - 1))
                    mm.then_inc(S["out_ps"], 1)

                turn_q(0)
                fast_weights(0)
                turn_q(1)
                down(0)
                fast_weights(1)
                down(1)
                for i in range(NT):
                    turn_o(i)
                    if i >= 1:
                        output(i - 1)
                output(NT - 1)

            def cross2():
                pe.wait_ge(ld["attn"], 16)
                pe.wait_ge(S["ot4_copied"], NT)
                for b in range(B + 1):
                    def project(n):
                        g = 12 * b + n
                        c, t = divmod(n - KT, 2)
                        src, i, w, lo = (XT, b * 2 + t, wqT, c * 512) if n >= KT else \
                            (CTXT, b * 2 + n, wkT, 0) if n < CTXT_TILES else (XT, b * 2 + n - CTXT_TILES, wkT, 0)
                        if n >= EARLY:
                            pe.wait_ge(S["tr_copied"], g)
                        elif g >= 2:
                            pe.wait_ge(S["kq_copied"], g - 1)
                        if n == 0 and b > 0:
                            pe.wait_ge(S["at_copied"], QH * b)
                        if n == 1 and b > 0:
                            pe.wait_ge(S["tr_copied"], g - 1)
                        for k in range(KD):
                            mm = pe.matmul(bank(7 if n >= EARLY else 6 + n % 2), src[:, k, i * P:(i + 1) * P],
                                           w[:, k, lo:lo + 512], start=(k == 0), stop=(k == KD - 1))
                        mm.then_inc(S["kq_ps"], 1)

                    def turn(n):
                        g = 12 * b + n
                        if n == 0 and b > 0:
                            pe.wait_ge(S["pt5_copied"], 2 * QH * b)
                        pe.wait_ge(S["rope_sum"], g + 1)
                        if g >= 2:
                            pe.wait_ge(S["tr_copied"], g - 1)
                        if n < KT:
                            pe.wait_ge(S["k_scaled"], KT * b + n + 1)
                        for h in range(4):
                            mm = pe.transpose(psum[:, 7 if n >= EARLY else 4 + n % 2, h * P:(h + 1) * P],
                                              RT1[:, n % 2, h * P:(h + 1) * P], ident)
                        mm.then_inc(S["tr_ps"], 1)

                    def values(t, wait):
                        src, i = (CTXT, b * 2 + t) if t < CTXT_TILES else (XT, b * 2 + t - CTXT_TILES)
                        if wait:
                            pe.wait_ge(S["x_added"], 4 * NT + 2 * b)
                        for k in range(KD):
                            mm = pe.matmul(bank(t), src[:, k, i * P:(i + 1) * P], wvT[:, k, :],
                                           start=(k == 0), stop=(k == KD - 1))
                        mm.then_inc(S["v_ps"], 1)

                    def output(m):
                        if m == 0:
                            pe.wait_ge(S["at_copied"], QH * b)
                            pe.wait_ge(S["p5_ready"], 2 * QH * b)
                        for h in range(QH):
                            mm = pe.matmul(psum[:, m, 0:D], AT[:, h, m * P:(m + 1) * P], woT[:, h, :],
                                           start=(h == 0), stop=(h == QH - 1))
                        mm.then_inc(S["out_ps"], 1)

                    if b == B:
                        output(0)
                        output(1)
                        break
                    project(0)
                    project(1)
                    if b > 0:
                        output(0)
                    else:
                        turn_x(4, bank0=4)
                    turn(0)
                    project(2)
                    turn(1)
                    project(3)
                    if b > 0:
                        output(1)
                    turn(2)
                    project(4)
                    turn(3)
                    project(5)
                    values(2, False)
                    values(3, False)
                    turn(4)
                    project(6)
                    values(0, b > 0)
                    values(1, b > 0)
                    turn(5)
                    turn(6)

                    def scores(h):
                        g = QH * b + h
                        if h == 0:
                            pe.wait_ge(S["v_copied"], KT * (b + 1))
                        if h % 4 == 0:
                            pe.wait_ge(S["tr_copied"], 12 * b + 6 + h // 2)
                        if h >= 2:
                            pe.wait_ge(S["p5_ready"], 2 * (g - 1))
                        for m in range(2):
                            mm = pe.matmul(bank(2 * (h % 2) + m), QTR[:, h, m * P:(m + 1) * P], KTR[:, h // 4, :],
                                           start=True, stop=True)
                            mm.then_inc(S["s5_ps"], 1)

                    def turn_p(h):
                        if h == 0:
                            pe.wait_ge(S["tr_copied"], 12 * b + EARLY)
                        for m in range(2):
                            g = 2 * (QH * b + h) + m
                            pe.wait_ge(S["p5_normed"], g + 1)
                            if g >= 2:
                                pe.wait_ge(S["pt5_copied"], g - 1)
                            for kt in range(KT):
                                mm = pe.transpose(psum[:, 4 + m, kt * P:(kt + 1) * P],
                                                  PR5[:, h % 2, m, kt * P:(kt + 1) * P], ident)
                            mm.then_inc(S["pt5_ps"], 1)

                    def weigh(h):
                        g = QH * b + h
                        pe.wait_ge(S["pt5_copied"], 2 * (g + 1))
                        if h >= 1:
                            pe.wait_ge(S["at_copied"], g)
                        for kt in range(KT):
                            mm = pe.matmul(psum[:, 6, 0:L], V5[:, kt, (h // 4) * HD:(h // 4 + 1) * HD],
                                           PT5[:, kt, :], start=(kt == 0), stop=(kt == KT - 1))
                        mm.then_inc(S["at_ps"], 1)

                    scores(0)
                    scores(1)
                    for h in range(QH):
                        turn_p(h)
                        if h + 2 < QH:
                            scores(h + 2)
                        weigh(h)
                        n = EARLY + h // 2
                        if n < 12:
                            if h % 2 == 0:
                                project(n)
                            else:
                                turn(n)

            def experts():
                pe.wait_ge(ld["moe"], 16)
                turn_x(5, range(NT - 1))
                for i in range(NT):
                    if i == NT - 1:
                        turn_x(5, [i])
                    for k in range(KD):
                        mm = pe.matmul(psum[:, 0, i * NE:(i + 1) * NE], XT[:, k, i * P:(i + 1) * P], wa6[:, k, :],
                                       start=(k == 0), stop=(k == KD - 1))
                mm.then_inc(S["aff_ps"], 1)

                def up(g):
                    n, e = g // NX, EXPERTS[g % NX]
                    if g >= 2:
                        pe.wait_ge(S["ye_ready"], g - 1)
                    for w, b0 in ((wg6, 2), (w16, 4)):
                        for k in range(KD):
                            mm = pe.matmul(bank(b0 + g % 2), w[:, e, k, :], XT[:, k, n * 512:(n + 1) * 512],
                                           start=(k == 0), stop=(k == KD - 1))
                        mm.then_inc(S["ge_ps"], 1)
                    if g == NSH:
                        pe.wait_ge(S["ct_ready"], 2)
                    if e < NE:
                        pe.matmul(bank(6 + g % 2), sel3[0:N3, e:e + 1].broadcast_to([N3, P]),
                                  ct3[0:N3, n * 512:(n + 1) * 512], start=True, stop=True).then_inc(S["cb_ps"], 1)

                def down(g):
                    n, e = g // NX, EXPERTS[g % NX]
                    if g == NX:
                        pe.wait_ge(S["ft_copied"], 2)
                    if g == 0:
                        pe.wait_ge(S["aff_exp"], 1)
                    pe.wait_ge(S["ye_ready"], g + 1)
                    for f in range(KD):
                        mm = pe.matmul(bank(f), w26[:, e, f * P:(f + 1) * P], YE[:, g % 2, :],
                                       start=(g % NX == 0), stop=False)
                        if g % NX == NX - 1:
                            mm = pe.matmul(bank(f), moe["b2"][0:NX, f * P:(f + 1) * P], CT[0:NX, n * 512:(n + 1) * 512],
                                           start=False, stop=True)
                    mm.then_inc(S["ye_used"], 1)

                def turn_weights():
                    pe.wait_ge(S["cmb_ready"], 1)
                    for i in range(NT):
                        mm = pe.transpose(psum[0:2 * NS, 6 + i // 4, (i % 4) * P:(i % 4 + 1) * P], CMB[:, i, :], ident)
                    mm.then_inc(S["ct_ps"], 1)

                for g in range(2 * NX):
                    up(g)
                    if g == NSH - 1:
                        turn_weights()
                    if g > 0:
                        down(g - 1)
                down(2 * NX - 1)
                for i in range(NT):
                    pe.wait_ge(S["ft_copied"], 4)
                    if i >= 2:
                        pe.wait_ge(S["x_added"], 5 * NT + i - 1)
                    for f in range(KD):
                        mm = pe.transpose(psum[:, 6 + i % 2, f * P:(f + 1) * P], FT[:, f, i * P:(i + 1) * P], ident)
                    mm.then_inc(S["out_ps"], 1)

            for program in (mamba, cross1, swiglu, ttt, cross2, experts):
                program()

        @block.scalar
        def _(act):
            def turn_x(k, tiles=range(NT), bank0=6):
                for i in tiles:
                    act.wait_ge(S["xt_ps"], NT * (k - 2) + i + 1)
                    act.activation(XT[:, :, i * P:(i + 1) * P],
                                   psum[:, bank0 + i % 2, 0:D].rearrange("p (f t) -> p f t", f=KD),
                                   ACT.Copy).then_inc(S["xt_ready"], 1)

            def mamba():
                for g in range(8):
                    m, n = g // 2, g % 2
                    act.wait_ge(S["proj_ps"], g + 1)
                    act.activation(XS[:, m, 2 * n:2 * n + 2, DCONV - 1:], bank(g).rearrange("p (b t) -> p b t", b=2),
                                   ACT.Copy).then_inc(S["xs_copied"], 1)

                def gate(g):
                    m, n = g // 2 - 4, g % 2
                    act.wait_ge(S["proj_ps"], g + 1)
                    act.activation(ZS[:, m, n * 512:(n + 1) * 512], bank(g % 8), ACT.Silu).then_inc(S["z_ready"], 1)

                def inner(m):
                    act.wait_ge(S["conv_done"], m + 1)
                    act.activation(U[:, m, :], U[:, m, :], ACT.Silu).then_inc(S["u_ready"], 1)

                inner(0)
                inner(1)
                gate(8)
                gate(9)
                inner(2)
                for g in range(10, 14):
                    gate(g)
                inner(3)
                gate(14)
                gate(15)
                act.wait_ge(S["dbl_ps"], 2)
                act.activation(DTR, bank(0, 2), ACT.Copy).then_inc(S["dtr_copied"], 1)
                act.activation(a_neg, a_log, ACT.Exp).then_inc(S["a_exp"], 1)
                def softplus(m):
                    act.wait_ge(S["spz_ready"], m + 1)
                    if m > 0:
                        act.wait_ge(S["spe_used"], m)
                    act.activation(SPE, SPZ[:, m, :], ACT.Abs).then_inc(S["act_step"], 1)
                    act.wait_ge(S["act_step"], 2 * m + 1)
                    act.activation(SPE, SPE, ACT.Exp, scale=-1.0).then_inc(S["act_step"], 1)
                    act.wait_ge(S["act_step"], 2 * m + 2)
                    act.activation(DTU[:, m, :], SPE, ACT.Ln, bias=one).then_inc(S["spl_ready"], 1)

                def softplus_in(m):
                    act.wait_ge(S["dt_ps"], m + 1)
                    act.activation(SPZ[:, m, :], bank(DT_BANKS[m], 2), ACT.Identity, bias=mb["b_dt"][:, m:m + 1])\
                       .then_inc(S["spz_ready"], 1)

                softplus_in(0)
                softplus(0)
                for m in range(1, NBLK):
                    softplus_in(m)
                act.wait_ge(S["a_ready"], 1)
                act.wait_ge(S["spz_ready"], NBLK)
                for it in range(NBLK * NS):
                    m, s = it // NS, it % NS
                    if s == 0:
                        act.wait_ge(S["dt_ready"], m + 1)
                    if it > 0:
                        act.wait_ge(S["h_ready"], it)
                    act.activation(bank(4, 2), DT[:, m, :], ACT.Exp, scale=a_neg[:, it:it + 1]).then_inc(S["da_ready"], 1)
                    act.wait_ge(S["c_ps"], it + 1)
                    if it >= 2:
                        act.wait_ge(S["hc_ready"], it - 1)
                    act.activation(CB[:, it % 2, :], bank(2, 2), ACT.Copy).then_inc(S["c_copied"], 1)
                    if s == 2 and m + 1 < NBLK:
                        softplus(m + 1)

            def cross1():
                def exps(u, odd):
                    i, j = u // 2, 2 * (u % 2) + odd
                    act.wait_ge(S["nbias_ready"], 2 * u + odd + 1)
                    if u >= 4:
                        act.wait_ge(S["pt_ps"], 2 * (u - 3))
                    for mt in range(2):
                        c = 8 * (i % 2) + 2 * j + mt
                        act.activation(PR[:, i % 2, j, mt, :], psum[:, j, mt * L:(mt + 1) * L], ACT.Exp,
                                       bias=nbias[:, c:c + 1], scale=XSCALE,
                                       accum_out=psums[:, c:c + 1]).then_inc(S["p_ready"], 1)

                exps(0, 0)
                exps(0, 1)
                for u in range(2 * NT):
                    for odd in range(2):
                        if u + 1 < 2 * NT:
                            exps(u + 1, odd)
                        act.wait_ge(S["pt_ps"], 2 * u + odd + 1)
                        act.activation(PT[:, odd, :, :].rearrange("p n m -> p (n m)"), bank(4 + odd), ACT.Copy)\
                           .then_inc(S["pt_copied"], 1)

            def sines(b):
                act.wait_ge(S["ang_ready"], 2 * (b + 1))
                act.activation(SINES[:, 0, :, :], ANG[:, 0, :, :], ACT.Sin, scale=-1.0).then_inc(S["sines_ready"], 1)
                act.activation(SINES[:, 1, :, :], ANG[:, 0, :, :], ACT.Sin).then_inc(S["sines_ready"], 1)
                act.activation(SINES[:, 2, :, :], ANG[:, 2, :, :], ACT.Sin).then_inc(S["sines_ready"], 1)

            def swiglu():
                for g in range(4):
                    act.wait_ge(S["had_ps"], g + 1)
                    act.activation(fw2[:, 2 * g:2 * g + 2, :].rearrange("p k d -> p (k d)"), bank(g), ACT.Copy,
                                   scale=float(FF) ** -0.5).then_inc(S["w2h_ready"], 1)
                turn_x(2, range(NT - 1))
                for g in range(2 * NFB):
                    if g == 2:
                        turn_x(2, [NT - 1])
                    act.wait_ge(S["up_ps"], 2 * g + 1)
                    if g >= 2:
                        act.wait_ge(S["hid_ready"], g - 1)
                    act.activation(SG[:, g % 2, :], bank(g % 2), ACT.Silu).then_inc(S["sg_ready"], 1)
                    if g == 8:
                        sines(0)

            def ttt():
                turn_x(3, range(NT - 1))
                for i in range(NT):
                    if i == NT - 1:
                        turn_x(3, [i])
                    act.wait_ge(S["q4_ps"], i + 1)
                    act.activation(s_raw[:, TH * i:TH * (i + 1)], psum[:, i % 4, D:D + TH], ACT.Copy).then_inc(S["s4_copied"], 1)
                    act.activation(Q4[:, i, :], psum[:, i % 4, 0:D], ACT.Silu).then_inc(S["q4_copied"], 1)

                def queries(n):
                    for i in range(4 * n, 4 * n + 4):
                        b, h = i // 2, i % 2
                        act.wait_ge(S["qt4_ps"], i + 1)
                        act.activation(QT4[:, h, b, :].rearrange("p (t h) -> p h t", h=TH),
                                       psum[:, 4 + i % 2, 0:D].rearrange("p (h t) -> p h t", h=TH), ACT.Copy)\
                           .then_inc(S["qt4_copied"], 1)

                def gates(n):
                    for g in (2 * n, 2 * n + 1):
                        act.wait_ge(S["f4_ps"], 2 * g + 1)
                        if g >= 2:
                            act.wait_ge(S["gh_ready"], g - 1)
                        act.activation(SG4[:, g % 2, :], bank(g % 2), ACT.Silu).then_inc(S["sg4_ready"], 1)

                def outputs(n):
                    for i in range(4 * n, 4 * n + 4):
                        act.wait_ge(S["o4_ps"], i + 1)
                        act.activation(O4[:, i, :], psum[:, 4 + i % 2, 0:D], ACT.Copy).then_inc(S["o4_copied"], 1)

                queries(0)
                gates(0)
                act.wait_ge(S["s4_raw"], 1)
                act.activation(s_gate, s_raw, ACT.Silu).then_inc(S["s4_ready"], 1)
                queries(1)
                outputs(0)
                gates(1)
                outputs(1)
                for i in range(NT):
                    act.wait_ge(S["ot4_ps"], i + 1)
                    act.activation(OT4[:, :, i * P:(i + 1) * P], psum[:, 6 + i % 2, 0:D].rearrange("p (h t) -> p h t", h=TH),
                                   ACT.Copy).then_inc(S["ot4_copied"], 1)

            def cross2():
                for b in range(B):
                    def project(n):
                        g = 12 * b + n
                        act.wait_ge(S["kq_ps"], g + 1)
                        if g >= 2:
                            act.wait_ge(S["rope_sum"], g - 1)
                        act.activation(RAW5[:, n % 2, :], bank(7 if n >= EARLY else 6 + n % 2), ACT.Copy)\
                           .then_inc(S["kq_copied"], 1)

                    def square(n):
                        g = 12 * b + n
                        act.wait_ge(S["kq_copied"], g + 1)
                        if g >= 1:
                            act.wait_ge(S["ss_ready"], 4 * g)
                        if n < KT:
                            sums = k_ss[:, KVH * n:KVH * (n + 1)]
                        else:
                            c, t = divmod(n - KT, 2)
                            sums = q_ss.rearrange("p (h m) -> p h m", m=2)[:, 4 * c:4 * c + 4, t]
                        for h in range(4):
                            act.activation(SQ5[:, h * HD:(h + 1) * HD], RAW5[:, n % 2, h * HD:(h + 1) * HD], ACT.Square,
                                           accum_out=sums[:, h:h + 1]).then_inc(S["ss_ready"], 1)

                    def turn(n):
                        act.wait_ge(S["tr_ps"], 12 * b + n + 1)
                        got = bank(7 if n >= EARLY else 4 + n % 2).rearrange("p (h t) -> p h t", h=4)
                        if n < KT:
                            dst = KTR[:, :, n * P:(n + 1) * P]
                        else:
                            c, t = divmod(n - KT, 2)
                            dst = QTR[:, 4 * c:4 * c + 4, t * P:(t + 1) * P]
                        act.activation(dst, got, ACT.Copy).then_inc(S["tr_copied"], 1)

                    def values(n, t):
                        act.wait_ge(S["v_ps"], KT * b + n + 1)
                        act.activation(V5[:, t, :], bank(t), ACT.Copy).then_inc(S["v_copied"], 1)

                    if b == 0:
                        act.wait_ge(S["out_ps"], 4 * NT)
                    project(0)
                    square(0)
                    for n in range(1, EARLY):
                        project(n)
                        square(n)
                        if b == 0 and n == 1:
                            turn_x(4, bank0=4)
                        if n == 6:
                            values(0, 2)
                            values(1, 3)
                        turn(n - 1)
                    values(2, 0)
                    values(3, 1)
                    turn(EARLY - 1)

                    def probs(h):
                        for m in range(2):
                            g = 2 * (QH * b + h) + m
                            act.wait_ge(S["nb5_ready"], g + 1)
                            if h >= 2:
                                act.wait_ge(S["pt5_ps"], g - 3)
                            c = 2 * h + m
                            act.activation(PR5[:, h % 2, m, :], bank(2 * (h % 2) + m), ACT.Exp, scale=q_rs[:, c:c + 1],
                                           bias=nbias[:, g % 4:g % 4 + 1],
                                           accum_out=psums[:, g % 4:g % 4 + 1]).then_inc(S["p5_ready"], 1)

                    probs(0)
                    for h in range(QH):
                        n = EARLY + (h - 1) // 2
                        if h >= 1 and n < 12:
                            if h % 2 == 1:
                                project(n)
                            else:
                                turn(n)
                        for m in range(2):
                            g = 2 * (QH * b + h) + m
                            act.wait_ge(S["pt5_ps"], g + 1)
                            act.activation(PT5[:, :, m * P:(m + 1) * P], bank(4 + m).rearrange("p (k n) -> p k n", k=KT),
                                           ACT.Copy).then_inc(S["pt5_copied"], 1)
                        if h + 1 < QH:
                            probs(h + 1)
                        if h % 2 == 1 and n < 12:
                            square(n)
                        if h == 12 and b + 1 < B:
                            sines(b + 1)

            def experts():
                turn_x(5)
                act.wait_ge(S["aff_ps"], 1)
                act.activation(AFF.rearrange("p t e -> p (t e)"), psum[:, 0, 0:NT * NE], ACT.Exp, scale=-1.0)\
                   .then_inc(S["aff_exp"], 1)
                for g in range(2 * NX):
                    e = EXPERTS[g % NX]
                    act.wait_ge(S["ge_ps"], 2 * g + 1)
                    if g >= 2:
                        act.wait_ge(S["ye_ready"], g - 1)
                    act.activation(GE[:, g % 2, :], bank(2 + g % 2), ACT.Gelu, bias=moe["gb"][:, e:e + 1])\
                       .then_inc(S["ge_ready"], 1)
                    if g == NSH - 1:
                        act.wait_ge(S["ct_ps"], 1)
                        act.activation(CT[0:2 * NS, :], psum[0:2 * NS, 6:8, :].rearrange("p b n -> p (b n)"), ACT.Copy)\
                           .then_inc(S["ct_copied"], 1)
                    if g % NX == NX - 1:
                        n = g // NX
                        act.wait_ge(S["ye_used"], g + 1)
                        for f in range(KD):
                            act.activation(FT[:, f, n * 512:(n + 1) * 512], bank(f), ACT.Copy).then_inc(S["ft_copied"], 1)

            act.wait_ge(consts_ready, 1)
            for program in (mamba, cross1, swiglu, ttt, cross2, experts):
                program()

        @block.vector
        def _(dve):
            steps = [0]

            def step(instruction):
                steps[0] += 1
                instruction.then_inc(S["dve_step"], 1)

            def settle():
                dve.wait_ge(S["dve_step"], steps[0])

            def spread(k, i):
                dve.wait_ge(S["x_added"], NT * (k - 1) + i + 1)
                step(dve.bn_stats(stats[:, i, :], X[:, i, :]))
                settle()
                dve.bn_aggr(mv[:, i, :], stats[:, i, :]).then_inc(S["ln_var"], 1)

            def apply_norm(k, i):
                dve.wait_ge(S["ln_rstd"], NT * (k - 1) + i + 1)
                dve.tensor_scalar(X[:, i, :], X[:, i, :], mv[:, i, 0:1], rstd[:, i:i + 1], ALU.subtract, ALU.mult)\
                   .then_inc(S["x_ready"], 1)

            def add_norm(k, source, twice=False, leave_last=False, groups=((0, 4), (4, 7), (7, 8))):
                for lo, hi in groups:
                    for i in range(lo, hi + 1):
                        if i < hi:
                            dve.wait_ge(S["out_ps"], NT * (k - 1) + i + 1)
                            dve.scalar_tensor_tensor(out=X[:, i, :], in0=X[:, i, :], scalar=2.0 if twice else 1.0,
                                                     in1=source(i), op0=ALU.mult, op1=ALU.add).then_inc(S["x_added"], 1)
                        if i > lo:
                            dve.wait_ge(S["x_added"], NT * (k - 1) + i)
                            step(dve.bn_stats(stats[:, i - 1, :], X[:, i - 1, :]))
                    settle()
                    for i in range(lo, hi):
                        step(dve.bn_aggr(mv[:, i, :], stats[:, i, :]))
                    settle()
                    inverse_root(rstd[:, lo:hi], mv[:, lo:hi, 1], 1.0, LN_EPS).then_inc(S["ln_rstd"], hi - lo)
                    for i in range(lo, hi):
                        if not (leave_last and i == NT - 1):
                            apply_norm(k, i)

            def inverse_root(out, v, scale, shift):
                n = v.shape[-1]
                arg, half, t = root_v[:, 0:n], root_v[:, 8:8 + n], root_v[:, 16:16 + n]
                step(dve.tensor_scalar(arg, v, scale, shift, ALU.mult, ALU.add))
                settle()
                step(dve.tensor_scalar(half, arg, -0.5, None, ALU.mult))
                step(dve.tensor_scalar(out.bitcast(I32), arg.bitcast(I32), -0.5, ROOT_GUESS, ALU.mult, ALU.add))
                settle()
                for it in range(3):
                    if n == 1:
                        step(dve.tensor_scalar(t, out, out, half, ALU.mult, ALU.mult))
                        settle()
                        last = dve.tensor_scalar(out, t, 1.5, out, ALU.add, ALU.mult)
                        if it < 2:
                            step(last)
                            settle()
                        continue
                    step(dve.tensor_tensor(t, out, out, ALU.mult))
                    settle()
                    step(dve.tensor_tensor(t, t, half, ALU.mult))
                    settle()
                    last = dve.scalar_tensor_tensor(out=out, in0=t, scalar=1.5, in1=out, op0=ALU.add, op1=ALU.mult)
                    if it < 2:
                        step(last)
                        settle()
                return last

            def tables(b):
                def table(dst_cos, dst_sin, w, w_swap, t0, n):
                    halves = "p t (i f) -> p t i f"
                    step(dve.tensor_tensor(dst_cos.rearrange(halves, i=2),
                                           w.rearrange("p (i f) -> p i f", i=2).unsqueeze(1).broadcast_to([P, n, 2, ROPE]),
                                           SINES[:, 2, t0:t0 + n, :].unsqueeze(2).broadcast_to([P, n, 2, ROPE]), ALU.mult))
                    step(dve.tensor_tensor(dst_sin.rearrange(halves, i=2),
                                           w_swap.rearrange("p (i f) -> p i f", i=2).unsqueeze(1).broadcast_to([P, n, 2, ROPE]),
                                           SINES[:, 0:2, t0:t0 + n, :].rearrange("p i t f -> p t i f"), ALU.mult))

                dve.wait_ge(S["sines_ready"], 3 * (b + 1))
                table(KCOS, KSIN, attn["k_w"], attn["k_w_swap"], 0, KT)
                table(QCOS, QSIN, attn["q_w"], attn["q_w_swap"], CTXT_TILES, 2)
                settle()


            def three_parts(source, out3, rest, mid, rows, ready):
                step(dve.tensor_copy(out3[0:rows, :], source))
                settle()
                step(dve.tensor_tensor(rest[0:rows, :], source, out3[0:rows, :], ALU.subtract))
                settle()
                step(dve.tensor_copy(mid[0:rows, :], rest[0:rows, :]))
                settle()
                dve.tensor_tensor(out3[64:64 + rows, :], rest[0:rows, :], mid[0:rows, :], ALU.subtract).then_inc(ready, 1)
                dve.tensor_copy(out3[32:32 + rows, :], mid[0:rows, :]).then_inc(ready, 1)

            def mamba():
                step(dve.memset(XS[:, :, :, 0:DCONV - 1], 0.0))
                dve.wait_ge(ld["mamba"], 16)
                step(dve.tensor_copy(sel3[0:N3, :], mb["sel3"][0:N3, :]))
                settle()
                for m in range(NBLK):
                    dve.wait_ge(S["xs_copied"], 2 * m + 2)
                    um = U[:, m, :].rearrange("p (b t) -> p b t", b=B)
                    step(dve.tensor_scalar(um, XS[:, m, :, 0:L], conv_w[:, m, 0:1], mb["conv_b"][:, m:m + 1], ALU.mult, ALU.add))
                    for k in range(1, DCONV):
                        settle()
                        tap = dve.scalar_tensor_tensor(out=um, in0=XS[:, m, :, k:k + L], scalar=conv_w[:, m, k:k + 1], in1=um,
                                                       op0=ALU.mult, op1=ALU.add)
                        if k < DCONV - 1:
                            step(tap)
                        else:
                            tap.then_inc(S["conv_done"], 1)
                def softplus_out(m):
                    dve.wait_ge(S["act_step"], 2 * m + 2)
                    step(dve.tensor_scalar(DT[:, m, :], SPE, 1.0, 1.0, ALU.add, ALU.subtract))
                    settle()
                    step(dve.tensor_tensor(DT[:, m, :], SPE, DT[:, m, :], ALU.subtract))
                    dve.wait_ge(S["spl_ready"], m + 1)
                    dve.scalar_tensor_tensor(out=SPZ[:, m, :], in0=SPZ[:, m, :], scalar=0.0, in1=DTU[:, m, :],
                                             op0=ALU.max, op1=ALU.add).then_inc(S["spe_used"], 1)
                    settle()
                    dve.wait_ge(S["spe_used"], m + 1)
                    step(dve.tensor_tensor(DT[:, m, :], SPZ[:, m, :], DT[:, m, :], ALU.add))
                    settle()
                    step(dve.tensor_tensor(DTU[:, m, :], DT[:, m, :], U[:, m, :], ALU.mult))
                    settle()
                    dve.memset(DT[:, m, :].rearrange("p (b t) -> p b t", b=B)[:, :, 0:1], STEP0_DT).then_inc(S["dt_ready"], 1)

                dve.wait_ge(S["a_exp"], 1)
                dve.tensor_scalar(a_neg, a_neg, -1.0, None, ALU.mult).then_inc(S["a_ready"], 1)
                dve.wait_ge(S["dbl_ps"], 4)
                three_parts(psum[0:2 * NS, 2:4, :].rearrange("p b n -> p (b n)"), bc3, bc_rest, bc_mid, 2 * NS,
                            S["bc_ready"])
                softplus_out(0)

                def input_term(it):
                    m = it // NS
                    dve.wait_ge(S["b_ps"], it + 1)
                    dve.tensor_tensor(DBU[:, it % 2, :], bank(0, 2), DTU[:, m, :], ALU.mult).then_inc(S["dbu_ready"], 1)

                def gate_y(m):
                    dve.wait_ge(S["hc_summed"], NS * (m + 1))
                    dve.scalar_tensor_tensor(out=YS[:, m, :], in0=U[:, m, :], scalar=mb["d_skip"][:, m:m + 1], in1=bank(6, 2),
                                             op0=ALU.mult, op1=ALU.add).then_inc(S["y_used"], 1)
                    dve.wait_ge(S["y_used"], m + 1)
                    dve.tensor_tensor(YS[:, m, :], YS[:, m, :], ZS[:, m, :], ALU.mult).then_inc(S["y_ready"], 1)

                n_it = NBLK * NS
                input_term(0)
                for it in range(n_it):
                    dve.wait_ge(S["da_ready"], it + 1)
                    dve.wait_ge(S["dbu_ready"], it + 1)
                    if it >= 2:
                        dve.wait_ge(S["hc_ready"], it - 1)
                    dve.tensor_tensor_scan(H[:, it % 2, :], bank(4, 2), DBU[:, it % 2, :], 0.0, ALU.mult, ALU.add)\
                       .then_inc(S["h_ready"], 1)
                    if it + 1 < n_it:
                        input_term(it + 1)
                    if it >= NS and it % NS == 1:
                        gate_y(it // NS - 1)
                    if it % NS == 4 and it // NS + 1 < NBLK:
                        softplus_out(it // NS + 1)
                gate_y(NBLK - 1)
                dve.wait_ge(ld["x"], 16)
                add_norm(1, lambda i: psum[:, 4 + i % 2, 0:D], leave_last=True,
                         groups=((0, 4), (4, 8)))

            def cross1():
                def columns(u, odd):
                    c = 8 * (u // 2 % 2) + 4 * (u % 2) + 2 * odd
                    return slice(c, c + 2)

                def bias(u):
                    dve.wait_ge(S["sc_ps"], u + 1)
                    for odd in range(2):
                        step(dve.tensor_reduce(nmax[:, columns(u, odd)], psum[:, 2 * (u % 2) + odd, :]
                                               .rearrange("p (m n) -> p m n", m=2), AX.X, ALU.max, negate=True))
                        settle()
                        dve.tensor_scalar(nbias[:, columns(u, odd)], nmax[:, columns(u, odd)], XSCALE, None, ALU.mult)\
                           .then_inc(S["nbias_ready"], 1)

                def normalise(u):
                    i = u // 2
                    for odd in range(2):
                        j = 2 * (u % 2) + odd
                        c = columns(u, odd)
                        dve.wait_ge(S["p_ready"], 4 * u + 2 * odd + 2)
                        step(dve.reciprocal(rinv[:, c], psums[:, c]))
                        settle()
                        for mt in range(2):
                            p = PR[:, i % 2, j, mt, :]
                            dve.tensor_scalar(p, p, rinv[:, c.start + mt:c.start + mt + 1], None, ALU.mult)\
                               .then_inc(S["p_normed"], 1)

                def add(i):
                    dve.wait_ge(S["out_ps"], NT + i + 1)
                    dve.tensor_tensor(X[:, i, :], X[:, i, :], psum[:, 6 + i % 2, 0:D], ALU.add).then_inc(S["x_added"], 1)
                    spread(2, i)

                bias(0)
                normalise(0)
                apply_norm(1, NT - 1)
                for u in range(2 * NT):
                    if u + 1 < 2 * NT:
                        bias(u + 1)
                        normalise(u + 1)
                    if u % 2 == 0 and u >= 2:
                        add(u // 2 - 1)
                    if u % 2 == 1 and u >= 3:
                        apply_norm(2, u // 2 - 1)
                add(NT - 1)
                apply_norm(2, NT - 1)

            def swiglu():
                dve.wait_ge(ld["pos"], 16)
                dve.tensor_copy(pos_f, pos_i[:, :]).then_inc(S["pos_ready"], 1)
                for g in range(2 * NFB):
                    n, h = g // NFB, g % NFB
                    dve.wait_ge(S["up_ps"], 2 * g + 2)
                    dve.wait_ge(S["sg_ready"], g + 1)
                    dve.tensor_tensor(HID[:, h, n * 512:(n + 1) * 512], SG[:, g % 2, :], bank(2 + g % 2), ALU.mult)\
                       .then_inc(S["hid_ready"], 1)
                    if g == 12:
                        tables(0)
                add_norm(3, lambda i: psum[:, 4 + i % 2, 0:D])

            def ttt():
                heads = Q4.rearrange("p t (h d) -> p (t h) d", h=TH)
                squares = SQ4.rearrange("p t (h d) -> p (t h) d", h=TH)

                def l2_norm(n):
                    dve.wait_ge(S["q4_copied"], 4 * n + 4)
                    c = slice(8 * n, 8 * n + 8)
                    step(dve.tensor_tensor(squares[:, c, :], heads[:, c, :], heads[:, c, :], ALU.mult))
                    settle()
                    step(dve.tensor_reduce(sum_sq[:, c], squares[:, c, :], AX.X, ALU.add))
                    settle()
                    step(inverse_root(rstd[:, c], sum_sq[:, c], 1.0, TINY))
                    settle()
                    step(dve.tensor_tensor(std[:, c], rstd[:, c], sum_sq[:, c], ALU.mult))
                    settle()
                    step(dve.tensor_scalar(std[:, c], std[:, c], L2_EPS, None, ALU.add))
                    settle()
                    step(dve.reciprocal(rstd[:, c], std[:, c]))
                    settle()
                    dve.tensor_tensor(heads[:, c, :], heads[:, c, :], rstd[:, c].unsqueeze(2).broadcast_to([P, 8, THD]),
                                      ALU.mult).then_inc(S["q4_ready"], 1)

                def gate(g):
                    n, h = g // 2, g % 2
                    dve.wait_ge(S["f4_ps"], 2 * g + 2)
                    dve.wait_ge(S["sg4_ready"], g + 1)
                    dve.tensor_tensor(GH[:, h, n * 512:(n + 1) * 512], SG4[:, g % 2, :], bank(2 + g % 2), ALU.mult)\
                       .then_inc(S["gh_ready"], 1)

                def spread_o(n):
                    for i in range(4 * n, 4 * n + 4):
                        dve.wait_ge(S["o4_copied"], i + 1)
                        for h in range(TH):
                            step(dve.bn_stats(stats[:, TH * i + h, :], O4[:, i, h * THD:(h + 1) * THD]))
                    settle()
                    for j in range(8 * n, 8 * n + 8):
                        step(dve.bn_aggr(mv[:, j, :], stats[:, j, :]))

                def norm_o(n):
                    settle()
                    c = slice(8 * n, 8 * n + 8)
                    step(inverse_root(rstd[:, c], mv[:, c, 1], 1.0, TTT_EPS))
                    settle()
                    step(dve.tensor_tensor(rstd[:, c], rstd[:, c], s_gate[:, c], ALU.mult))
                    settle()
                    for j in range(8 * n, 8 * n + 8):
                        o = O4[:, j // TH, (j % TH) * THD:(j % TH + 1) * THD]
                        step(dve.tensor_scalar(o, o, mv[:, j, 0:1], rstd[:, j:j + 1], ALU.subtract, ALU.mult))
                    settle()
                    for i in range(4 * n, 4 * n + 4):
                        o = O4[:, i, :].rearrange("p (h d) -> p h d", h=TH)
                        dve.tensor_tensor(o, o, ttt_w["ln_g"].unsqueeze(1).broadcast_to([P, TH, THD]), ALU.mult)\
                           .then_inc(S["o4_scaled"], 1)

                dve.wait_ge(ld["ttt"], 16)
                l2_norm(0)
                dve.wait_ge(S["s4_copied"], NT)
                s3 = s_raw.rearrange("p (t h) -> p t h", h=TH)
                dve.tensor_tensor(s3, s3, ttt_w["b_s"].unsqueeze(1).broadcast_to([P, NT, TH]), ALU.add)\
                   .then_inc(S["s4_raw"], 1)
                l2_norm(1)
                gate(0)
                gate(1)
                spread_o(0)
                gate(2)
                gate(3)
                dve.wait_ge(S["s4_ready"], 1)
                norm_o(0)
                spread_o(1)
                norm_o(1)
                add_norm(4, lambda i: psum[:, i % 4, 0:D], leave_last=True, groups=((0, 4), (4, 8)))

            def cross2():
                def add(i):
                    dve.wait_ge(S["out_ps"], 4 * NT + i + 1)
                    dve.tensor_tensor(X[:, i, :], X[:, i, :], psum[:, i % 2, 0:D], ALU.add).then_inc(S["x_added"], 1)
                    spread(5, i)

                for b in range(B):
                    def rope(n):
                        g = 12 * b + n
                        if n < KT:
                            cos, sin = KCOS[:, n, :], KSIN[:, n, :]
                        else:
                            c, t = divmod(n - KT, 2)
                            cos, sin = QCOS[:, t, :], QSIN[:, t, :]
                        raw = RAW5[:, n % 2, :].rearrange("p (h i f) -> p h i f", h=4, i=2)
                        dve.wait_ge(S["kq_copied"], g + 1)
                        if g >= 2:
                            dve.wait_ge(S["tr_ps"], g - 1)
                        dve.tensor_tensor(RT1[:, n % 2, :].rearrange("p (h d) -> p h d", h=4),
                                          RAW5[:, n % 2, :].rearrange("p (h d) -> p h d", h=4),
                                          cos.unsqueeze(1).broadcast_to([P, 4, HD]), ALU.mult).then_inc(S["t1_ready"], 1)
                        if g >= 1:
                            dve.wait_ge(S["rope_sum"], g)
                        for i in range(2):
                            dve.tensor_tensor(RT2.rearrange("p (h i f) -> p h i f", h=4, i=2)[:, :, i, :], raw[:, :, 1 - i, :],
                                              sin[:, i * ROPE:(i + 1) * ROPE].unsqueeze(1).broadcast_to([P, 4, ROPE]),
                                              ALU.mult).then_inc(S["t1_ready"], 1)

                    for n in range(EARLY):
                        rope(n)
                        if b == 0 and n == 0:
                            apply_norm(4, NT - 1)
                        if n < KT:
                            dve.wait_ge(S["ss_ready"], 4 * (12 * b + n + 1))
                            keys = slice(KVH * n, KVH * (n + 1))
                            inverse_root(k_rs[:, keys], k_ss[:, keys], 1.0 / HD, RMS_EPS).then_inc(S["krs_ready"], 1)
                        if b > 0 and n in (1, 3):
                            add(2 * (b - 1) + n // 2)

                    def bias(h, m):
                        if h % 4 == 0 and m == 0:
                            dve.wait_ge(S["qrs_ready"], 4 * b + h // 4 + 1)
                        g = 2 * (QH * b + h) + m
                        dve.wait_ge(S["s5_ps"], g + 1)
                        step(dve.tensor_reduce(nmax[:, g % 4:g % 4 + 1], bank(2 * (h % 2) + m), AX.X, ALU.max, negate=True))
                        settle()
                        dve.tensor_tensor(nbias[:, g % 4:g % 4 + 1], nmax[:, g % 4:g % 4 + 1],
                                          q_rs[:, 2 * h + m:2 * h + m + 1], ALU.mult).then_inc(S["nb5_ready"], 1)

                    def inverse(h, m):
                        g = 2 * (QH * b + h) + m
                        dve.wait_ge(S["p5_ready"], g + 1)
                        step(dve.reciprocal(rinv[:, g % 4:g % 4 + 1], psums[:, g % 4:g % 4 + 1]))
                        settle()
                        dve.tensor_scalar(PR5[:, h % 2, m, :], PR5[:, h % 2, m, :], rinv[:, g % 4:g % 4 + 1], None, ALU.mult)\
                           .then_inc(S["p5_normed"], 1)

                    for m in range(2):
                        bias(0, m)
                    for h in range(QH):
                        for m in range(2):
                            if h + 1 < QH:
                                bias(h + 1, m)
                            inverse(h, m)
                        if h >= 1:
                            dve.wait_ge(S["at_ps"], QH * b + h)
                            dve.tensor_copy(AT[:, h - 1, :], psum[:, 6, 0:L]).then_inc(S["at_copied"], 1)
                        if h % 2 == 1 and EARLY + h // 2 < 12:
                            rope(EARLY + h // 2)
                        if h == 3 and b > 0:
                            apply_norm(5, 2 * b - 2)
                            apply_norm(5, 2 * b - 1)
                        if h == 14 and b + 1 < B:
                            tables(b + 1)
                    dve.wait_ge(S["at_ps"], QH * (b + 1))
                    dve.tensor_copy(AT[:, QH - 1, :], psum[:, 6, 0:L]).then_inc(S["at_copied"], 1)
                add(NT - 2)
                add(NT - 1)
                apply_norm(5, NT - 2)
                apply_norm(5, NT - 1)

            def experts():
                dve.wait_ge(S["aff_exp"], 1)
                step(dve.tensor_scalar(AFF, AFF, 1.0, None, ALU.add))
                step(dve.memset(CMB, 0.0))
                settle()
                step(dve.reciprocal(AFF, AFF))
                settle()
                for i in range(NT):
                    step(dve.max(TOP[:, i, :], AFF[:, i, :]))
                settle()
                for i in range(NT):
                    step(dve.max_index(top_i[:, i, :], TOP[:, i, :], AFF[:, i, :]))
                step(dve.tensor_tensor(PS, TOP[:, :, 0], TOP[:, :, 1], ALU.add))
                settle()
                step(dve.tensor_copy(TOPI, top_i[:, :, :]))
                step(dve.reciprocal(PS, PS))
                settle()
                step(dve.tensor_tensor(PW, TOP[:, :, 0:2], PS.unsqueeze(2).broadcast_to([P, NT, 2]), ALU.mult))
                settle()
                steps_e = moe["iota"].unsqueeze(1).broadcast_to([P, NT, NE])
                for c in range(2):
                    step(dve.tensor_tensor(PICK, steps_e, TOPI[:, :, c:c + 1].broadcast_to([P, NT, NE]), ALU.is_equal))
                    settle()
                    step(dve.tensor_tensor(PICK, PICK, PW[:, :, c:c + 1].broadcast_to([P, NT, NE]), ALU.mult))
                    settle()
                    step(dve.tensor_tensor(CMB[:, :, 0:NE], CMB[:, :, 0:NE], PICK, ALU.add))
                    settle()
                dve.memset(CMB[:, :, NE:NX], 1.0).then_inc(S["cmb_ready"], 1)
                for g in range(2 * NX):
                    n, e = g // NX, EXPERTS[g % NX]
                    if g == NSH:
                        dve.wait_ge(S["ct_copied"], 1)
                        three_parts(CT[0:2 * NS, :], ct3, ct_rest, ct_mid, 2 * NS, S["ct_ready"])
                    dve.wait_ge(S["ge_ps"], 2 * g + 2)
                    dve.wait_ge(S["ge_ready"], g + 1)
                    if g >= 2:
                        dve.wait_ge(S["ye_used"], g - 1)
                    y = dve.scalar_tensor_tensor(out=YE[:, g % 2, :], in0=bank(4 + g % 2), scalar=moe["b1"][:, e:e + 1],
                                                 in1=GE[:, g % 2, :], op0=ALU.add, op1=ALU.mult)
                    if e < NE:
                        step(y)
                        settle()
                        dve.wait_ge(S["cb_ps"], n * NE + e + 1)
                        dve.tensor_tensor(YE[:, g % 2, :], YE[:, g % 2, :], bank(6 + g % 2), ALU.mult).then_inc(S["ye_ready"], 1)
                    else:
                        y.then_inc(S["ye_ready"], 1)
                add_norm(6, lambda i: psum[:, 6 + i % 2, 0:D], twice=True)

            dve.memset(one, 1.0).then_inc(consts_ready, 1)
            for program in (mamba, cross1, swiglu, ttt, cross2, experts):
                program()

        @block.gpsimd
        def _(pool):
            pool_steps = [0]

            def step(instruction):
                pool_steps[0] += 1
                instruction.then_inc(S["pool_step"], 1)
                pool.wait_ge(S["pool_step"], pool_steps[0])

            def inverse_root(out, v, scale, shift):
                n = v.shape[-1]
                arg, half, t = root_tmp[:, 0:n], root_tmp[:, 16:16 + n], root_tmp[:, 32:32 + n]
                step(pool.tensor_scalar(arg, v, scale, shift, ALU.mult, ALU.add))
                pool_steps[0] += 1
                pool.tensor_scalar(half, arg, -0.5, None, ALU.mult).then_inc(S["pool_step"], 1)
                step(pool.tensor_scalar(out.bitcast(I32), arg.bitcast(I32), -0.5, ROOT_GUESS, ALU.mult, ALU.add))
                for it in range(3):
                    if n == 1:
                        step(pool.tensor_scalar(t, out, out, half, ALU.mult, ALU.mult))
                        last = pool.tensor_scalar(out, t, 1.5, out, ALU.add, ALU.mult)
                        if it < 2:
                            step(last)
                        continue
                    step(pool.tensor_tensor(t, out, out, ALU.mult))
                    step(pool.tensor_tensor(t, t, half, ALU.mult))
                    step(pool.tensor_scalar(t, t, 1.5, None, ALU.add))
                    last = pool.tensor_tensor(out, out, t, ALU.mult)
                    if it < 2:
                        step(last)
                return last

            def angles(b):
                x_, k_, c_ = ANG[:, 0, :, :], ANG[:, 1, :, :], ANG[:, 2, :, :]
                for t in range(KT):
                    step(pool.tensor_scalar(x_[:, t, :], attn["inv_freq"], pos_f[:, KT * b + t:KT * b + t + 1], None, ALU.mult))
                step(pool.tensor_scalar(k_, x_, float(1 / (2 * np.pi)), ROUND, ALU.mult, ALU.add))
                step(pool.tensor_scalar(k_, k_, ROUND, None, ALU.subtract))
                for part in (TURN_HI, TURN_LO):
                    step(pool.tensor_scalar(c_, k_, part, None, ALU.mult))
                    step(pool.tensor_tensor(x_, x_, c_, ALU.subtract))
                step(pool.tensor_scalar(c_, x_, float(np.pi / 2), None, ALU.add))
                step(pool.tensor_scalar(k_, c_, float(np.pi), -float(2 * np.pi), ALU.is_gt, ALU.mult))
                step(pool.tensor_tensor(c_, c_, k_, ALU.add))
                pool.tensor_scalar(c_, c_, PI_MAX, -PI_MAX, ALU.min, ALU.max).then_inc(S["ang_ready"], 1)
                pool.tensor_scalar(x_, x_, PI_MAX, -PI_MAX, ALU.min, ALU.max).then_inc(S["ang_ready"], 1)

            def rstd_tile(k, i):
                pool.wait_ge(S["ln_var"], {2: 0, 5: NT}[k] + i + 1)
                inverse_root(rstd[:, i:i + 1], mv[:, i, 1:2], 1.0, LN_EPS).then_inc(S["ln_rstd"], 1)

            def mamba():
                for it in range(NBLK * NS):
                    pool.wait_ge(S["h_ready"], it + 1)
                    pool.wait_ge(S["c_copied"], it + 1)
                    if it >= 3:
                        pool.wait_ge(S["hc_summed"], it - 2)
                    pool.tensor_tensor(HC[:, it % 3, :], H[:, it % 2, :], CB[:, it % 2, :], ALU.mult)\
                        .then_inc(S["hc_ready"], 1)

            def swiglu():
                for i in range(3):
                    rstd_tile(2, i)
                pool.wait_ge(ld["ffn"], 16)
                for n, (src, dst) in enumerate(((fw2, fw2b), (fw2b, fw2), (fw2, fw2b))):
                    h = 1 << n
                    a = src.rearrange("p (g i h) d -> p g i (h d)", i=2, h=h)
                    o = dst.rearrange("p (g i h) d -> p g i (h d)", i=2, h=h)
                    if n > 0:
                        pool.wait_ge(S["bf_ready"], 2 * n)
                    pool.tensor_tensor(o[:, :, 0, :], a[:, :, 0, :], a[:, :, 1, :], ALU.add).then_inc(S["bf_ready"], 1)
                    pool.tensor_tensor(o[:, :, 1, :], a[:, :, 0, :], a[:, :, 1, :], ALU.subtract).then_inc(S["bf_ready"], 1)
                    rstd_tile(2, 3 + n)
                for i in range(6, NT):
                    rstd_tile(2, i)
                pool.wait_ge(S["pos_ready"], 1)
                pool.wait_ge(ld["attn"], 16)
                angles(0)

            def ttt():
                pool.wait_ge(ld["ttt"], 16)
                pool.wait_ge(S["s4_ready"], 1)
                pool.wait_ge(S["q4_ready"], 2)
                SB = SQ4.rearrange("p t (h d) -> p (t h) d", h=TH)
                step(pool.tensor_tensor(SB, ttt_w["ln_b"].unsqueeze(1).broadcast_to([P, TH * NT, THD]),
                                        s_gate.unsqueeze(2).broadcast_to([P, TH * NT, THD]), ALU.mult))
                for i in range(NT):
                    pool.wait_ge(S["o4_scaled"], i + 1)
                    pool.tensor_tensor(O4[:, i, :], O4[:, i, :], SQ4[:, i, :], ALU.add).then_inc(S["o4_normed"], 1)

            def cross2():
                for b in range(B):
                    for n in range(12):
                        g = 12 * b + n
                        pool.wait_ge(S["t1_ready"], 3 * (g + 1))
                        pool.tensor_tensor(RT1[:, n % 2, :], RT1[:, n % 2, :], RT2, ALU.add).then_inc(S["rope_sum"], 1)
                        if n < KT:
                            pool.wait_ge(S["krs_ready"], KT * b + n + 1)
                            pool.wait_ge(S["rope_sum"], g + 1)
                            k3 = RT1[:, n % 2, :].rearrange("p (h d) -> p h d", h=KVH)
                            pool.tensor_tensor(k3, k3, k_rs[:, KVH * n:KVH * (n + 1)].unsqueeze(2).broadcast_to([P, KVH, HD]),
                                               ALU.mult).then_inc(S["k_scaled"], 1)
                        elif n % 2 == 1:
                            c = (n - KT) // 2
                            pool.wait_ge(S["ss_ready"], 4 * (g + 1))
                            q = q_rs[:, 8 * c:8 * c + 8]
                            step(inverse_root(q, q_ss[:, 8 * c:8 * c + 8], 1.0 / HD, RMS_EPS))
                            pool.tensor_scalar(q, q, ASCALE, None, ALU.mult).then_inc(S["qrs_ready"], 1)
                        if n == 11 and b + 1 < B:
                            angles(b + 1)
                        if n == EARLY - 1 and b > 0:
                            rstd_tile(5, 2 * b - 2)
                            rstd_tile(5, 2 * b - 1)
                rstd_tile(5, NT - 2)
                rstd_tile(5, NT - 1)

            mamba()
            swiglu()
            ttt()
            cross2()


def _columns(w):
    k, n = w.shape
    return w.reshape(k // P, P, n).transpose(1, 0, 2)


def _rows(v):
    return np.broadcast_to(v.reshape(1, -1), (P, v.size))


def _hadamard(n):
    h = np.ones((1, 1), np.float32)
    while h.shape[0] < n:
        h = np.concatenate([np.concatenate([h, h], 1), np.concatenate([h, -h], 1)], 0)
    return h


def _few(w):
    return np.concatenate([w, np.zeros((P - w.shape[0], w.shape[1]), w.dtype)], 0)


def kernel(**inputs):
    import concourse.bacc as _bacc
    from concourse.bass_utils import run_bass_kernel_spmd as _run

    a = {k: np.asarray(v) for k, v in inputs.items()}
    x2 = a["x"].reshape(T, D)
    ctx2 = a["ctx_2048"].reshape(T, D)
    qkv = a["L1_attn_W_qkv"].reshape(D, TH, 3, THD)
    experts = {k: np.concatenate([a["L1_ffn_r" + k], a["L1_ffn_s" + k]], 0) for k in ("g", "gb", "w1", "b1", "w2", "b2")}
    swap = lambda v: np.concatenate([v[ROPE:], v[:ROPE]])
    eye = np.eye(P, dtype=np.float32)
    parts = {
        "xT": _columns(x2.T), "w_inT": _columns(a["L0_attn_W_in"].T),
        "w_xT": _columns(a["L0_attn_W_x"].T), "w_dtT": a["L0_attn_W_dt"].T, "w_outT": _columns(a["L0_attn_W_out"].T),
        "conv_w": _columns(a["L0_attn_conv_w"]), "conv_b": _columns(a["L0_attn_conv_b"][:, None]),
        "b_dt": _columns(a["L0_attn_b_dt"][:, None]), "a_log": _columns(a["L0_attn_A_log"]),
        "d_skip": _columns(a["L0_attn_D"][:, None]), "ident": eye,
        "sel3": _few(np.tile(eye[:2 * NS, :2 * NS], (3, 1))),
        "x": _columns(x2), "ctx": _columns(ctx2), "ctxT": _columns(ctx2.T),
        "w_qs": _columns(np.concatenate([qkv[:, :, 0].reshape(D, TH * THD), a["L1_attn_W_s"]], 1)),
        "w0T": a["L1_attn_w0"].transpose(2, 0, 1), "w2T": a["L1_attn_w2"].transpose(2, 0, 1),
        "w1T": a["L1_attn_w1"].transpose(2, 0, 1), "w_oT": _columns(a["L1_attn_W_o"]),
        "ln_g": _rows(a["L1_attn_ln_g"]), "ln_b": _rows(a["L1_attn_ln_b"]), "b_s": _rows(a["L1_attn_b_s"]),
        "ffn1T": _columns(a["L0_ffn_W1"].T), "ffn3T": _columns(a["L0_ffn_W3"].T),
        "ffn2T": _columns(a["L0_ffn_W2"].T), "hadamard": _hadamard(P),
        "wqT": _columns(a["L1_xattn_Wq"].T), "wkT": _columns(a["L1_xattn_Wk"].T),
        "wvT": _columns(a["L1_xattn_Wv"].T), "woT": _columns(a["L1_xattn_Wo"].T),
        "q_w": _rows(a["L1_xattn_q_norm_w"]), "q_w_swap": _rows(swap(a["L1_xattn_q_norm_w"])),
        "k_w": _rows(a["L1_xattn_k_norm_w"]), "k_w_swap": _rows(swap(a["L1_xattn_k_norm_w"])),
        "inv_freq": _rows((1.0 / np.float32(10000.0) ** (np.arange(0, HD, 2, dtype=np.float32) / HD)).astype(np.float32)),
        "wa": _columns(a["L1_ffn_wa"]),
        "wg": experts["g"].reshape(NX, KD, P, EF).transpose(2, 0, 1, 3),
        "w1": experts["w1"].reshape(NX, KD, P, EF).transpose(2, 0, 1, 3),
        "w2": experts["w2"].transpose(1, 0, 2), "gb": experts["gb"].T, "b1": experts["b1"].T,
        "b2": _few(experts["b2"]), "iota": _rows(np.arange(NE, dtype=np.float32)),
    }
    arrays = {}
    for name, inside in PACKS.items():
        arrays["in_" + name] = np.ascontiguousarray(
            np.concatenate([parts[p].reshape(P, w) for p, w in inside], 1))
    pos = np.concatenate([a["pos_BxS2"].reshape(B, CTXT_TILES, P), a["itok_BxS_4096_4607"].reshape(B, CTXT_TILES, P)], 1)
    arrays["in_pos"] = np.ascontiguousarray(pos.reshape(B * KT, P).T.astype(np.int32))

    nc = _bacc.Bacc("TRN2", target_bir_lowering=False, num_devices=1)
    aps = {k[3:]: nc.dram_tensor(k, v.shape, mybir.dt.from_np(v.dtype), kind="ExternalInput").ap()
           for k, v in arrays.items()}
    out = nc.dram_tensor("out_x", (T, D), F32, kind="ExternalOutput").ap()
    decoder(nc, aps, out)
    r = _run(nc, [arrays], core_ids=[0])
    return r.results[0]["out_x"].reshape(B, L, D)
```
